# Optimizing a Trainium2 kernel written in Bass

```python
import numpy as np
import jax
import jax.numpy as jnp

def _softmax(x, axis=-1):
    return jax.nn.softmax(x, axis=axis)

def _gelu(x):
    return jax.nn.gelu(x, approximate=True)

def _silu(x):
    return jax.nn.silu(x)

def _sigmoid(x):
    return jax.nn.sigmoid(x)

def _layernorm(x, axis=-1, eps=1e-05):
    m = jnp.mean(x, axis=axis, keepdims=True)
    v = jnp.var(x, axis=axis, keepdims=True)
    return (x - m) / jnp.sqrt(v + eps)

def _scatter_add(tgt, idx, src, axis=0):
    return tgt.at[idx].add(src)

def _segment_sum(src, seg, n):
    return jax.ops.segment_sum(src, seg, n)
kernel_name = 'mk_early_fusion_embed_d1_tok_img768_r4_697ea9'

def setup_inputs(seed: int=0):
    np.random.seed(seed)
    _w = jnp.asarray

    def _rec_inputs():
        import jax
        import jax.numpy as jnp
        _rk = jax.random.key(seed)
        x = -9.30917e-05 + 1.0002 * jax.random.normal(jax.random.fold_in(_rk, 1), (16, 3, 112, 112), jnp.float32)
        x_txt = jax.random.randint(jax.random.fold_in(_rk, 51), (16, 128), 0, 250, jnp.int32)
        return (x, x_txt)
    x, x_txt = _rec_inputs()

    def _L0_tok_setup():
        import jax, jax.numpy as jnp
        import numpy as np
        PATCH = 16
        EPS = 1e-05

        def _shift(x, pad_spec):
            l, r, t, b = pad_spec
            H, W = (x.shape[2], x.shape[3])
            xp = jnp.pad(x, ((0, 0), (0, 0), (max(t, 0), max(b, 0)), (max(l, 0), max(r, 0))))
            h0 = -t if t < 0 else 0
            w0 = -l if l < 0 else 0
            return xp[:, :, h0:h0 + H, w0:w0 + W]
        key = jax.random.key(seed)
        k1, k2 = jax.random.split(key)
        B, C, H, Wd = (32, 3, 224, 224)
        patch_dim = PATCH * PATCH * 5 * C
        dim = 192
        x = jax.random.normal(k1, (B, C, H, Wd), dtype=jnp.float32)
        ln_gamma = jnp.ones((patch_dim,), dtype=jnp.float32)
        ln_beta = jnp.zeros((patch_dim,), dtype=jnp.float32)
        W = jax.random.normal(k2, (patch_dim, dim), dtype=jnp.float32) * patch_dim ** (-0.5)
        b = jnp.zeros((dim,), dtype=jnp.float32)
        return {'x': x, 'ln_gamma': ln_gamma, 'ln_beta': ln_beta, 'W': W, 'b': b}
    _L0_tok_all = _L0_tok_setup()
    _L0_tok_in = {k: v for k, v in _L0_tok_all.items() if k in ('ln_gamma', 'ln_beta', 'W', 'b')}
    del _L0_tok_all

    def _L0_txt_setup():
        import jax, jax.numpy as jnp
        import numpy as np
        TRACE_LR = 0.1
        TRACE_DECAY = 0.99
        ERASE_LR = 1.0
        N_HEADS = 8
        D_TRACE = 64

        def _layer_norm(x, gamma, beta, eps=1e-05):
            mu = jnp.mean(x, axis=-1, keepdims=True)
            var = jnp.mean(jnp.square(x - mu), axis=-1, keepdims=True)
            return (x - mu) * jax.lax.rsqrt(var + eps) * gamma + beta
        key = jax.random.key(seed)
        ks = jax.random.split(key, 8)
        B, S, V, D, HD = (8, 1024, 50257, 192, N_HEADS * D_TRACE)
        return {'input_ids': jax.random.randint(ks[0], (B, S), 0, 250), 'link_ids': jax.random.randint(ks[1], (8,), 0, 250), 'wte': jax.random.normal(ks[2], (V, D), jnp.float32), 'gamma': jnp.ones((D,), jnp.float32), 'beta': jnp.zeros((D,), jnp.float32), 'W_proj': jax.random.normal(ks[3], (HD, D), jnp.float32) * 0.02, 'W_val': jax.random.normal(ks[4], (HD, D), jnp.float32) * 0.02, 'W_out': jax.random.normal(ks[5], (D, HD), jnp.float32) * 0.02, 'value_traces': jax.random.normal(ks[6], (N_HEADS, D_TRACE, D_TRACE), jnp.float32) * 0.02}
    _L0_txt_all = _L0_txt_setup()
    _L0_txt_in = {k: v for k, v in _L0_txt_all.items() if k in ('link_ids', 'wte', 'gamma', 'beta', 'W_proj', 'W_val', 'W_out', 'value_traces')}
    del _L0_txt_all

    def _L0_attn_setup():
        import jax, jax.numpy as jnp
        import numpy as np
        DIM = 192
        H = 12
        HD = DIM // H
        TTT_BASE_LR = 1.0
        EPS = 1e-06

        def ln_fwd(x, gamma, beta):
            mu = jnp.mean(x, axis=-1, keepdims=True)
            var = jnp.mean((x - mu) ** 2, axis=-1, keepdims=True)
            x_hat = (x - mu) / jnp.sqrt(var + EPS)
            return gamma * x_hat + beta

        def ln_fused_l2_bwd(x, l2_target, gamma, beta):
            D = x.shape[-1]
            mu = jnp.mean(x, axis=-1, keepdims=True)
            var = jnp.mean((x - mu) ** 2, axis=-1, keepdims=True)
            std = jnp.sqrt(var + EPS)
            x_hat = (x - mu) / std
            y = gamma * x_hat + beta
            grad_out = y - l2_target
            g = grad_out * gamma
            z = (D * g - jnp.sum(g, -1, keepdims=True) - x_hat * jnp.sum(g * x_hat, -1, keepdims=True)) / (D * std)
            return z
        key = jax.random.key(seed)
        ks = jax.random.split(key, 10)
        B, N, C = (16, 256, DIM)
        return {'x': jax.random.normal(ks[0], (B, N, C), jnp.float32), 'qkv_weight': jax.random.normal(ks[1], (3 * C, C), jnp.float32) * 0.02, 'q_bias': jnp.zeros((C,), jnp.float32), 'v_bias': jnp.zeros((C,), jnp.float32), 'proj_weight': jax.random.normal(ks[2], (C, C), jnp.float32) * 0.02, 'proj_bias': jnp.zeros((C,), jnp.float32), 'ttt_lr_weight': jax.random.normal(ks[3], (H, 1, C), jnp.float32) * 0.02, 'ttt_lr_bias': jnp.zeros((H, 1), jnp.float32), 'ttt_norm_weight': jnp.ones((H, HD), jnp.float32), 'ttt_norm_bias': jnp.zeros((H, HD), jnp.float32), 'W1': jax.random.normal(ks[4], (H, HD, HD), jnp.float32) * 0.02, 'b1': jnp.zeros((H, 1, HD), jnp.float32)}
    _L0_attn_all = _L0_attn_setup()
    _L0_attn_in = {k: v for k, v in _L0_attn_all.items() if k in ('qkv_weight', 'q_bias', 'v_bias', 'proj_weight', 'proj_bias', 'ttt_lr_weight', 'ttt_lr_bias', 'ttt_norm_weight', 'ttt_norm_bias', 'W1', 'b1')}
    del _L0_attn_all

    def _L0_ffn_setup():
        import jax, jax.numpy as jnp
        import numpy as np
        D_MODEL, D_FF, N_EXPERTS, TOP_K = (192, 768, 8, 2)
        B, S = (2, 256)
        LN_EPS = 1e-05

        def _layernorm(x, gamma, beta):
            mu = jnp.mean(x, axis=-1, keepdims=True)
            var = jnp.mean(jnp.square(x - mu), axis=-1, keepdims=True)
            return (x - mu) * jax.lax.rsqrt(var + LN_EPS) * gamma + beta
        key = jax.random.key(seed)
        k1, k2, k3, k4 = jax.random.split(key, 4)
        return {'hidden_states': jax.random.normal(k1, (B, S, D_MODEL), dtype=jnp.float32), 'ln_gamma': jnp.ones((D_MODEL,), dtype=jnp.float32), 'ln_beta': jnp.zeros((D_MODEL,), dtype=jnp.float32), 'router_w': jax.random.normal(k2, (D_MODEL, N_EXPERTS), dtype=jnp.float32) * 0.02, 'w1': jax.random.normal(k3, (N_EXPERTS, D_MODEL, D_FF), dtype=jnp.float32) * 0.02, 'w2': jax.random.normal(k4, (N_EXPERTS, D_FF, D_MODEL), dtype=jnp.float32) * 0.02}
    _L0_ffn_all = _L0_ffn_setup()
    _L0_ffn_in = {k: v for k, v in _L0_ffn_all.items() if k in ('ln_gamma', 'ln_beta', 'router_w', 'w1', 'w2')}
    del _L0_ffn_all
    return {'x': x, 'x_txt': x_txt, 'L0_tok_ln_gamma': _L0_tok_in['ln_gamma'], 'L0_tok_ln_beta': _L0_tok_in['ln_beta'], 'L0_tok_W': _L0_tok_in['W'], 'L0_tok_b': _L0_tok_in['b'], 'L0_txt_link_ids': _L0_txt_in['link_ids'], 'L0_txt_wte': _L0_txt_in['wte'], 'L0_txt_gamma': _L0_txt_in['gamma'], 'L0_txt_beta': _L0_txt_in['beta'], 'L0_txt_W_proj': _L0_txt_in['W_proj'], 'L0_txt_W_val': _L0_txt_in['W_val'], 'L0_txt_W_out': _L0_txt_in['W_out'], 'L0_txt_value_traces': _L0_txt_in['value_traces'], 'L0_attn_qkv_weight': _L0_attn_in['qkv_weight'], 'L0_attn_q_bias': _L0_attn_in['q_bias'], 'L0_attn_v_bias': _L0_attn_in['v_bias'], 'L0_attn_proj_weight': _L0_attn_in['proj_weight'], 'L0_attn_proj_bias': _L0_attn_in['proj_bias'], 'L0_attn_ttt_lr_weight': _L0_attn_in['ttt_lr_weight'], 'L0_attn_ttt_lr_bias': _L0_attn_in['ttt_lr_bias'], 'L0_attn_ttt_norm_weight': _L0_attn_in['ttt_norm_weight'], 'L0_attn_ttt_norm_bias': _L0_attn_in['ttt_norm_bias'], 'L0_attn_W1': _L0_attn_in['W1'], 'L0_attn_b1': _L0_attn_in['b1'], 'L0_ffn_ln_gamma': _L0_ffn_in['ln_gamma'], 'L0_ffn_ln_beta': _L0_ffn_in['ln_beta'], 'L0_ffn_router_w': _L0_ffn_in['router_w'], 'L0_ffn_w1': _L0_ffn_in['w1'], 'L0_ffn_w2': _L0_ffn_in['w2']}

def reference(x, x_txt, L0_tok_ln_gamma, L0_tok_ln_beta, L0_tok_W, L0_tok_b, L0_txt_link_ids, L0_txt_wte, L0_txt_gamma, L0_txt_beta, L0_txt_W_proj, L0_txt_W_val, L0_txt_W_out, L0_txt_value_traces, L0_attn_qkv_weight, L0_attn_q_bias, L0_attn_v_bias, L0_attn_proj_weight, L0_attn_proj_bias, L0_attn_ttt_lr_weight, L0_attn_ttt_lr_bias, L0_attn_ttt_norm_weight, L0_attn_ttt_norm_bias, L0_attn_W1, L0_attn_b1, L0_ffn_ln_gamma, L0_ffn_ln_beta, L0_ffn_router_w, L0_ffn_w1, L0_ffn_w2):
    import jax
    import jax.numpy as jnp

    def _L0_tok_ref(x, ln_gamma, ln_beta, W, b):
        import jax, jax.numpy as jnp
        import numpy as np
        PATCH = 16
        EPS = 1e-05

        def _shift(x, pad_spec):
            l, r, t, b = pad_spec
            H, W = (x.shape[2], x.shape[3])
            xp = jnp.pad(x, ((0, 0), (0, 0), (max(t, 0), max(b, 0)), (max(l, 0), max(r, 0))))
            h0 = -t if t < 0 else 0
            w0 = -l if l < 0 else 0
            return xp[:, :, h0:h0 + H, w0:w0 + W]
        shifts = [(1, -1, 0, 0), (-1, 1, 0, 0), (0, 0, 1, -1), (0, 0, -1, 1)]
        xs = jnp.concatenate([x] + [_shift(x, s) for s in shifts], axis=1)
        B, C5, H, Wd = xs.shape
        h, w = (H // PATCH, Wd // PATCH)
        t = xs.reshape(B, C5, h, PATCH, w, PATCH)
        t = t.transpose(0, 2, 4, 3, 5, 1)
        t = t.reshape(B, h * w, PATCH * PATCH * C5)
        mu = jnp.mean(t, axis=-1, keepdims=True)
        var = jnp.var(t, axis=-1, keepdims=True)
        tn = (t - mu) * jax.lax.rsqrt(var + EPS) * ln_gamma + ln_beta
        return jnp.einsum('bnp,pd->bnd', tn, W) + b

    def _L0_txt_ref(input_ids, link_ids, wte, gamma, beta, W_proj, W_val, W_out, value_traces):
        import jax, jax.numpy as jnp
        import numpy as np
        TRACE_LR = 0.1
        TRACE_DECAY = 0.99
        ERASE_LR = 1.0
        N_HEADS = 8
        D_TRACE = 64

        def _layer_norm(x, gamma, beta, eps=1e-05):
            mu = jnp.mean(x, axis=-1, keepdims=True)
            var = jnp.mean(jnp.square(x - mu), axis=-1, keepdims=True)
            return (x - mu) * jax.lax.rsqrt(var + eps) * gamma + beta
        B, S = input_ids.shape
        H, dt = (N_HEADS, D_TRACE)
        tok = jax.lax.stop_gradient(wte[input_ids])
        Q = _layer_norm(tok, gamma, beta) @ W_proj.T
        Q = Q.reshape(B, S, H, dt).transpose(0, 2, 1, 3)
        V = (tok @ W_val.T).reshape(B, S, H, dt).transpose(0, 2, 1, 3)
        Q_store = Q[:, :, :-2, :]
        V_store = V[:, :, 2:, :]
        mid = input_ids[:, 1:-1]
        arrow_mask = (mid[:, :, None] == link_ids[None, None, :]).any(-1)
        Q_store = Q_store * arrow_mask[:, None, :, None].astype(Q.dtype)
        denom = jnp.maximum(arrow_mask.sum().astype(Q.dtype) * H, 1.0)
        Q_norm = jnp.clip(jnp.linalg.norm(Q_store, axis=-1, keepdims=True), 1e-08)
        Q_erase = Q_store / Q_norm
        V_old = jnp.einsum('bhip,hpq->bhiq', Q_erase, value_traces)
        erase = jnp.einsum('bhip,bhiq->hpq', Q_erase, V_old) / denom
        traces = value_traces - ERASE_LR * erase
        v_update = jnp.einsum('bhip,bhiq->hpq', Q_store, V_store) / denom
        traces = TRACE_DECAY * traces + TRACE_LR * v_update
        traces = jax.lax.stop_gradient(traces)
        Q_addr = jnp.concatenate([jnp.zeros_like(Q[:, :, :1, :]), Q[:, :, :-1, :]], axis=2)
        V_ret = jnp.einsum('bhsp,hpq->bhsq', Q_addr, traces)
        V_ret = V_ret.transpose(0, 2, 1, 3).reshape(B, S, H * dt)
        return V_ret @ W_out.T

    def _L0_attn_ref(x, qkv_weight, q_bias, v_bias, proj_weight, proj_bias, ttt_lr_weight, ttt_lr_bias, ttt_norm_weight, ttt_norm_bias, W1, b1):
        import jax, jax.numpy as jnp
        import numpy as np
        DIM = 192
        H = 12
        HD = DIM // H
        TTT_BASE_LR = 1.0
        EPS = 1e-06

        def ln_fwd(x, gamma, beta):
            mu = jnp.mean(x, axis=-1, keepdims=True)
            var = jnp.mean((x - mu) ** 2, axis=-1, keepdims=True)
            x_hat = (x - mu) / jnp.sqrt(var + EPS)
            return gamma * x_hat + beta

        def ln_fused_l2_bwd(x, l2_target, gamma, beta):
            D = x.shape[-1]
            mu = jnp.mean(x, axis=-1, keepdims=True)
            var = jnp.mean((x - mu) ** 2, axis=-1, keepdims=True)
            std = jnp.sqrt(var + EPS)
            x_hat = (x - mu) / std
            y = gamma * x_hat + beta
            grad_out = y - l2_target
            g = grad_out * gamma
            z = (D * g - jnp.sum(g, -1, keepdims=True) - x_hat * jnp.sum(g * x_hat, -1, keepdims=True)) / (D * std)
            return z
        B, N, C = x.shape
        num_mini_batch = 1
        m = N // num_mini_batch
        qkv_bias = jnp.concatenate([q_bias, jnp.zeros_like(q_bias), v_bias])
        qkv = x @ qkv_weight.T + qkv_bias
        qkv = qkv.reshape(B, N, 3, H, HD).transpose(2, 0, 3, 1, 4)
        q, k, v = (qkv[0], qkv[1], qkv[2])
        ttt_lr = jnp.einsum('bnc,hdc->bhnd', x, ttt_lr_weight) + ttt_lr_bias.reshape(1, H, 1, 1)
        ttt_lr_eta = TTT_BASE_LR * jax.nn.sigmoid(ttt_lr) / HD
        gamma = ttt_norm_weight.reshape(H, 1, HD)
        beta = ttt_norm_bias.reshape(H, 1, HD)

        def compute_mini_batch(carry, inp):
            W1c, b1c = carry
            XQ, XK, XV, eta = inp
            Z1 = XK @ W1c + b1c
            g = ln_fused_l2_bwd(Z1, XV - XK, gamma, beta)
            g = g * eta / m
            grad_W1 = jnp.einsum('bhmd,bhme->bhde', XK, g)
            grad_b1 = jnp.sum(g, axis=2, keepdims=True)
            W1n = W1c - grad_W1
            b1n = b1c - grad_b1
            Z1_bar = ln_fwd(XQ @ W1n + b1n, gamma, beta)
            return ((W1n, b1n), XQ + Z1_bar)

        def to_scan(t):
            return t.reshape(B, H, num_mini_batch, m, t.shape[-1]).transpose(2, 0, 1, 3, 4)
        xs = (to_scan(q), to_scan(k), to_scan(v), to_scan(ttt_lr_eta))
        init = (jnp.broadcast_to(W1, (B, H, HD, HD)), jnp.broadcast_to(b1, (B, H, 1, HD)))
        _, XQW = jax.lax.scan(compute_mini_batch, init, xs)
        out = XQW.transpose(1, 2, 0, 3, 4).reshape(B, H, N, HD)
        out = out.transpose(0, 2, 1, 3).reshape(B, N, C)
        out = out @ proj_weight.T + proj_bias
        return out

    def _L0_ffn_ref(hidden_states, ln_gamma, ln_beta, router_w, w1, w2):
        import jax, jax.numpy as jnp
        import numpy as np
        D_MODEL, D_FF, N_EXPERTS, TOP_K = (192, 768, 8, 2)
        B, S = (2, 256)
        LN_EPS = 1e-05

        def _layernorm(x, gamma, beta):
            mu = jnp.mean(x, axis=-1, keepdims=True)
            var = jnp.mean(jnp.square(x - mu), axis=-1, keepdims=True)
            return (x - mu) * jax.lax.rsqrt(var + LN_EPS) * gamma + beta
        Bz, Sz, D = hidden_states.shape
        residual = hidden_states
        x = _layernorm(hidden_states, ln_gamma, ln_beta)
        tokens = x.reshape(-1, D)
        T = tokens.shape[0]
        logits = tokens @ router_w
        probs = jax.nn.softmax(logits, axis=-1)
        topw, topi = jax.lax.top_k(probs, TOP_K)
        topw = topw / jnp.sum(topw, axis=-1, keepdims=True)
        gates = jnp.zeros((T, N_EXPERTS), dtype=tokens.dtype)
        gates = gates.at[jnp.arange(T)[:, None], topi].set(topw)
        h = jnp.einsum('td,edf->etf', tokens, w1)
        h = jax.nn.silu(h)
        y = jnp.einsum('etf,efd->etd', h, w2)
        out = jnp.einsum('te,etd->td', gates, y)
        return residual + out.reshape(Bz, Sz, D)
    h = _L0_tok_ref(x, L0_tok_ln_gamma, L0_tok_ln_beta, L0_tok_W, L0_tok_b)
    h = jnp.concatenate([h, _L0_txt_ref(x_txt, L0_txt_link_ids, L0_txt_wte, L0_txt_gamma, L0_txt_beta, L0_txt_W_proj, L0_txt_W_val, L0_txt_W_out, L0_txt_value_traces)], axis=1)
    h = h + _L0_attn_ref(_layernorm(h, axis=-1), L0_attn_qkv_weight, L0_attn_q_bias, L0_attn_v_bias, L0_attn_proj_weight, L0_attn_proj_bias, L0_attn_ttt_lr_weight, L0_attn_ttt_lr_bias, L0_attn_ttt_norm_weight, L0_attn_ttt_norm_bias, L0_attn_W1, L0_attn_b1)
    h = h + _L0_ffn_ref(_layernorm(h, axis=-1), L0_ffn_ln_gamma, L0_ffn_ln_beta, L0_ffn_router_w, L0_ffn_w1, L0_ffn_w2)
    return h

_drawn_inputs = setup_inputs


def setup_inputs(seed=0):
    import zlib

    import numpy as np

    out = dict(_drawn_inputs(seed))
    spreads = {'L0_tok_ln_gamma': (1.0, 0.2),
     'L0_tok_ln_beta': (0.0, 0.1),
     'L0_tok_b': (0.0, 0.1),
     'L0_txt_gamma': (1.0, 0.2),
     'L0_txt_beta': (0.0, 0.1),
     'L0_attn_q_bias': (0.0, 0.1),
     'L0_attn_v_bias': (0.0, 0.1),
     'L0_attn_proj_bias': (0.0, 0.1),
     'L0_attn_ttt_lr_bias': (0.0, 0.525),
     'L0_attn_ttt_norm_weight': (1.0, 0.2),
     'L0_attn_ttt_norm_bias': (0.0, 0.1),
     'L0_attn_b1': (0.0, 0.1),
     'L0_ffn_ln_gamma': (1.0, 0.6),
     'L0_ffn_ln_beta': (0.0, 0.786)}
    factors = {'L0_txt_W_val': 26.529, 'L0_attn_ttt_lr_weight': 3.682}
    for name, (base, spread) in spreads.items():
        noise = np.random.default_rng([zlib.crc32(name.encode()), seed]).standard_normal(out[name].shape)
        drawn = base * np.exp(spread * noise) if base else spread * noise
        out[name] = jnp.asarray(drawn.astype(out[name].dtype))
    for name, factor in factors.items():
        out[name] = (out[name] * factor).astype(out[name].dtype)
    return out
```

```python
import concourse.bass as bass
from concourse import mybir
from contextlib import ExitStack

B, SEQ, DM, PATCHES = 16, 128, 192, 49
P = 128
PAIRS = B // 2
TILES = 3 * PAIRS
LO = DM - P
LOA = LO + 1
WIN_ROWS, WIN_CHUNKS = 120, 8
SHIFTS = 5
HM, DT = 8, 64
QW = HM * DT
MC = QW // P
HA, HD = 12, 16
TOKENS = PATCHES + SEQ
EXP, FF = 8, 768
FC = FF // P
SLOTS = (2 * B * TOKENS + EXP * (P - 1)) // P
MAXT = (B * TOKENS + P - 1) // P
N3 = 3 * P
C_COUNT, C_VALID, C_TOKV = 0, 8, 9
C_BLKHI, C_BLKLO, C_UT = 33, 225, 417
CONSTS = C_UT + P


def early_fusion(nc: bass.Bass, win, w5, gb5, tok_b, ids, ids_next, link, wte, txt_gb, wprojT, wvalT, woutT,
                 traces, qkvT, wk, qv_bias, projT, proj_b, lrT, lr_b, ttt_rows, ttt_cols,
                 w1s, b1, ffn_gb, router, fw1, fw2, consts, out):
    f32, i32, u32 = mybir.dt.float32, mybir.dt.int32, mybir.dt.uint32
    ALU, ACT, AX = mybir.AluOpType, mybir.ActivationFunctionType, mybir.AxisListType.X
    ADD, SUB, MUL, MAX = ALU.add, ALU.subtract, ALU.mult, ALU.max
    ds = bass.ds

    def tools(ctx, stage):
        def sb(name, shape, dt=f32):
            return ctx.enter_context(nc.sbuf_tensor(f"{stage}_{name}", shape, dt))

        def sem(name):
            return ctx.enter_context(nc.semaphore(f"{stage}_{name}"))
        return sb, sem

    def pairwise(eng, n, body):
        body(0, 0)
        body(1, 1)
        with eng.Fori(1, n // 2) as i:
            body(i * 2, 0)
            body(i * 2 + 1, 1)

    def late(t, k):
        return not isinstance(t, int) or t >= k

    whole = ExitStack()
    with whole:
        sb, sem = tools(whole, "all")
        h = sb("h", [P, TILES, DM])
        con = sb("con", [P, CONSTS])
        ident = sb("ident", [P, P])
        ones = sb("ones", [P, P])
        zeros = sb("zeros", [P, 512])
        eps5, eps6 = sb("eps5", [P, 1]), sb("eps6", [P, 1])
        ps = whole.enter_context(nc.psum_tensor("ps", [P, 16, 256], f32))
        psb = ps[:].rearrange("p s c -> p (s c)")
        count = con[0:WIN_ROWS, C_COUNT:C_COUNT + WIN_CHUNKS]
        blk_hi, blk_lo = con[:, C_BLKHI:C_BLKHI + DM], con[0:LOA, C_BLKLO:C_BLKLO + DM]
        upper = con[:, C_UT:C_UT + P]

        def image_stage(ctx):
            sb, sem = tools(ctx, "image")
            w5s = sb("w5s", [WIN_ROWS, SHIFTS, WIN_CHUNKS, DM])
            gb5s = sb("gb5s", [WIN_ROWS, 2, SHIFTS, WIN_CHUNKS])
            wc = sb("wc", [WIN_ROWS, WIN_CHUNKS, DM + 1])
            colsum = sb("colsum", [WIN_ROWS, DM])
            tokb = sb("tokb", [P, DM])
            brow = sb("brow", [P, DM])
            brow1 = sb("brow1", [1, DM])
            winb = sb("winb", [WIN_ROWS, 2, WIN_CHUNKS, P])
            sqb = sb("sqb", [WIN_ROWS, 2, WIN_CHUNKS, P])
            st = sb("st", [P, PAIRS, 4])
            consts_in, w_in = sem("consts_in"), sem("w_in")
            win_in = [sem("win_in0"), sem("win_in1")]
            basics, products, colsum_ps, colsum_used, wc_ready = (
                sem("basics"), sem("products"), sem("colsum_ps"), sem("colsum_used"), sem("wc_ready"))
            beta_ps, brow_copied, brow_ps, brow_ready = sem("beta_ps"), sem("brow_copied"), sem("brow_ps"), sem("brow_ready")
            squared, patch_mm, raw_out, var_ready, std_ready = (
                sem("squared"), sem("patch_mm"), sem("raw_out"), sem("var_ready"), sem("std_ready"))
            block = ctx.enter_context(nc.Block())

            @block.sync
            def _(sp):
                sp.dma_start(w5s[:], w5.rearrange("p (s c d) -> p s c d", s=SHIFTS, c=WIN_CHUNKS)).then_inc(w_in, 16)
                sp.dma_start(gb5s[:], gb5.rearrange("p (a s c) -> p a s c", a=2, s=SHIFTS)).then_inc(w_in, 16)
                sp.dma_start(tokb[:], tok_b).then_inc(w_in, 16)
                sp.dma_start(con[:], consts).then_inc(consts_in, 16)

                def load(t, u):
                    if late(t, 2):
                        sp.wait_ge(patch_mm, t - 1)
                    sp.dma_start(winb[:, u].rearrange("p c n -> p (c n)"),
                                 win[ds(t, 1)].rearrange("a p n -> (a p) n")).then_inc(win_in[u], 16)
                pairwise(sp, PAIRS, load)

            @block.gpsimd
            def _(pool):
                nc.gpsimd.memset(zeros[:], 0.0).then_inc(basics, 1)
                pool.wait_ge(basics, 1)
                nc.gpsimd.memset(ones[:], 1.0).then_inc(basics, 1)
                pool.wait_ge(basics, 2)
                nc.gpsimd.memset(eps5[:], 1e-5).then_inc(basics, 1)
                pool.wait_ge(basics, 3)
                nc.gpsimd.memset(eps6[:], 1e-6).then_inc(basics, 1)
                pool.wait_ge(basics, 4)
                nc.gpsimd.affine_select(out=ident[:], in_=zeros[:, 0:P], compare_op=ALU.not_equal, fill=1.0, base=0,
                                        pattern=[[-1, P]], channel_multiplier=1).then_inc(basics, 1)

            @block.scalar
            def _(act):

                def square(t, u):
                    act.wait_ge(win_in[u], (t // 2) * 16 + 16 if isinstance(t, int) else t * 8 + 16 - 8 * u)
                    nc.scalar.activation(sqb[:, u], winb[:, u], ACT.Square).then_inc(squared, 1)
                pairwise(act, PAIRS, square)
                act.wait_ge(var_ready, 1)
                nc.scalar.activation(st[:, :, 2:3], st[:, :, 2:3], ACT.Sqrt, bias=eps5[:]).then_inc(std_ready, 1)

            @block.vector
            def _(dve):
                dve.wait_ge(w_in, 48)
                dve.wait_ge(consts_in, 16)
                for s in range(SHIFTS):
                    for c in range(WIN_CHUNKS):
                        g = gb5s[:, 0, s, c:c + 1]
                        if s == 0:
                            last = nc.vector.tensor_scalar(wc[:, c, 0:DM], w5s[:, s, c], g, None, MUL)
                        else:
                            last = nc.vector.scalar_tensor_tensor(wc[:, c, 0:DM], w5s[:, s, c], g, wc[:, c, 0:DM], MUL, ADD)
                    dve.drain()
                nc.vector.tensor_copy(wc[:, :, DM:DM + 1].rearrange("p c a -> p (c a)"), count).then_inc(products, 1)
                dve.wait_ge(colsum_ps, 1)
                nc.vector.tensor_scalar(colsum[:], psb[0:WIN_ROWS, 0:DM], -1.0, None, MUL).then_inc(colsum_used, 1)
                dve.drain()
                for c in range(WIN_CHUNKS):
                    last = nc.vector.scalar_tensor_tensor(wc[:, c, 0:DM], colsum[:], count[:, c:c + 1], wc[:, c, 0:DM], MUL, ADD)
                last.then_inc(wc_ready, 1)
                dve.wait_ge(beta_ps, 1)
                nc.vector.tensor_copy(brow1[:], psb[0:1, 512:512 + DM]).then_inc(brow_copied, 1)
                dve.wait_ge(brow_ps, 1)
                nc.vector.tensor_tensor(brow[:], psb[:, 1024:1024 + DM], tokb[:], ADD)

                def take_out(t, u):
                    bank = (6 + u) * 512
                    dve.wait_ge(patch_mm, t + 1)
                    nc.vector.tensor_copy(h[:, ds(t * 3, 1)].rearrange("p a d -> p (a d)"), psb[:, bank:bank + DM])
                    nc.vector.tensor_copy(st[:, ds(t, 1), 0:2].rearrange("p a d -> p (a d)"),
                                          psb[:, bank + DM:bank + DM + 2]).then_inc(raw_out, 1)
                pairwise(dve, PAIRS, take_out)
                dve.drain()
                nc.vector.tensor_tensor(st[:, :, 2], st[:, :, 0], st[:, :, 0], MUL)
                dve.drain()
                nc.vector.tensor_tensor(st[:, :, 2], st[:, :, 1], st[:, :, 2], SUB).then_inc(var_ready, 1)
                dve.wait_ge(std_ready, 1)
                nc.vector.reciprocal(st[:, :, 3], st[:, :, 2])
                dve.drain()
                for t in range(PAIRS):
                    nc.vector.scalar_tensor_tensor(h[:, 3 * t], h[:, 3 * t], st[:, t, 3:4], brow[:], MUL, ADD)

            @block.tensor
            def _(pe):
                pe.wait_ge(basics, 5)
                pe.wait_ge(w_in, 48)
                n = SHIFTS * WIN_CHUNKS
                for k in range(n):
                    s, c = divmod(k, WIN_CHUNKS)
                    last = nc.tensor.matmul(psb[0:1, 512:512 + DM], gb5s[:, 1, s, c:c + 1], w5s[:, s, c],
                                            start=(k == 0), stop=(k == n - 1))
                last.then_inc(beta_ps, 1)
                pe.wait_ge(products, 1)
                for c in range(WIN_CHUNKS):
                    last = nc.tensor.matmul(psb[0:WIN_ROWS, 0:DM], ones[0:WIN_ROWS, 0:WIN_ROWS], wc[:, c, 0:DM],
                                            start=(c == 0), stop=(c == WIN_CHUNKS - 1))
                last.then_inc(colsum_ps, 1)
                pe.wait_ge(brow_copied, 1)
                nc.tensor.matmul(psb[:, 1024:1024 + DM], ones[0:1, :], brow1[:], start=True, stop=True).then_inc(brow_ps, 1)
                pe.wait_ge(wc_ready, 1)

                def patches(t, u):
                    bank = (6 + u) * 512
                    pe.wait_ge(squared, t + 1)
                    if late(t, 2):
                        pe.wait_ge(raw_out, t - 1)
                    for c in range(WIN_CHUNKS):
                        nc.tensor.matmul(psb[:, bank:bank + DM + 1], winb[:, u, c], wc[:, c],
                                         start=(c == 0), stop=(c == WIN_CHUNKS - 1))
                    for c in range(WIN_CHUNKS):
                        last = nc.tensor.matmul(psb[:, bank + DM + 1:bank + DM + 2], sqb[:, u, c], count[:, c:c + 1],
                                                start=(c == 0), stop=(c == WIN_CHUNKS - 1))
                    last.then_inc(patch_mm, 1)
                pairwise(pe, PAIRS, patches)

        def text_stage(ctx):
            sb, sem = tools(ctx, "text")
            ids_s, idn_s, link_s = sb("ids_s", [P, B], i32), sb("idn_s", [P, B], i32), sb("link_s", [P, 8], i32)
            idn, linkf, mask = sb("idn", [P, B]), sb("linkf", [P, 8]), sb("mask", [P, B])
            masked_rows, den = sb("masked_rows", [P, 1]), sb("den", [P, 3])
            gb = sb("gb", [P, 2, 2])
            tok, tok2 = sb("tok", [P, B, DM]), sb("tok2", [P, B, DM])
            st, mv, rstd = sb("st", [P, B, 6]), sb("mv", [P, B, 2]), sb("rstd", [P, B])
            xb, xm = sb("xb", [P, 2, DM + 1]), sb("xm", [P, 2, DM + 1])
            xa_hi, xa_lo = sb("xa_hi", [P, B, SEQ + 1]), sb("xa_lo", [LOA, B, SEQ + 1])
            xl_hi, xl_lo = sb("xl_hi", [P, 2, SEQ]), sb("xl_lo", [LOA, 2, SEQ])
            sq, qe = sb("sq", [P, 2, QW]), sb("qe", [P, 2, QW])
            ss, nrm, wgt = sb("ss", [P, 2, HM]), sb("nrm", [P, 2, HM]), sb("wgt", [P, 2, HM])
            wpT_hi, wpT_lo = sb("wpT_hi", [P, QW]), sb("wpT_lo", [LOA, QW])
            wvT_hi, wvT_lo = sb("wvT_hi", [P, QW]), sb("wvT_lo", [LO, QW])
            woT, old = sb("woT", [P, MC, DM]), sb("old", [P, MC, DT])
            gram, new = sb("gram", [P, MC, P]), sb("new", [P, MC, P])
            kept = sb("kept", [P, MC, DT])
            ca_hi, ca_lo = sb("ca_hi", [P, DM]), sb("ca_lo", [LOA, DM])
            m1_hi, m1_lo = sb("m1_hi", [P, QW]), sb("m1_lo", [LO, QW])
            wpa, rts = sb("wpa", [P, MC, 256]), sb("rts", [P, MC, 256])
            na_hi, na_lo = sb("na_hi", [P, DM]), sb("na_lo", [LOA, DM])
            ids_in, misc_in, w_in, tok_in, tok2_in, padded, started = (
                sem("ids_in"), sem("misc_in"), sem("w_in"), sem("tok_in"), sem("tok2_in"), sem("padded"), sem("started"))
            wp_scaled, beta_ps, wp_ready, mask_sum, mask_tot, mv_ready, std_ready = (
                sem("wp_scaled"), sem("beta_ps"), sem("wp_ready"), sem("mask_sum"), sem("mask_tot"), sem("mv_ready"), sem("std_ready"))
            x_ready, xT_ps, xT_ready, q_ps, q_squared, ss_ready, nrm_ready, qe_ready, sums_mm = (
                sem("x_ready"), sem("xT_ps"), sem("xT_ready"), sem("q_ps"), sem("q_squared"), sem("ss_ready"), sem("nrm_ready"),
                sem("qe_ready"), sem("sums_mm"))
            sums_out, small_ps, m1_out, new_ready, wpa_out, rts_out, na_out = (
                sem("sums_out"), sem("small_ps"), sem("m1_out"), sem("new_ready"), sem("wpa_out"), sem("rts_out"), sem("na_out"))
            shift_ready, out_ps, out_done = sem("shift_ready"), sem("out_ps"), sem("out_done")
            GRAM, CROSS, XT, Q = 0, 512, 1024, 2048
            block = ctx.enter_context(nc.Block())

            @block.sync
            def _(sp):
                sp.dma_start(ids_s[:], ids).then_inc(ids_in, 16)
                sp.dma_start(idn_s[:], ids_next).then_inc(misc_in, 16)
                sp.dma_start(link_s[:], link).then_inc(misc_in, 16)
                for dst, src in ((gb[:].rearrange("p a b -> p (a b)"), txt_gb), (wpT_hi[:], wprojT[0:P]), (wpT_lo[0:LO], wprojT[P:DM]),
                                 (wvT_hi[:], wvalT[0:P]), (wvT_lo[:], wvalT[P:DM]),
                                 (woT[:].rearrange("p a b -> p (a b)"), woutT), (old[:].rearrange("p a b -> p (a b)"), traces)):
                    sp.dma_start(dst, src).then_inc(w_in, 16)
                sp.wait_ge(padded, 1)
                sp.wait_ge(tok_in, 16 * B)
                sp.dma_start(tok2[0:SEQ - 2], tok[2:SEQ]).then_inc(tok2_in, 16)

            @block.gpsimd
            def _(pool):
                nc.gpsimd.memset(tok2[96:P], 0.0).then_inc(padded, 1)
                pool.wait_ge(ids_in, 16)
                for b in range(B):
                    pool.indirect_dma_start(out=tok[:, b], out_offset=None, in_=wte,
                                            in_offset=bass.IndirectOffsetOnAxis(ap=ids_s[:, b:b + 1], axis=0)).then_inc(tok_in, 16)
                pool.wait_ge(padded, 1)
                nc.gpsimd.memset(xb[:, :, DM:DM + 1], 1.0).then_inc(started, 1)
                pool.wait_ge(started, 1)
                nc.gpsimd.memset(xa_hi[:, :, 0:1], 0.0).then_inc(started, 1)
                pool.wait_ge(started, 2)
                nc.gpsimd.memset(xa_lo[:, :, 0:1], 0.0).then_inc(started, 1)
                pool.wait_ge(started, 3)
                nc.gpsimd.memset(gram[:], 0.0).then_inc(started, 1)
                pool.wait_ge(started, 4)
                nc.gpsimd.memset(new[:], 0.0).then_inc(started, 1)

            @block.scalar
            def _(act):
                act.wait_ge(mv_ready, 1)
                nc.scalar.activation(rstd[:], mv[:, :, 1], ACT.Sqrt, bias=eps5[:]).then_inc(std_ready, 1)
                act.wait_ge(started, 5)

                def token_tile(b, u):
                    xt = XT + 512 * u
                    act.wait_ge(xT_ps, b + 1)
                    nc.scalar.copy(xa_hi[:, ds(b, 1), 1:SEQ + 1].rearrange("p a s -> p (a s)"), psb[:, xt:xt + SEQ])
                    nc.scalar.copy(xa_lo[:, ds(b, 1), 1:SEQ + 1].rearrange("p a s -> p (a s)"), psb[0:LOA, xt + 256:xt + 256 + SEQ])
                    nc.scalar.copy(xl_hi[:, u], psb[:, xt:xt + SEQ])
                    nc.scalar.copy(xl_lo[:, u], psb[0:LOA, xt + 256:xt + 256 + SEQ]).then_inc(xT_ready, 1)
                    act.wait_ge(q_ps, b + 1)
                    nc.scalar.activation(sq[:, u], psb[:, Q + 512 * u:Q + 512 * u + QW], ACT.Square).then_inc(q_squared, 1)
                    act.wait_ge(ss_ready, b + 1)
                    nc.scalar.activation(nrm[:, u], ss[:, u], ACT.Sqrt).then_inc(nrm_ready, 1)
                pairwise(act, B, token_tile)
                def pair_out(t):
                    for j in range(2):
                        act.wait_ge(out_ps, t * 2 + j + 1)
                        nc.scalar.copy(h[:, ds(t * 3 + 1 + j, 1)].rearrange("p a d -> p (a d)"),
                                       psb[:, Q + 512 * j:Q + 512 * j + DM]).then_inc(out_done, 1)
                pair_out(0)
                with act.Fori(1, PAIRS) as t:
                    pair_out(t)

            @block.vector
            def _(dve):
                dve.wait_ge(w_in, 16 * 7)
                dve.wait_ge(beta_ps, 1)
                nc.vector.tensor_copy(wpT_lo[LO:LOA], psb[LO:LOA, Q:Q + QW])
                nc.vector.tensor_scalar(wpT_hi[:], wpT_hi[:], gb[:, 0, 0:1], None, MUL)
                nc.vector.tensor_scalar(wpT_lo[0:LO], wpT_lo[0:LO], gb[0:LO, 0, 1:2], None, MUL).then_inc(wp_ready, 1)
                dve.wait_ge(misc_in, 32)
                nc.vector.tensor_copy(idn[:], idn_s[:])
                nc.vector.tensor_copy(linkf[:], link_s[:])
                dve.drain()
                nc.vector.tensor_scalar(mask[:], idn[:], linkf[:, 0:1], None, ALU.is_equal)
                for l in range(1, 8):
                    dve.drain()
                    nc.vector.scalar_tensor_tensor(mask[:], idn[:], linkf[:, l:l + 1], mask[:], ALU.is_equal, MAX)
                dve.drain()
                nc.vector.tensor_scalar(mask[:], mask[:], con[:, C_VALID:C_VALID + 1], None, MUL)
                dve.drain()
                nc.vector.reduce_sum(masked_rows[:], mask[:], axis=AX).then_inc(mask_sum, 1)
                dve.wait_ge(mask_tot, 1)
                nc.vector.tensor_scalar(den[:, 0:1], psb[:, CROSS:CROSS + 1], float(HM), 1.0, MUL, MAX)
                dve.drain()
                nc.vector.reciprocal(den[:, 1:2], den[:, 0:1])
                dve.drain()
                nc.vector.tensor_scalar(den[:, 2:3], den[:, 1:2], 0.1, None, MUL)
                nc.vector.tensor_scalar(den[:, 0:1], den[:, 1:2], -0.99, None, MUL)
                dve.wait_ge(tok_in, 16 * B)
                with dve.Fori(0, B) as b:
                    nc.vector.bn_stats(st[:, ds(b, 1)].rearrange("p a d -> p (a d)"), tok[:, ds(b, 1)].rearrange("p a d -> p (a d)"))
                dve.drain()
                for b in range(B):
                    nc.vector.bn_aggr(mv[:, b], st[:, b])
                dve.drain()
                nc.vector.tensor_copy(st[:, :, 0:1], mv[:, :, 0:1]).then_inc(mv_ready, 1)
                dve.wait_ge(std_ready, 1)
                nc.vector.reciprocal(rstd[:], rstd[:])
                dve.drain()
                dve.wait_ge(started, 5)

                def normalise(b, u):
                    if late(b, 2):
                        dve.wait_ge(xT_ps, b - 1)
                        dve.wait_ge(sums_mm, b - 1)
                    nc.vector.tensor_scalar(xb[:, u, 0:DM], tok[:, ds(b, 1)].rearrange("p a d -> p (a d)"),
                                            mv[:, ds(b, 1), 0:1].rearrange("p a d -> p (a d)"), rstd[:, ds(b, 1)], SUB, MUL).then_inc(x_ready, 1)
                    dve.drain()
                    nc.vector.tensor_scalar(xm[:, u], xb[:, u], mask[:, ds(b, 1)], None, MUL)

                def query(b, u):
                    dve.wait_ge(q_squared, b + 1)
                    nc.vector.reduce_sum(ss[:, u], sq[:, u].rearrange("p (h d) -> p h d", h=HM), axis=AX).then_inc(ss_ready, 1)
                    dve.wait_ge(nrm_ready, b + 1)
                    nc.vector.tensor_scalar(nrm[:, u], nrm[:, u], 1e-8, None, MAX)
                    dve.drain()
                    nc.vector.reciprocal(wgt[:, u], nrm[:, u])
                    dve.drain()
                    nc.vector.tensor_scalar(wgt[:, u], wgt[:, u], mask[:, ds(b, 1)], None, MUL)
                    dve.drain()
                    nc.vector.tensor_tensor(qe[:, u].rearrange("p (h d) -> p h d", h=HM),
                                            psb[:, Q + 512 * u:Q + 512 * u + QW].rearrange("p (h d) -> p h d", h=HM),
                                            wgt[:, u].unsqueeze(2).to_broadcast([P, HM, DT]), MUL).then_inc(qe_ready, 1)

                def token_tile(b, u):
                    normalise(b, u)
                    query(b, u)
                pairwise(dve, B, token_tile)
                dve.wait_ge(sums_mm, B)
                for half in range(2):
                    r = slice(DT * half, DT * half + DT)
                    nc.vector.tensor_copy(gram[r, :, r], psb[r, GRAM:GRAM + 512].rearrange("p (c d) -> p c d", c=MC)[:, :, r])
                nc.vector.tensor_copy(ca_hi[:], psb[:, CROSS:CROSS + DM])
                nc.vector.tensor_copy(ca_lo[:], psb[0:LOA, CROSS + 256:CROSS + 256 + DM]).then_inc(sums_out, 1)
                dve.wait_ge(small_ps, 1)
                nc.vector.tensor_copy(wpa[:, 0:2, 0:DM + 1], psb[:, XT:XT + 512].rearrange("p (c d) -> p c d", c=2)[:, :, 0:DM + 1])
                nc.vector.tensor_copy(wpa[:, 2:4, 0:DM + 1], psb[:, XT + 512:XT + 1024].rearrange("p (c d) -> p c d", c=2)[:, :, 0:DM + 1]).then_inc(wpa_out, 1)
                dve.wait_ge(small_ps, 2)
                nc.vector.tensor_copy(m1_hi[:], psb[:, Q:Q + QW])
                nc.vector.tensor_copy(m1_lo[:], psb[0:LO, Q + 512:Q + 512 + QW]).then_inc(m1_out, 1)
                dve.wait_ge(small_ps, 3)
                nc.vector.tensor_scalar(kept[:], psb[:, CROSS:CROSS + MC * DT].rearrange("p (c d) -> p c d", c=MC), den[:, 0:1], None, MUL)
                dve.drain()
                nc.vector.scalar_tensor_tensor(kept[:], old[:], 0.99, kept[:], MUL, ADD)
                dve.drain()
                dve.wait_ge(small_ps, 4)
                for half in range(2):
                    r = slice(DT * half, DT * half + DT)
                    last = nc.vector.scalar_tensor_tensor(new[r, :, r], psb[r, GRAM:GRAM + 512].rearrange("p (c d) -> p c d", c=MC)[:, :, r],
                                                          den[r, 2:3], kept[r], MUL, ADD)
                last.then_inc(new_ready, 1)
                dve.wait_ge(small_ps, 5)
                nc.vector.tensor_copy(rts[:, 0:2, 0:DM + 1], psb[:, XT:XT + 512].rearrange("p (c d) -> p c d", c=2)[:, :, 0:DM + 1])
                nc.vector.tensor_copy(rts[:, 2:4, 0:DM + 1], psb[:, XT + 512:XT + 1024].rearrange("p (c d) -> p c d", c=2)[:, :, 0:DM + 1]).then_inc(rts_out, 1)
                dve.wait_ge(small_ps, 6)
                nc.vector.tensor_copy(na_hi[:], psb[:, CROSS:CROSS + DM])
                nc.vector.tensor_copy(na_lo[:], psb[0:LOA, CROSS + 256:CROSS + 256 + DM]).then_inc(na_out, 1)

                def shifted(b, u):
                    if late(b, 2):
                        dve.wait_ge(out_ps, b - 1)
                    nc.vector.tensor_copy(xl_hi[:, u], xa_hi[:, ds(b, 1), 0:SEQ].rearrange("p a s -> p (a s)"))
                    nc.vector.tensor_copy(xl_lo[:, u], xa_lo[:, ds(b, 1), 0:SEQ].rearrange("p a s -> p (a s)")).then_inc(shift_ready, 1)
                pairwise(dve, B, shifted)

            @block.tensor
            def _(pe):
                pe.wait_ge(w_in, 16 * 7)
                nc.tensor.matmul(psb[LO:LOA, Q:Q + QW], gb[:, 1, 0:1], wpT_hi[:], start=True, stop=False)
                nc.tensor.matmul(psb[LO:LOA, Q:Q + QW], gb[0:LO, 1, 1:2], wpT_lo[0:LO], start=False, stop=True).then_inc(beta_ps, 1)
                pe.wait_ge(mask_sum, 1)
                nc.tensor.matmul(psb[:, CROSS:CROSS + 1], ones[:], masked_rows[:], start=True, stop=True).then_inc(mask_tot, 1)
                nc.tensor.matmul(psb[:, GRAM:GRAM + 512], ones[:], zeros[:], start=True, stop=True)
                pe.wait_ge(mv_ready, 1)
                nc.tensor.matmul(psb[:, CROSS:CROSS + 512], ones[:], zeros[:], start=True, stop=True)
                pe.wait_ge(tok2_in, 16)
                pe.wait_ge(wp_ready, 1)

                def project(b, u):
                    xt = XT + 512 * u
                    pe.wait_ge(x_ready, b + 1)
                    if late(b, 2):
                        pe.wait_ge(xT_ready, b - 1)
                    nc.tensor.transpose(psb[:, xt:xt + SEQ], xb[:, u, 0:P], ident[:])
                    nc.tensor.transpose(psb[0:LOA, xt + 256:xt + 256 + SEQ], xb[:, u, P:DM + 1], ident[:]).then_inc(xT_ps, 1)
                    pe.wait_ge(xT_ready, b + 1)
                    if late(b, 2):
                        pe.wait_ge(qe_ready, b - 1)
                    nc.tensor.matmul(psb[:, Q + 512 * u:Q + 512 * u + QW], xl_hi[:, u], wpT_hi[:], start=True, stop=False)
                    nc.tensor.matmul(psb[:, Q + 512 * u:Q + 512 * u + QW], xl_lo[:, u], wpT_lo[:], start=False, stop=True).then_inc(q_ps, 1)

                def sums(b, u):
                    pe.wait_ge(qe_ready, b + 1)
                    for c in range(MC):
                        r = slice(P * c, P * c + P)
                        nc.tensor.matmul(psb[:, GRAM + P * c:GRAM + P * c + P], qe[:, u, r], qe[:, u, r], start=False, stop=True,
                                         skip_group_check=True)
                    v = tok2[:, ds(b, 1)].rearrange("p a d -> p (a d)")
                    nc.tensor.matmul(psb[:, CROSS:CROSS + DM], xm[:, u, 0:P], v, start=False, stop=True, skip_group_check=True)
                    nc.tensor.matmul(psb[0:LOA, CROSS + 256:CROSS + 256 + DM], xm[:, u, P:DM + 1], v, start=False, stop=True,
                                     skip_group_check=True).then_inc(sums_mm, 1)

                def token_tile(b, u):
                    project(b, u)
                    sums(b, u)
                pairwise(pe, B, token_tile)
                for c in range(MC):
                    o = XT + 256 * c
                    nc.tensor.transpose(psb[:, o:o + P], wpT_hi[:, P * c:P * c + P], ident[:])
                    last = nc.tensor.transpose(psb[:, o + P:o + DM + 1], wpT_lo[:, P * c:P * c + P], ident[0:LOA, 0:LOA])
                last.then_inc(small_ps, 1)
                pe.wait_ge(sums_out, 1)
                for o, m in ((Q, slice(0, P)), (Q + 512, slice(P, DM))):
                    nc.tensor.matmul(psb[0:m.stop - m.start, o:o + QW], ca_hi[:, m], wpT_hi[:], start=True, stop=False)
                    last = nc.tensor.matmul(psb[0:m.stop - m.start, o:o + QW], ca_lo[:, m], wpT_lo[:], start=False, stop=True)
                last.then_inc(small_ps, 1)
                for c in range(MC):
                    last = nc.tensor.matmul(psb[:, CROSS + DT * c:CROSS + DT * c + DT], gram[:, c], old[:, c], start=True, stop=True)
                last.then_inc(small_ps, 1)
                pe.wait_ge(m1_out, 1)
                for c in range(MC):
                    r = slice(P * c, P * c + P)
                    nc.tensor.matmul(psb[:, GRAM + P * c:GRAM + P * c + P], m1_hi[:, r], wvT_hi[:, r], start=True, stop=False)
                    last = nc.tensor.matmul(psb[:, GRAM + P * c:GRAM + P * c + P], m1_lo[:, r], wvT_lo[:, r], start=False, stop=True)
                last.then_inc(small_ps, 1)
                pe.wait_ge(new_ready, 1)
                pe.wait_ge(wpa_out, 1)
                for c in range(MC):
                    last = nc.tensor.matmul(psb[:, XT + 256 * c:XT + 256 * c + DM + 1], new[:, c], wpa[:, c, 0:DM + 1], start=True, stop=True)
                last.then_inc(small_ps, 1)
                pe.wait_ge(rts_out, 1)
                for o, m in ((CROSS, slice(0, P)), (CROSS + 256, slice(P, DM + 1))):
                    for c in range(MC):
                        last = nc.tensor.matmul(psb[0:m.stop - m.start, o:o + DM], rts[:, c, m], woT[:, c], start=(c == 0), stop=(c == MC - 1))
                last.then_inc(small_ps, 1)
                pe.wait_ge(na_out, 1)

                def recall(b, u):
                    pe.wait_ge(shift_ready, b + 1)
                    if late(b, 2):
                        pe.wait_ge(out_done, b - 1)
                    o = Q + 512 * u
                    nc.tensor.matmul(psb[:, o:o + DM], xl_hi[:, u], na_hi[:], start=True, stop=False)
                    nc.tensor.matmul(psb[:, o:o + DM], xl_lo[:, u], na_lo[:], start=False, stop=True).then_inc(out_ps, 1)
                pairwise(pe, B, recall)

        def attention_stage(ctx):
            sb, sem = tools(ctx, "att")
            ZI, TI, KI, OI = 0, 3, 6, 9
            TR_HI, TR_LO = 12 * 256, 14 * 256
            ALLC = 3 * DM + HA
            wall_hi, wall_lo = sb("wall_hi", [P, ALLC]), sb("wall_lo", [LOA, ALLC])
            wv_hi, wv_lo = sb("wv_hi", [P, DM]), sb("wv_lo", [LOA, DM])
            wq_hi, wq_lo = sb("wq_hi", [P, DM]), sb("wq_lo", [LOA, DM])
            wk_hi, wk_lo = sb("wk_hi", [P, DM]), sb("wk_lo", [LO, DM])
            w1_hi, w1_lo = sb("w1_hi", [P, HD]), sb("w1_lo", [LO, HD])
            w1c_hi, w1c_lo = sb("w1c_hi", [P, DM]), sb("w1c_lo", [LOA, DM])
            av_hi, av_lo, av_b = sb("av_hi", [P, 1]), sb("av_lo", [LO, 1]), sb("av_b", [LOA, HA])
            pT_hi, pT_lo = sb("pT_hi", [P, DM]), sb("pT_lo", [LOA, DM])
            rows, gam2, cols_ = sb("rows", [P, 2, DM]), sb("gam2", [P, DM]), sb("cols", [P, 2, 2])
            st, mv, rstd, shift = sb("st", [P, TILES, 6]), sb("mv", [P, TILES, 2]), sb("rstd", [P, TILES]), sb("shift", [P, TILES])
            xn = sb("xn", [P, 2, 3, DM])
            xt_hi, xt_lo = sb("xt_hi", [P, 2, N3]), sb("xt_lo", [LOA, 2, N3])
            xq_hi, xq_lo = sb("xq_hi", [P, 2, N3]), sb("xq_lo", [LOA, 2, N3])
            rt_hi, rt_lo = sb("rt_hi", [P, 2, N3]), sb("rt_lo", [LOA, 2, N3])
            ka = sb("ka", [P, 2, 3, DM + 1])
            sqz, sqo, xz, gz, tz = (sb(n, [P, 3, DM]) for n in ("sqz", "sqo", "xz", "gz", "tz"))
            zz, zh = sb("zz", [P, 2, 3, DM]), sb("zh", [P, 2, 3, DM])
            var, std, inv, ex, sg, sx, varo, stdo = (sb(n, [P, 3 * HA]) for n in ("var", "std", "inv", "ex", "sg", "sx", "varo", "stdo"))
            w1n_hi, w1n_lo = sb("w1n_hi", [P, 2, P]), sb("w1n_lo", [LOA, 2, DM])
            w_in, bias0, w1_done, wz_ps, w_done, pb_ps = (sem(n) for n in ("w_in", "bias0", "w1_done", "wz_ps", "w_done", "pb_ps"))
            mv_ready, lnstd_ready, ln_ready, ones_set = (sem(n) for n in ("mv_ready", "lnstd_ready", "ln_ready", "ones_set"))
            xn_ready, xT_ps, xt_ready, xq_ps, xq_ready, wall_ps, k_ready, z_squared, e_ready, var_ready, std_ready, z_ready = (
                sem(n) for n in ("xn_ready", "xT_ps", "xt_ready", "xq_ps", "xq_ready", "wall_ps", "k_ready", "z_squared", "e_ready",
                                 "var_ready", "std_ready", "z_ready"))
            grad_ps, w1n_ready, o_ps, o_squared, varo_ready, stdo_ready, zh_ready, zhT_ps, rt_ready, proj_ps, h_done = (
                sem(n) for n in ("grad_ps", "w1n_ready", "o_ps", "o_squared", "varo_ready", "stdo_ready", "zh_ready", "zhT_ps",
                                 "rt_ready", "proj_ps", "h_done"))
            grad_half = sem("grad_half")
            zcol, tcol = slice(DM, 2 * DM), slice(2 * DM, ALLC)
            block = ctx.enter_context(nc.Block())

            def schedule(eng, before, step):
                before()
                step(0, 0)
                step(1, 1)
                with eng.Fori(1, PAIRS // 2 - 1) as i:
                    step(i * 2, 0)
                    step(i * 2 + 1, 1)
                step(PAIRS - 2, 0)
                step(PAIRS - 1, 1)

            def more(t, k):
                return not isinstance(t, int) or t + k < PAIRS

            @block.sync
            def _(sp):
                for dst, src in ((up_hi, fw1[0:P]), (up_lo, fw1[P:DM]), (down_w, fw2)):
                    sp.dma_start(dst[:], src.rearrange("p (e f) -> p e f", e=EXP) if dst is not down_w else
                                 src.rearrange("p (e c d) -> p e c d", e=EXP, c=FC)).then_inc(experts_in, 16)
                sp.dma_start(slots_x.rearrange("(s p) d -> p s d", p=P), zeros[:, 0:DM].unsqueeze(1).to_broadcast([P, SLOTS, DM])).then_inc(zeroed, 16)
                sp.wait_ge(bias0, 1)
                for dst, src in ((wall_hi[:, 0:DM], qkvT[0:P, DM:2 * DM]), (wall_lo[0:LO, 0:DM], qkvT[P:DM, DM:2 * DM]),
                                 (wv_hi[:], qkvT[0:P, 2 * DM:3 * DM]), (wv_lo[0:LO], qkvT[P:DM, 2 * DM:3 * DM]),
                                 (wv_lo[LO:LOA], qv_bias[:, DM:2 * DM]), (wq_hi[:], qkvT[0:P, 0:DM]), (wq_lo[0:LO], qkvT[P:DM, 0:DM]),
                                 (wq_lo[LO:LOA], qv_bias[:, 0:DM]), (wk_hi[:], wk[0:P]), (wk_lo[:], wk[P:DM]),
                                 (w1_hi[:], w1s[0:P]), (w1_lo[:], w1s[P:DM]), (w1c_lo[LO:LOA], b1),
                                 (pT_hi[:], projT[0:P]), (pT_lo[0:LO], projT[P:DM]), (pT_lo[LO:LOA], proj_b),
                                 (wall_hi[:, 3 * DM:], lrT[0:P]), (wall_lo[0:LO, 3 * DM:], lrT[P:DM]), (wall_lo[LO:LOA, 3 * DM:], lr_b),
                                 (rows[:].rearrange("p a d -> p (a d)"), ttt_rows), (cols_[:].rearrange("p a d -> p (a d)"), ttt_cols)):
                    sp.dma_start(dst, src).then_inc(w_in, 16)

            @block.gpsimd
            def _(pool):
                nc.gpsimd.memset(wall_lo[LO:LOA, 0:DM], 0.0).then_inc(bias0, 1)
                pool.wait_ge(bias0, 1)
                nc.gpsimd.memset(xt_lo[LO:LOA], 1.0).then_inc(ones_set, 1)
                pool.wait_ge(ones_set, 1)
                nc.gpsimd.memset(xq_lo[LO:LOA], 1.0).then_inc(ones_set, 1)
                pool.wait_ge(ones_set, 2)
                nc.gpsimd.memset(rt_lo[LO:LOA], 1.0).then_inc(ones_set, 1)
                pool.wait_ge(ones_set, 3)
                nc.gpsimd.memset(ka[:, :, :, DM:DM + 1], 1.0).then_inc(ones_set, 1)

            @block.scalar
            def _(act):
                act.wait_ge(mv_ready, 1)
                nc.scalar.activation(rstd[:], mv[:, :, 1], ACT.Sqrt, bias=eps5[:]).then_inc(lnstd_ready, 1)
                act.wait_ge(ln_ready, 1)
                act.wait_ge(ones_set, 4)

                def normalise(t, u):
                    if late(t, 2):
                        act.wait_ge(xT_ps, t - 1)
                    for k in range(3):
                        last = nc.scalar.activation(xn[:, u, k], h[:, ds(t * 3 + k, 1)].rearrange("p a d -> p (a d)"), ACT.Identity,
                                                    bias=shift[:, ds(t * 3 + k, 1)], scale=rstd[:, ds(t * 3 + k, 1)])
                    last.then_inc(xn_ready, 1)

                def take_x(t, u):
                    act.wait_ge(xT_ps, t + 1)
                    if late(t, 2):
                        act.wait_ge(wall_ps, t - 1)
                    nc.scalar.copy(xt_hi[:, u], psb[:, TR_HI:TR_HI + N3])
                    nc.scalar.copy(xt_lo[0:LO, u], psb[0:LO, TR_LO:TR_LO + N3]).then_inc(xt_ready, 1)
                    act.wait_ge(xq_ps, t + 1)
                    if late(t, 2):
                        act.wait_ge(rt_ready, t - 1)
                    nc.scalar.copy(xq_hi[:, u], psb[:, TR_HI:TR_HI + N3])
                    nc.scalar.copy(xq_lo[0:LO, u], psb[0:LO, TR_LO:TR_LO + N3]).then_inc(xq_ready, 1)

                def inner(t, u):
                    act.wait_ge(wall_ps, t + 1)
                    if late(t, 1):
                        act.wait_ge(var_ready, t)
                    nc.scalar.activation(sqz[:], ps[:, ZI:ZI + 3, 0:DM], ACT.Square).then_inc(z_squared, 1)
                    if late(t, 2):
                        act.wait_ge(grad_ps, t - 1)
                    nc.scalar.copy(ka[:, u, :, 0:DM], ps[:, KI:KI + 3, 0:DM]).then_inc(k_ready, 1)
                    if late(t, 1):
                        act.wait_ge(z_ready, t)
                    nc.scalar.activation(ex[:].rearrange("p (k a) -> p k a", k=3), ps[:, TI:TI + 3, DM:DM + HA], ACT.Exp,
                                         scale=-1.0).then_inc(e_ready, 1)
                    act.wait_ge(var_ready, t + 1)
                    nc.scalar.activation(std[:], var[:], ACT.Sqrt, bias=eps6[:], scale=1.0 / HD).then_inc(std_ready, 1)

                def outer(t, u):
                    act.wait_ge(o_ps, t + 1)
                    if late(t, 1):
                        act.wait_ge(varo_ready, t)
                    nc.scalar.activation(sqo[:], ps[:, OI:OI + 3, 0:DM], ACT.Square).then_inc(o_squared, 1)
                    act.wait_ge(varo_ready, t + 1)
                    nc.scalar.activation(stdo[:], varo[:], ACT.Sqrt, bias=eps6[:], scale=1.0 / HD).then_inc(stdo_ready, 1)

                def before():
                    normalise(0, 0)
                    take_x(0, 0)
                    normalise(1, 1)
                    inner(0, 0)

                def step(t, u):
                    if more(t, 1):
                        take_x(t + 1, 1 - u)
                    outer(t, u)
                    if more(t, 2):
                        normalise(t + 2, u)
                    if more(t, 1):
                        inner(t + 1, 1 - u)
                schedule(act, before, step)

            @block.vector
            def _(dve):
                with dve.Fori(0, TILES) as t:
                    nc.vector.bn_stats(st[:, ds(t, 1)].rearrange("p a d -> p (a d)"), h[:, ds(t, 1)].rearrange("p a d -> p (a d)"))
                dve.drain()
                for t in range(TILES):
                    last = nc.vector.bn_aggr(mv[:, t], st[:, t])
                last.then_inc(mv_ready, 1)
                dve.wait_ge(lnstd_ready, 1)
                nc.vector.reciprocal(rstd[:], rstd[:])
                dve.drain()
                nc.vector.scalar_tensor_tensor(shift[:], mv[:, :, 0], -1.0, rstd[:], MUL, MUL).then_inc(ln_ready, 1)
                dve.wait_ge(w_in, 16 * 21)
                nc.vector.reduce_sum(av_hi[:], w1_hi[:], axis=AX)
                nc.vector.reduce_sum(av_lo[:], w1_lo[:], axis=AX)
                nc.vector.reduce_sum(av_b[LO:LOA], w1c_lo[LO:LOA].rearrange("p (a d) -> p a d", a=HA), axis=AX)
                dve.drain()
                nc.vector.tensor_scalar(av_hi[:], av_hi[:], 1.0 / HD, None, MUL)
                nc.vector.tensor_scalar(av_lo[:], av_lo[:], 1.0 / HD, None, MUL)
                nc.vector.tensor_scalar(av_b[LO:LOA], av_b[LO:LOA], 1.0 / HD, None, MUL)
                dve.drain()
                nc.vector.tensor_scalar(w1_hi[:], w1_hi[:], av_hi[:], None, SUB)
                nc.vector.tensor_scalar(w1_lo[:], w1_lo[:], av_lo[:], None, SUB)
                rowb = w1c_lo[LO:LOA].rearrange("p (a d) -> p a d", a=HA)
                nc.vector.tensor_tensor(rowb, rowb, av_b[LO:LOA].unsqueeze(2).to_broadcast([1, HA, HD]), SUB)
                dve.drain()
                for w, c, blk, n in ((w1_hi, w1c_hi, blk_hi, P), (w1_lo, w1c_lo, blk_lo, LO)):
                    last = nc.vector.tensor_tensor(c[0:n].rearrange("p (a d) -> p a d", a=HA), w[0:n].unsqueeze(1).to_broadcast([n, HA, HD]),
                                                   blk[0:n].rearrange("p (a d) -> p a d", a=HA), MUL)
                last.then_inc(w1_done, 1)
                nc.vector.tensor_tensor(gam2[:], rows[:, 0], rows[:, 0], MUL)
                nc.vector.tensor_tensor(wv_hi[:], wv_hi[:], wall_hi[:, 0:DM], SUB)
                nc.vector.tensor_tensor(wv_lo[0:LO], wv_lo[0:LO], wall_lo[0:LO, 0:DM], SUB)
                nc.vector.tensor_tensor(wv_lo[LO:LOA], wv_lo[LO:LOA], rows[LO:LOA, 1], SUB)
                dve.drain()
                nc.vector.tensor_tensor(wall_hi[:, 2 * DM:3 * DM], wv_hi[:], rows[:, 0], MUL)
                nc.vector.tensor_tensor(wall_lo[:, 2 * DM:3 * DM], wv_lo[:], rows[0:LOA, 0], MUL)
                dve.wait_ge(wz_ps, 1)
                nc.vector.tensor_copy(wall_hi[:, zcol], ps[:, 0, 0:DM])
                nc.vector.tensor_copy(wall_lo[0:LO, zcol], ps[0:LO, 2, 0:DM])
                nc.vector.tensor_copy(wall_lo[LO:LOA, zcol], w1c_lo[LO:LOA])
                nc.vector.tensor_tensor(pT_lo[LO:LOA], pT_lo[LO:LOA], ps[LO:LOA, 4, 0:DM], ADD).then_inc(w_done, 1)

                def heads(ap):
                    return ap.rearrange("p k (a d) -> p (k a) d", a=HA)

                def per_head(ap):
                    return ap[:].unsqueeze(2).to_broadcast([P, 3 * HA, HD])

                def zslots(s):
                    return ps[:, s:s + 3, 0:DM].rearrange("p k (a d) -> p k a d", a=HA)

                def four(ap):
                    return ap.rearrange("p k (a d) -> p k a d", a=HA)

                def per_head4(ap):
                    return ap[:].rearrange("p (k a) -> p k a", k=3).unsqueeze(3).to_broadcast([P, 3, HA, HD])

                def inner(t, u):
                    dve.wait_ge(z_squared, t + 1)
                    nc.vector.reduce_sum(var[:], heads(sqz[:]), axis=AX).then_inc(var_ready, 1)
                    dve.wait_ge(std_ready, t + 1)
                    nc.vector.reciprocal(inv[:], std[:])
                    dve.wait_ge(e_ready, t + 1)
                    nc.vector.tensor_scalar(ex[:], ex[:], 1.0, None, ADD)
                    dve.drain()
                    nc.vector.tensor_tensor(four(xz[:]), zslots(ZI), per_head4(inv), MUL)
                    nc.vector.reciprocal(ex[:], ex[:])
                    dve.drain()
                    nc.vector.tensor_tensor(gz[:], xz[:], gam2[:].unsqueeze(1).to_broadcast([P, 3, DM]), MUL)
                    nc.vector.scalar_tensor_tensor(ex[:], ex[:], 1.0 / (HD * HD * TOKENS), inv[:], MUL, MUL)
                    dve.drain()
                    nc.vector.tensor_tensor(gz[:], gz[:], ps[:, TI:TI + 3, 0:DM], SUB)
                    dve.drain()
                    nc.vector.tensor_tensor(tz[:], gz[:], xz[:], MUL)
                    nc.vector.reduce_sum(sg[:], heads(gz[:]), axis=AX)
                    dve.drain()
                    nc.vector.reduce_sum(sx[:], heads(tz[:]), axis=AX)
                    nc.vector.scalar_tensor_tensor(heads(gz[:]), heads(gz[:]), float(HD), per_head(sg), MUL, SUB)
                    dve.drain()
                    nc.vector.tensor_tensor(heads(tz[:]), heads(xz[:]), per_head(sx), MUL)
                    dve.drain()
                    nc.vector.tensor_tensor(gz[:], gz[:], tz[:], SUB)
                    dve.drain()
                    if late(t, 2):
                        dve.wait_ge(grad_ps, t - 1)
                    nc.vector.tensor_tensor(heads(zz[:, u]), heads(gz[:]), per_head(ex), MUL).then_inc(z_ready, 1)

                def new_weights(t, u):
                    dve.wait_ge(grad_ps, t + 1)
                    if late(t, 1):
                        dve.wait_ge(o_ps, t)
                    nc.vector.tensor_tensor(w1n_hi[:], ps[:, KI].rearrange("p (j d) -> p j d", j=2), blk_hi[:, 0:P].unsqueeze(1).to_broadcast([P, 2, P]), MUL)
                    nc.vector.tensor_tensor(w1n_lo[:], ps[0:LOA, KI + 1:KI + 3, 0:DM], blk_lo.unsqueeze(1).to_broadcast([LOA, 2, DM]), MUL)
                    dve.drain()
                    nc.vector.tensor_tensor(w1n_hi[:], w1c_hi[:, 0:P].unsqueeze(1).to_broadcast([P, 2, P]), w1n_hi[:], SUB)
                    nc.vector.tensor_tensor(w1n_lo[:], w1c_lo[:].unsqueeze(1).to_broadcast([LOA, 2, DM]), w1n_lo[:], SUB).then_inc(w1n_ready, 1)

                def outer(t, u):
                    dve.wait_ge(o_squared, t + 1)
                    nc.vector.reduce_sum(varo[:], heads(sqo[:]), axis=AX).then_inc(varo_ready, 1)
                    dve.wait_ge(stdo_ready, t + 1)
                    nc.vector.reciprocal(sg[:], stdo[:])
                    dve.drain()
                    nc.vector.tensor_tensor(four(zh[:, u]), zslots(OI), per_head4(sg), MUL).then_inc(zh_ready, 1)
                    dve.wait_ge(zhT_ps, t + 1)
                    nc.vector.scalar_tensor_tensor(rt_hi[:, u], psb[:, TR_HI:TR_HI + N3], cols_[:, 0, 0:1], xq_hi[:, u], MUL, ADD)
                    nc.vector.scalar_tensor_tensor(rt_lo[0:LO, u], psb[0:LO, TR_LO:TR_LO + N3], cols_[0:LO, 0, 1:2], xq_lo[0:LO, u],
                                                   MUL, ADD).then_inc(rt_ready, 1)

                def add(t, u):
                    dve.wait_ge(proj_ps, t + 1)
                    nc.vector.tensor_tensor(h[:, ds(t * 3, 3)], h[:, ds(t * 3, 3)], ps[:, OI:OI + 3, 0:DM], ADD).then_inc(h_done, 1)

                def before():
                    inner(0, 0)

                def step(t, u):
                    new_weights(t, u)
                    outer(t, u)
                    if more(t, 1):
                        inner(t + 1, 1 - u)
                    add(t, u)
                schedule(dve, before, step)

            @block.tensor
            def _(pe):
                pe.wait_ge(w_in, 16 * 21)
                pe.wait_ge(w1_done, 1)
                nc.tensor.matmul(ps[:, 0, 0:DM], wk_hi[:, 0:P], w1c_hi[:], start=True, stop=False)
                nc.tensor.matmul(ps[:, 0, 0:DM], wk_lo[:, 0:P], w1c_lo[0:LO], start=False, stop=True)
                nc.tensor.matmul(ps[0:LO, 2, 0:DM], wk_hi[:, P:DM], w1c_hi[:], start=True, stop=False)
                nc.tensor.matmul(ps[0:LO, 2, 0:DM], wk_lo[:, P:DM], w1c_lo[0:LO], start=False, stop=True)
                nc.tensor.matmul(ps[LO:LOA, 4, 0:DM], cols_[:, 1, 0:1], pT_hi[:], start=True, stop=False)
                nc.tensor.matmul(ps[LO:LOA, 4, 0:DM], cols_[0:LO, 1, 1:2], pT_lo[0:LO], start=False, stop=True).then_inc(wz_ps, 1)
                pe.wait_ge(w_done, 1)

                def tile_cols(k):
                    return slice(P * k, P * k + P)

                def transposes(t, u):
                    pe.wait_ge(xn_ready, t + 1)
                    if late(t, 1):
                        pe.wait_ge(xq_ready, t)
                    if late(t, 2):
                        pe.wait_ge(rt_ready, t - 1)
                    for k in range(3):
                        nc.tensor.transpose(psb[:, TR_HI + P * k:TR_HI + P * k + P], xn[:, u, k, 0:P], ident[:])
                        last = nc.tensor.transpose(psb[0:LO, TR_LO + P * k:TR_LO + P * k + P], xn[:, u, k, P:DM], ident[:])
                    last.then_inc(xT_ps, 1)
                    pe.wait_ge(xt_ready, t + 1)
                    nc.tensor.matmul(psb[:, TR_HI:TR_HI + N3], wq_hi[:, 0:P], xt_hi[:, u], start=True, stop=False)
                    nc.tensor.matmul(psb[:, TR_HI:TR_HI + N3], wq_lo[:, 0:P], xt_lo[:, u], start=False, stop=True)
                    nc.tensor.matmul(psb[0:LO, TR_LO:TR_LO + N3], wq_hi[:, P:DM], xt_hi[:, u], start=True, stop=False)
                    nc.tensor.matmul(psb[0:LO, TR_LO:TR_LO + N3], wq_lo[:, P:DM], xt_lo[:, u], start=False, stop=True).then_inc(xq_ps, 1)

                def inner(t, u):
                    if late(t, 1):
                        pe.wait_ge(z_ready, t)
                        pe.wait_ge(k_ready, t)
                        pe.wait_ge(w1n_ready, t)
                    for k in range(3):
                        for slot, c in ((ZI + k, zcol), (TI + k, tcol), (KI + k, slice(0, DM))):
                            if k == 2 and slot == KI + k and late(t, 1):
                                pe.wait_ge(zh_ready, t)
                            n = c.stop - c.start
                            nc.tensor.matmul(ps[:, slot, 0:n], xt_hi[:, u, tile_cols(k)], wall_hi[:, c], start=True, stop=False)
                            last = nc.tensor.matmul(ps[:, slot, 0:n], xt_lo[:, u, tile_cols(k)], wall_lo[:, c], start=False, stop=True)
                    last.then_inc(wall_ps, 1)

                def gradient(t, u):
                    pe.wait_ge(z_ready, t + 1)
                    pe.wait_ge(k_ready, t + 1)
                    if late(t, 1):
                        pe.wait_ge(h_done, t)
                    for j in range(2):
                        rows_ = slice(64 * j, 64 * j + PATCHES)
                        hi, lo = ps[:, KI, P * j:P * j + P], ps[0:LOA, KI + 1 + j, 0:DM]
                        nc.tensor.matmul(hi, ka[:, u, 1 + j, 0:P], zz[:, u, 1 + j, 0:P], start=True, stop=False)
                        nc.tensor.matmul(hi, ka[rows_, u, 0, 0:P], zz[rows_, u, 0, 0:P], start=False, stop=True)
                        nc.tensor.matmul(lo, ka[:, u, 1 + j, P:DM + 1], zz[:, u, 1 + j], start=True, stop=False)
                        last = nc.tensor.matmul(lo, ka[rows_, u, 0, P:DM + 1], zz[rows_, u, 0], start=False, stop=True)
                        last.then_inc(grad_ps if j else grad_half, 1)
                        if j == 0:
                            pe.wait_ge(grad_half, t + 1)

                def outer(t, u):
                    pe.wait_ge(w1n_ready, t + 1)
                    pe.wait_ge(xq_ready, t + 1)
                    if late(t, 1):
                        pe.wait_ge(h_done, t)
                    for j in range(2):
                        c = slice(64 * j, 64 * j + 64)
                        for o, q in ((ps[c, OI], c), (ps[:, OI + 1 + j], tile_cols(1 + j))):
                            nc.tensor.matmul(o[:, 0:DM], xq_lo[:, u, q], w1n_lo[:, j], start=True, stop=True)
                            last = nc.tensor.matmul(o[:, 0:P], xq_hi[:, u, q], w1n_hi[:, j], start=False, stop=True, skip_group_check=True)
                    last.then_inc(o_ps, 1)

                def back(t, u):
                    pe.wait_ge(zh_ready, t + 1)
                    pe.wait_ge(xq_ready, t + 2 if more(t, 1) else t + 1)
                    for k in range(3):
                        nc.tensor.transpose(psb[:, TR_HI + P * k:TR_HI + P * k + P], zh[:, u, k, 0:P], ident[:])
                        last = nc.tensor.transpose(psb[0:LO, TR_LO + P * k:TR_LO + P * k + P], zh[:, u, k, P:DM], ident[:])
                    last.then_inc(zhT_ps, 1)

                def project(t, u):
                    pe.wait_ge(rt_ready, t + 1)
                    if more(t, 1):
                        pe.wait_ge(k_ready, t + 2)
                    for k in range(3):
                        nc.tensor.matmul(ps[:, OI + k, 0:DM], rt_hi[:, u, tile_cols(k)], pT_hi[:], start=True, stop=False)
                        last = nc.tensor.matmul(ps[:, OI + k, 0:DM], rt_lo[:, u, tile_cols(k)], pT_lo[:], start=False, stop=True)
                    last.then_inc(proj_ps, 1)

                def before():
                    transposes(0, 0)
                    inner(0, 0)

                def step(t, u):
                    gradient(t, u)
                    if more(t, 1):
                        transposes(t + 1, 1 - u)
                    outer(t, u)
                    if more(t, 1):
                        inner(t + 1, 1 - u)
                    back(t, u)
                    project(t, u)
                schedule(pe, before, step)

        def route_stage(ctx):
            sb, sem = tools(ctx, "route")
            TR_HI, TR_LO, LG = 0, 512, 1024
            rt_hi, rt_lo = sb("rt_hi", [P, EXP]), sb("rt_lo", [LO, EXP])
            st, mv = sb("st", [P, TILES, 6]), sb("mv", [P, TILES, 2])
            r1, shift, r2 = sb("r1", [P, TILES]), sb("shift", [P, TILES]), sb("r2", [P, TILES])
            xu = sb("xu", [P, 2, 3, DM])
            xs = sb("xs", [P, 2, 3, DM])
            xf = sb("xf", [P, TILES, DM])
            ft_hi, ft_lo = sb("ft_hi", [P, 2, N3]), sb("ft_lo", [LO, 2, N3])
            logit, top, topf = (sb(n, [P, TILES, 8]) for n in ("logit", "top", "topf"))
            topi = sb("topi", [P, TILES, 8], u32)
            oh1, oh2, sel, pos, prod = (sb(n, [P, TILES, EXP]) for n in ("oh1", "oh2", "sel", "pos", "prod"))
            tot, cum, keep = (sb(n, [P, EXP, TILES]) for n in ("tot", "cum", "keep"))
            gap, posf = sb("gap", [P, TILES]), sb("posf", [P, 2, TILES])
            iota_e, iota_s, iota_k = sb("iota_e", [P, EXP]), sb("iota_s", [P, SLOTS]), sb("iota_k", [P, MAXT])
            put_row = [sb("put_row1", [P, TILES], i32), sb("put_row2", [P, TILES], i32)]
            over = sb("over", [P, EXP, MAXT])
            tiles_e, tiles_to = sb("tiles_e", [P, EXP]), sb("tiles_to", [P, EXP])
            past, se, base = sb("past", [P, SLOTS, EXP]), sb("se", [P, SLOTS]), sb("base", [P, EXP])
            (w_in, iotas, mv_ready, std1, v2_ready, std2, ln_ready, xu_ready, xf_ready, xT_ps, xT_ready, logit_ps, logits_out,
             gap_ready, exp_ready, sel_ready, rank_ps, index_ready, scattered) = (sem(n) for n in (
                 "w_in", "iotas", "mv_ready", "std1", "v2_ready", "std2", "ln_ready", "xu_ready", "xf_ready", "xT_ps", "xT_ready",
                 "logit_ps", "logits_out", "gap_ready", "exp_ready", "sel_ready", "rank_ps", "index_ready", "scattered"))
            block = ctx.enter_context(nc.Block())

            @block.sync
            def _(sp):
                sp.dma_start(rt_hi[:], router[0:P]).then_inc(w_in, 16)
                sp.dma_start(rt_lo[:], router[P:DM]).then_inc(w_in, 16)
                sp.dma_start(fgb[:].rearrange("p a b -> p (a b)"), ffn_gb).then_inc(w_in, 16)

            @block.gpsimd
            def _(pool):
                nc.gpsimd.iota(iota_e[:], [[1, EXP]], base=0, channel_multiplier=0, allow_small_or_imprecise_dtypes=True).then_inc(iotas, 1)
                pool.wait_ge(iotas, 1)
                nc.gpsimd.iota(iota_s[:], [[1, SLOTS]], base=0, channel_multiplier=0, allow_small_or_imprecise_dtypes=True).then_inc(iotas, 1)
                pool.wait_ge(iotas, 2)
                nc.gpsimd.iota(iota_k[:], [[P, MAXT]], base=0, channel_multiplier=0, allow_small_or_imprecise_dtypes=True).then_inc(iotas, 1)
                pool.wait_ge(zeroed, 16)
                pool.wait_ge(index_ready, 1)
                for t in range(TILES):
                    for k in range(2):
                        pool.indirect_dma_start(out=slots_x, out_offset=bass.IndirectOffsetOnAxis(ap=put_row[k][:, t:t + 1], axis=0),
                                                in_=xf[:, t], in_offset=None, bounds_check=SLOTS * P - 1,
                                                oob_is_err=False).then_inc(scattered, 16)
                pool.wait_ge(scattered, 16 * 2 * TILES)

            @block.scalar
            def _(act):
                act.wait_ge(mv_ready, 1)
                nc.scalar.activation(r1[:], mv[:, :, 1], ACT.Sqrt, bias=eps5[:]).then_inc(std1, 1)
                act.wait_ge(v2_ready, 1)
                nc.scalar.activation(r2[:], r2[:], ACT.Sqrt, bias=eps5[:]).then_inc(std2, 1)
                act.wait_ge(ln_ready, 1)
                act.wait_ge(w_in, 48)

                def pair(t, u):
                    if late(t, 2):
                        act.wait_ge(xf_ready, t - 1)
                    for k in range(3):
                        last = nc.scalar.activation(xu[:, u, k], h[:, ds(t * 3 + k, 1)].rearrange("p a d -> p (a d)"), ACT.Identity,
                                                    bias=shift[:, ds(t * 3 + k, 1)], scale=r1[:, ds(t * 3 + k, 1)])
                    last.then_inc(xu_ready, 1)
                    act.wait_ge(xT_ps, t + 1)
                    if late(t, 2):
                        act.wait_ge(logit_ps, t - 1)
                    nc.scalar.activation(ft_hi[:, u], psb[:, TR_HI:TR_HI + N3], ACT.Identity, bias=fgb[:, 1, 0:1], scale=fgb[:, 0, 0:1])
                    nc.scalar.activation(ft_lo[:, u], psb[0:LO, TR_LO:TR_LO + N3], ACT.Identity, bias=fgb[0:LO, 1, 1:2],
                                         scale=fgb[0:LO, 0, 1:2]).then_inc(xT_ready, 1)
                pairwise(act, PAIRS, pair)
                act.wait_ge(gap_ready, 1)
                nc.scalar.activation(gap[:], gap[:], ACT.Exp).then_inc(exp_ready, 1)

            @block.vector
            def _(dve):
                with dve.Fori(0, TILES) as t:
                    nc.vector.bn_stats(st[:, ds(t, 1)].rearrange("p a d -> p (a d)"), h[:, ds(t, 1)].rearrange("p a d -> p (a d)"))
                dve.drain()
                for t in range(TILES):
                    last = nc.vector.bn_aggr(mv[:, t], st[:, t])
                last.then_inc(mv_ready, 1)
                dve.wait_ge(std1, 1)
                nc.vector.reciprocal(r1[:], r1[:])
                dve.drain()
                nc.vector.scalar_tensor_tensor(shift[:], mv[:, :, 0], -1.0, r1[:], MUL, MUL)
                nc.vector.tensor_tensor(r2[:], r1[:], r1[:], MUL)
                dve.drain()
                nc.vector.tensor_tensor(r2[:], r2[:], mv[:, :, 1], MUL).then_inc(v2_ready, 1)
                dve.wait_ge(std2, 1)
                nc.vector.reciprocal(r2[:], r2[:]).then_inc(ln_ready, 1)
                dve.drain()

                def pair(t, u):
                    dve.wait_ge(xu_ready, t + 1)
                    nc.vector.tensor_tensor(xf[:, ds(t * 3, 3)], xu[:, u], r2[:, ds(t * 3, 3)].unsqueeze(2).to_broadcast([P, 3, DM]), MUL)
                    nc.vector.tensor_tensor(h[:, ds(t * 3, 3)], h[:, ds(t * 3, 3)], xu[:, u], ADD)
                    if late(t, 2):
                        dve.wait_ge(xT_ps, t - 1)
                    nc.vector.tensor_tensor(xs[:, u], xu[:, u], r2[:, ds(t * 3, 3)].unsqueeze(2).to_broadcast([P, 3, DM]), MUL).then_inc(xf_ready, 1)
                    dve.wait_ge(logit_ps, t + 1)
                    nc.vector.tensor_copy(logit[:, ds(t * 3, 3)], psb[:, LG + 512 * u:LG + 512 * u + 24].rearrange("p (k e) -> p k e", k=3)).then_inc(logits_out, 1)
                pairwise(dve, PAIRS, pair)
                dve.drain()
                for t in range(TILES):
                    nc.vector.max(top[:, t], logit[:, t])
                dve.drain()
                for t in range(TILES):
                    nc.vector.max_index(topi[:, t], top[:, t], logit[:, t])
                nc.vector.tensor_tensor(gap[:], top[:, :, 1], top[:, :, 0], SUB).then_inc(gap_ready, 1)
                dve.drain()
                nc.vector.tensor_copy(topf[:], topi[:])
                dve.wait_ge(iotas, 3)
                dve.drain()

                def tiles_bc(ap):
                    return ap.unsqueeze(2).to_broadcast([P, TILES, EXP])
                experts_bc = iota_e[:].unsqueeze(1).to_broadcast([P, TILES, EXP])
                valid = con[:, C_TOKV:C_TOKV + TILES]
                nc.vector.tensor_tensor(oh1[:], experts_bc, tiles_bc(topf[:, :, 0]), ALU.is_equal)
                nc.vector.tensor_tensor(oh2[:], experts_bc, tiles_bc(topf[:, :, 1]), ALU.is_equal)
                dve.drain()
                nc.vector.tensor_tensor(oh1[:], oh1[:], tiles_bc(valid), MUL)
                nc.vector.tensor_tensor(oh2[:], oh2[:], tiles_bc(valid), MUL)
                dve.drain()
                nc.vector.tensor_tensor(sel[:], oh1[:], oh2[:], ADD).then_inc(sel_ready, 1)
                dve.wait_ge(exp_ready, 1)
                nc.vector.tensor_scalar(gate[:, 0], gap[:], 1.0, None, ADD)
                nc.vector.memset(keep[:], 1.0)
                dve.drain()
                nc.vector.reciprocal(gate[:, 0], gate[:, 0])
                nc.vector.memset(keep[:, :, 0:1], 0.0)
                dve.drain()
                nc.vector.tensor_tensor(gate[:, 1], gap[:], gate[:, 0], MUL)
                dve.wait_ge(rank_ps, 1)
                nc.vector.tensor_copy(tot[:], psb[:, 512:512 + TILES * EXP].rearrange("p (t e) -> p e t", e=EXP))
                dve.drain()
                nc.vector.tensor_tensor_scan(cum[:].rearrange("p e t -> p (e t)"), keep[:].rearrange("p e t -> p (e t)"),
                                             tot[:].rearrange("p e t -> p (e t)"), 0.0, MUL, ADD)
                dve.drain()
                nc.vector.tensor_tensor(over[:], cum[:, :, TILES - 1:TILES].to_broadcast([P, EXP, MAXT]),
                                        iota_k[:].unsqueeze(1).to_broadcast([P, EXP, MAXT]), ALU.is_gt)
                nc.vector.tensor_tensor(tot[:], cum[:], tot[:], SUB)
                dve.drain()
                nc.vector.reduce_sum(tiles_e[:], over[:], axis=AX)
                dve.drain()
                nc.vector.tensor_tensor_scan(tiles_to[:], ones[:, 0:EXP], tiles_e[:], 0.0, MUL, ADD)
                dve.drain()
                nc.vector.tensor_tensor(base[:], tiles_to[:], tiles_e[:], SUB)
                dve.drain()
                nc.vector.tensor_scalar(base[:], base[:], float(P), None, MUL)
                dve.drain()
                nc.vector.tensor_tensor(pos[:], psb[:, 0:TILES * EXP].rearrange("p (t e) -> p t e", e=EXP),
                                        base[:].unsqueeze(1).to_broadcast([P, TILES, EXP]), ADD)
                dve.drain()
                nc.vector.tensor_tensor(pos[:], pos[:], tot[:].rearrange("p e t -> p t e"), ADD)
                nc.vector.tensor_scalar(gap[:], valid, -float(SLOTS * P), float(SLOTS * P), MUL, ADD)
                dve.drain()
                for k, oh in enumerate((oh1, oh2)):
                    nc.vector.tensor_tensor(prod[:], oh[:], pos[:], MUL)
                    dve.drain()
                    nc.vector.reduce_sum(posf[:, k], prod[:], axis=AX)
                    dve.drain()
                    nc.vector.tensor_copy(row_of[k][:], posf[:, k])
                    last = nc.vector.tensor_tensor(put_row[k][:], posf[:, k], gap[:], ADD)
                last.then_inc(index_ready, 1)
                nc.vector.tensor_tensor(past[:], iota_s[:].unsqueeze(2).to_broadcast([P, SLOTS, EXP]),
                                        tiles_to[:].unsqueeze(1).to_broadcast([P, SLOTS, EXP]), ALU.is_ge)
                dve.drain()
                nc.vector.reduce_sum(se[:], past[:], axis=AX)
                dve.drain()
                nc.vector.tensor_scalar(slot_expert[:], se[:], float(EXP - 1), None, ALU.min)

            @block.tensor
            def _(pe):
                pe.wait_ge(w_in, 48)

                def pair(t, u):
                    pe.wait_ge(xf_ready, t + 1)
                    if late(t, 1):
                        pe.wait_ge(xT_ready, t)
                    for k in range(3):
                        nc.tensor.transpose(psb[:, TR_HI + P * k:TR_HI + P * k + P], xs[:, u, k, 0:P], ident[:])
                        last = nc.tensor.transpose(psb[0:LO, TR_LO + P * k:TR_LO + P * k + P], xs[:, u, k, P:DM], ident[:])
                    last.then_inc(xT_ps, 1)
                    pe.wait_ge(xT_ready, t + 1)
                    if late(t, 2):
                        pe.wait_ge(logits_out, t - 1)
                    for k in range(3):
                        o = LG + 512 * u + EXP * k
                        nc.tensor.matmul(psb[:, o:o + EXP], ft_hi[:, u, P * k:P * k + P], rt_hi[:], start=True, stop=False)
                        last = nc.tensor.matmul(psb[:, o:o + EXP], ft_lo[:, u, P * k:P * k + P], rt_lo[:], start=False, stop=True)
                    last.then_inc(logit_ps, 1)
                pairwise(pe, PAIRS, pair)
                pe.wait_ge(sel_ready, 1)
                chosen = sel[:].rearrange("p t e -> p (t e)")
                nc.tensor.matmul(psb[:, 0:TILES * EXP], upper, chosen, start=True, stop=True)
                nc.tensor.matmul(psb[:, 512:512 + TILES * EXP], ones[:], chosen, start=True, stop=True).then_inc(rank_ps, 1)

        def expert_stage(ctx):
            sb, sem = tools(ctx, "exp")
            XC, YC, HTC = 6 * 512, 7 * 512, 4 * 512
            HALF = FF // 2
            xs = sb("xs", [P, 4, DM])
            xT_hi, xT_lo = sb("xT_hi", [P, 2, P]), sb("xT_lo", [LO, 2, P])
            hs, hT, ys = sb("hs", [P, 2, FF]), sb("hT", [P, 2, FC, P]), sb("ys", [P, 2, DM])
            x_in = [sem(f"x_in{i}") for i in range(2)]
            xT_ps, xT_ready, h_ps, h_ready, hT_ps, hT_ready, y_ps, y_ready = (sem(n) for n in (
                "xT_ps", "xT_ready", "h_ps", "h_ready", "hT_ps", "hT_ready", "y_ps", "y_ready"))
            y_stored = [sem(f"y_stored{i}") for i in range(2)]
            block = ctx.enter_context(nc.Block())

            def schedule(eng, before, step):
                before()
                step(0, 0)
                step(1, 1)
                with eng.Fori(1, SLOTS // 2 - 1) as i:
                    step(i * 2, 0)
                    step(i * 2 + 1, 1)
                step(SLOTS - 2, 0)
                step(SLOTS - 1, 1)

            def more(s, k):
                return not isinstance(s, int) or s + k < SLOTS

            def of_slot(eng, table, s, top_value):
                return eng.value_load(table[0:1, ds(s, 1)], min_val=0, max_val=top_value)

            @block.sync
            def _(sp):
                def load(s, u):
                    if late(s, 2):
                        sp.wait_ge(xT_ps, s - 1)
                    sp.dma_start(xs[:, u], slots_x[ds(s * P, P)]).then_inc(x_in[u], 16)
                pairwise(sp, SLOTS, load)

            @block.gpsimd
            def _(pool):
                def store(s, u):
                    pool.wait_ge(y_ready, s + 1)
                    pool.dma_start(slots_y[ds(s * P, P)], ys[:, u]).then_inc(y_stored[u], 16)
                pairwise(pool, SLOTS, store)
                for u in range(2):
                    pool.wait_ge(y_stored[u], 8 * SLOTS)

            @block.scalar
            def _(act):
                def take_x(s, u):
                    act.wait_ge(xT_ps, s + 1)
                    if late(s, 2):
                        act.wait_ge(h_ps, s - 1)
                    nc.scalar.activation(xT_hi[:, u], psb[:, XC:XC + P], ACT.Identity, bias=fgb[:, 1, 0:1], scale=fgb[:, 0, 0:1])
                    nc.scalar.activation(xT_lo[:, u], psb[0:LO, XC + P:XC + 2 * P], ACT.Identity, bias=fgb[0:LO, 1, 1:2],
                                         scale=fgb[0:LO, 0, 1:2]).then_inc(xT_ready, 1)

                def hidden(s, u):
                    act.wait_ge(h_ps, s + 1)
                    if late(s, 2):
                        act.wait_ge(hT_ps, s - 1)
                    nc.scalar.activation(hs[:, u].rearrange("p (b f) -> p b f", b=2),
                                         psb[:, 1024 * u:1024 * u + 1024].rearrange("p (b f) -> p b f", b=2)[:, :, 0:HALF],
                                         ACT.Silu).then_inc(h_ready, 1)

                def result(s, u):
                    act.wait_ge(y_ps, s + 1)
                    if late(s, 2):
                        act.wait_ge(y_stored[u], (s // 2) * 16 if isinstance(s, int) else s * 8 - 8 * u)
                    nc.scalar.copy(ys[:, u], psb[:, YC:YC + DM]).then_inc(y_ready, 1)

                def before():
                    take_x(0, 0)

                def step(s, u):
                    hidden(s, u)
                    if more(s, 1):
                        take_x(s + 1, 1 - u)
                    if late(s, 1):
                        result(s - 1, 1 - u)
                schedule(act, before, step)
                result(SLOTS - 1, 1)

            @block.vector
            def _(dve):
                def take_hT(s, u):
                    dve.wait_ge(hT_ps, s + 1)
                    if late(s, 2):
                        dve.wait_ge(y_ps, s - 1)
                    nc.vector.tensor_copy(hT[:, u].rearrange("p (b c) n -> p b (c n)", b=2),
                                          psb[:, HTC:HTC + 1024].rearrange("p (b f) -> p b f", b=2)[:, :, 0:HALF]).then_inc(hT_ready, 1)
                pairwise(dve, SLOTS, take_hT)

            @block.tensor
            def _(pe):
                pe.wait_ge(experts_in, 16 * 3)

                def turn_x(s, u):
                    pe.wait_ge(x_in[u], (s // 2) * 16 + 16 if isinstance(s, int) else s * 8 + 16 - 8 * u)
                    if late(s, 1):
                        pe.wait_ge(xT_ready, s)
                    nc.tensor.transpose(psb[:, XC:XC + P], xs[:, u, 0:P], ident[:])
                    nc.tensor.transpose(psb[0:LO, XC + P:XC + 2 * P], xs[:, u, P:DM], ident[:]).then_inc(xT_ps, 1)

                def up(s, u):
                    e = of_slot(pe, slot_expert, s, EXP - 1)
                    pe.wait_ge(xT_ready, s + 1)
                    if late(s, 2):
                        pe.wait_ge(h_ready, s - 1)
                    for b in range(2):
                        o, f = 1024 * u + 512 * b, slice(HALF * b, HALF * b + HALF)
                        nc.tensor.matmul(psb[:, o:o + HALF], xT_hi[:, u], up_hi[:, ds(e, 1), f].rearrange("p a f -> p (a f)"), start=True, stop=False)
                        last = nc.tensor.matmul(psb[:, o:o + HALF], xT_lo[:, u], up_lo[:, ds(e, 1), f].rearrange("p a f -> p (a f)"), start=False, stop=True)
                    last.then_inc(h_ps, 1)

                def turn_h(s, u):
                    pe.wait_ge(h_ready, s + 1)
                    if late(s, 1):
                        pe.wait_ge(hT_ready, s)
                    for c in range(FC):
                        o = HTC + 512 * (c // 3) + P * (c % 3)
                        last = nc.tensor.transpose(psb[:, o:o + P], hs[:, u, P * c:P * c + P], ident[:])
                    last.then_inc(hT_ps, 1)

                def down(s, u):
                    e = of_slot(pe, slot_expert, s, EXP - 1)
                    pe.wait_ge(hT_ready, s + 1)
                    if late(s, 1):
                        pe.wait_ge(y_ready, s)
                    for c in range(FC):
                        last = nc.tensor.matmul(psb[:, YC:YC + DM], hT[:, u, c], down_w[:, ds(e, 1), c].rearrange("p a d -> p (a d)"),
                                                start=(c == 0), stop=(c == FC - 1))
                    last.then_inc(y_ps, 1)

                def before():
                    turn_x(0, 0)
                    up(0, 0)

                def step(s, u):
                    if more(s, 1):
                        turn_x(s + 1, 1 - u)
                    turn_h(s, u)
                    if more(s, 1):
                        up(s + 1, 1 - u)
                    down(s, u)
                schedule(pe, before, step)

        def combine_stage(ctx):
            sb, sem = tools(ctx, "comb")
            RING = 4
            yg = sb("yg", [P, RING, 2, DM])
            fetched = [sem(f"fetched{i}") for i in range(RING)]
            added, stored, half = sem("added"), sem("stored"), sem("half")
            block = ctx.enter_context(nc.Block())

            @block.gpsimd
            def _(pool):
                for t in range(TILES):
                    if t >= RING:
                        pool.wait_ge(added, t - RING + 1)
                    for k in range(2):
                        pool.indirect_dma_start(out=yg[:, t % RING, k], out_offset=None, in_=slots_y,
                                                in_offset=bass.IndirectOffsetOnAxis(ap=row_of[k][:, t:t + 1], axis=0)).then_inc(fetched[t % RING], 16)

            @block.vector
            def _(dve):
                for t in range(TILES):
                    dve.wait_ge(fetched[t % RING], 32 * (t // RING + 1))
                    nc.vector.scalar_tensor_tensor(h[:, t], yg[:, t % RING, 0], gate[:, 0, t:t + 1], h[:, t], MUL, ADD)
                    dve.drain()
                    nc.vector.scalar_tensor_tensor(h[:, t], yg[:, t % RING, 1], gate[:, 1, t:t + 1], h[:, t], MUL, ADD).then_inc(added, 1)

            @block.sync
            def _(sp):
                for t in range(TILES):
                    sp.wait_ge(added, t + 1)
                    pair, k = divmod(t, 3)
                    if k == 0:
                        for j in range(2):
                            sp.dma_start(out[2 * pair + j, 0:PATCHES], h[64 * j:64 * j + PATCHES, t]).then_inc(stored, 16)
                    else:
                        sp.dma_start(out[2 * pair + k - 1, PATCHES:TOKENS], h[:, t]).then_inc(stored, 16)
                sp.wait_ge(stored, 16 * 4 * PAIRS)

        with ExitStack() as ctx:
            image_stage(ctx)
        with ExitStack() as ctx:
            text_stage(ctx)
        up_hi, up_lo = sb("up_hi", [P, EXP, FF]), sb("up_lo", [LO, EXP, FF])
        down_w = sb("down_w", [P, EXP, FC, DM])
        fgb, gate = sb("fgb", [P, 2, 2]), sb("gate", [P, 2, TILES])
        row_of = [sb("row_of1", [P, TILES], i32), sb("row_of2", [P, TILES], i32)]
        slot_expert = sb("slot_expert", [P, SLOTS], i32)
        slots_x = nc.dram_tensor("slots_x", (SLOTS * P, DM), f32).ap()
        slots_y = nc.dram_tensor("slots_y", (SLOTS * P, DM), f32).ap()
        experts_in, zeroed = sem("experts_in"), sem("zeroed")
        with ExitStack() as ctx:
            attention_stage(ctx)
        with ExitStack() as ctx:
            route_stage(ctx)
        with ExitStack() as ctx:
            expert_stage(ctx)
        with ExitStack() as ctx:
            combine_stage(ctx)


def _shape_constants(np):
    pixels = [(y, x) for y in range(16) for x in range(16)]
    pixels += [(-1, x) for x in range(16)] + [(16, x) for x in range(16)]
    pixels += [(y, -1) for y in range(16)] + [(y, 16) for y in range(16)]
    moves = [(0, 0), (0, 1), (0, -1), (1, 0), (-1, 0)]
    source = np.array([[(y + dy) * 16 + x + dx if 0 <= y + dy < 16 and 0 <= x + dx < 16 else -1
                        for y, x in pixels] for dy, dx in moves])
    c = np.zeros((P, CONSTS), np.float32)
    often = np.tile((source >= 0).sum(0), 3) / 3840.0
    c[0:WIN_ROWS, C_COUNT:C_COUNT + WIN_CHUNKS] = often.reshape(WIN_CHUNKS, WIN_ROWS).T
    c[0:SEQ - 2, C_VALID] = 1.0
    c[:, C_TOKV:C_TOKV + TILES] = 1.0
    c[PATCHES:64, C_TOKV:C_TOKV + TILES:3] = 0.0
    c[64 + PATCHES:, C_TOKV:C_TOKV + TILES:3] = 0.0
    own = (np.arange(DM)[:, None] // HD == np.arange(DM)[None, :] // HD).astype(np.float32)
    c[:, C_BLKHI:C_BLKHI + DM] = own[0:P]
    c[0:LO, C_BLKLO:C_BLKLO + DM] = own[P:DM]
    c[LO, C_BLKLO:C_BLKLO + DM] = 1.0
    c[:, C_UT:C_UT + P] = (np.arange(P)[:, None] < np.arange(P)[None, :])
    return pixels, source, c


def kernel(**inputs):
    import numpy as np
    import concourse.bacc as bacc
    from concourse.bass_utils import run_bass_kernel_spmd as run

    x = {k.replace("L0_", ""): np.asarray(v) for k, v in inputs.items()}
    pixels, source, consts = _shape_constants(np)
    ys, xs = (np.array(v) for v in zip(*pixels))

    def window_rows(w):
        w = w.reshape(256, SHIFTS, 3, -1)
        o = np.zeros((SHIFTS, 3, len(pixels), w.shape[-1]), w.dtype)
        for s in range(SHIFTS):
            k = source[s] >= 0
            o[s][:, k] = w[source[s][k], s].transpose(1, 0, 2)
        return o.reshape(SHIFTS, WIN_CHUNKS, WIN_ROWS, -1).transpose(2, 0, 1, 3)

    image = np.pad(x["x"], ((0, 0), (0, 0), (1, 1), (1, 1)))
    at = np.arange(7) * 16 + 1
    w = image[:, :, (at[:, None] + ys[None])[:, None, :], (at[:, None] + xs[None])[None, :, :]]
    w = w.transpose(0, 2, 3, 1, 4).reshape(B, PATCHES, 3 * len(pixels))
    win = np.zeros((B, 64, 3 * len(pixels)), w.dtype)
    win[:, :PATCHES] = w
    win = win.reshape(PAIRS, P, WIN_CHUNKS, WIN_ROWS).transpose(0, 3, 2, 1)

    def cols(*vectors):
        o = np.zeros((P, len(vectors), 2), vectors[0].dtype)
        for n, v in enumerate(vectors):
            o[:, n, 0], o[0:LO, n, 1] = v[:P], v[P:]
        return o

    def spread(*rows):
        return np.broadcast_to(np.stack(rows)[None], (P, len(rows), rows[0].shape[-1]))

    ids = x["x_txt"].T
    nxt = np.zeros_like(ids)
    nxt[:-1] = ids[1:]
    qkv = x["attn_qkv_weight"]
    data = dict(
        win=win, w5=window_rows(x["tok_W"]),
        gb5=np.stack([window_rows(x["tok_ln_gamma"][:, None]), window_rows(x["tok_ln_beta"][:, None])], 1),
        tok_b=spread(x["tok_b"]), ids=ids, ids_next=nxt,
        link=np.broadcast_to(x["txt_link_ids"].astype(np.int32)[None], (P, 8)), wte=x["txt_wte"],
        txt_gb=cols(x["txt_gamma"], x["txt_beta"]), wprojT=x["txt_W_proj"].T, wvalT=x["txt_W_val"].T,
        woutT=x["txt_W_out"].T.reshape(MC, P, DM).transpose(1, 0, 2),
        traces=x["txt_value_traces"].reshape(MC, P, DT).transpose(1, 0, 2),
        qkvT=qkv.T, wk=qkv[DM:2 * DM], qv_bias=np.stack([x["attn_q_bias"], x["attn_v_bias"]])[None],
        projT=x["attn_proj_weight"].T, proj_b=x["attn_proj_bias"][None], lrT=x["attn_ttt_lr_weight"][:, 0].T,
        lr_b=x["attn_ttt_lr_bias"].T, ttt_rows=spread(x["attn_ttt_norm_weight"].reshape(-1), x["attn_ttt_norm_bias"].reshape(-1)),
        ttt_cols=cols(x["attn_ttt_norm_weight"].reshape(-1), x["attn_ttt_norm_bias"].reshape(-1)),
        w1s=x["attn_W1"].reshape(DM, HD), b1=x["attn_b1"].reshape(1, DM), ffn_gb=cols(x["ffn_ln_gamma"], x["ffn_ln_beta"]),
        router=x["ffn_router_w"], fw1=x["ffn_w1"].transpose(1, 0, 2),
        fw2=x["ffn_w2"].reshape(EXP, FC, P, DM).transpose(2, 0, 1, 3), consts=consts)
    flat = {"win": (PAIRS, WIN_ROWS, WIN_CHUNKS * P)}
    nc = bacc.Bacc("TRN2", target_bir_lowering=False, num_devices=1)
    arrays, args = {}, []
    for name, a in data.items():
        a = np.ascontiguousarray(a)
        a = a.reshape(flat[name] if name in flat else (a.shape[0], -1))
        arrays["in_" + name] = a
        args.append(nc.dram_tensor("in_" + name, a.shape, mybir.dt.from_np(a.dtype), kind="ExternalInput").ap())
    res = nc.dram_tensor("out_h", (B, TOKENS, DM), mybir.dt.float32, kind="ExternalOutput").ap()
    early_fusion(nc, *args, res)
    return run(nc, [arrays], core_ids=[0]).results[0]["out_h"]
```

```python
import concourse.bass as bass
from concourse import mybir
from contextlib import ExitStack

B, SEQ, DM, PATCHES = 16, 128, 192, 49
P = 128
PAIRS = B // 2
TILES = 3 * PAIRS
LO = DM - P
LOA = LO + 1
WIN_ROWS, WIN_CHUNKS = 120, 8
SHIFTS = 5
HM, DT = 8, 64
QW = HM * DT
MC = QW // P
HA, HD = 12, 16
TOKENS = PATCHES + SEQ
EXP, FF = 8, 768
FC = FF // P
SLOTS = (2 * B * TOKENS + EXP * (P - 1)) // P
MAXT = (B * TOKENS + P - 1) // P
N3 = 3 * P
C_COUNT, C_VALID, C_TOKV = 0, 8, 9
C_BLKHI, C_BLKLO, C_UT = 33, 225, 417
C_ROW, C_EMPTY = C_UT + P, C_UT + P + TILES
CONSTS = C_EMPTY + 1
ROW = DM + 2


def early_fusion(nc: bass.Bass, win, w5, gb5, tok_b, ids, ids_next, link, wte, txt_gb, wprojT, wvalT, woutT,
                 traces, qkvT, wk, qv_bias, projT, proj_b, lrT, lr_b, ttt_rows, ttt_cols,
                 w1s, b1, ffn_gb, router, fw1, fw2, consts, out):
    f32, f32r, i32, u32 = mybir.dt.float32, mybir.dt.float32r, mybir.dt.int32, mybir.dt.uint32
    ALU, ACT, AX = mybir.AluOpType, mybir.ActivationFunctionType, mybir.AxisListType.X
    ADD, SUB, MUL, MAX = ALU.add, ALU.subtract, ALU.mult, ALU.max
    ds = bass.ds

    def tools(ctx, stage):
        def sb(name, shape, dt=f32):
            return ctx.enter_context(nc.sbuf_tensor(f"{stage}_{name}", shape, dt))

        def sem(name):
            return ctx.enter_context(nc.semaphore(f"{stage}_{name}"))
        return sb, sem

    def pairwise(eng, n, body):
        body(0, 0)
        body(1, 1)
        with eng.Fori(1, n // 2) as i:
            body(i * 2, 0)
            body(i * 2 + 1, 1)

    def late(t, k):
        return not isinstance(t, int) or t >= k

    whole = ExitStack()
    with whole:
        sb, sem = tools(whole, "all")
        h = sb("h", [P, TILES, DM])
        con = sb("con", [P, CONSTS])
        ident = sb("ident", [P, P])
        ones = sb("ones", [P, P])
        eps5, eps6 = sb("eps5", [P, 1]), sb("eps6", [P, 1])
        ps = whole.enter_context(nc.psum_tensor("ps", [P, 16, 256], f32))
        psb = ps[:].rearrange("p s c -> p (s c)")
        count = con[0:WIN_ROWS, C_COUNT:C_COUNT + WIN_CHUNKS]
        blk_hi, blk_lo = con[:, C_BLKHI:C_BLKHI + DM], con[0:LOA, C_BLKLO:C_BLKLO + DM]
        upper = con[:, C_UT:C_UT + P]

        def image_stage(ctx):
            sb, sem = tools(ctx, "image")
            w5s = sb("w5s", [WIN_ROWS, SHIFTS, WIN_CHUNKS, DM])
            gb5s = sb("gb5s", [WIN_ROWS, 2, SHIFTS, WIN_CHUNKS])
            wc = sb("wc", [WIN_ROWS, WIN_CHUNKS, DM + 1])
            colsum = sb("colsum", [WIN_ROWS, DM])
            tokb = sb("tokb", [P, DM])
            brow = sb("brow", [P, DM])
            brow1 = sb("brow1", [1, DM])
            winb = sb("winb", [WIN_ROWS, 2, WIN_CHUNKS, P])
            sqb = sb("sqb", [WIN_ROWS, 2, WIN_CHUNKS, P])
            st = sb("st", [P, PAIRS, 4])
            consts_in, w_in = sem("consts_in"), sem("w_in")
            win_in = [sem("win_in0"), sem("win_in1")]
            basics, products, colsum_ps, colsum_used, wc_ready = (
                sem("basics"), sem("products"), sem("colsum_ps"), sem("colsum_used"), sem("wc_ready"))
            beta_ps, brow_copied, brow_ps, brow_ready = sem("beta_ps"), sem("brow_copied"), sem("brow_ps"), sem("brow_ready")
            tok_mv_ready = sem("tok_mv_ready")
            squared, patch_mm, raw_out, var_ready, std_ready = (
                sem("squared"), sem("patch_mm"), sem("raw_out"), sem("var_ready"), sem("std_ready"))
            block = ctx.enter_context(nc.Block())

            @block.sync
            def _(sp):
                sp.dma_start(w5s[:], w5.rearrange("p (s c d) -> p s c d", s=SHIFTS, c=WIN_CHUNKS)).then_inc(w_in, 16)
                sp.dma_start(gb5s[:], gb5.rearrange("p (a s c) -> p a s c", a=2, s=SHIFTS)).then_inc(w_in, 16)
                sp.dma_start(tokb[:], tok_b).then_inc(w_in, 16)
                sp.dma_start(con[:], consts).then_inc(consts_in, 16)

                def load(t, u):
                    if late(t, 2):
                        sp.wait_ge(patch_mm, t - 1)
                    sp.dma_start(winb[:, u].rearrange("p c n -> p (c n)"),
                                 win[ds(t, 1)].rearrange("a p n -> (a p) n")).then_inc(win_in[u], 16)
                sp.dma_start(ids_s[:], ids).then_inc(ids_in, 16)
                sp.dma_start(idn_s[:], ids_next).then_inc(misc_in, 16)
                sp.dma_start(link_s[:], link).then_inc(misc_in, 16)
                pairwise(sp, PAIRS, load)
                for dst, src in ((gb[:].rearrange("p a b -> p (a b)"), txt_gb), (wpT_hi[:], wprojT[0:P]), (wpT_lo[0:LO], wprojT[P:DM]),
                                 (wvT_hi[:], wvalT[0:P]), (wvT_lo[:], wvalT[P:DM]),
                                 (woT[:].rearrange("p a b -> p (a b)"), woutT), (old[:].rearrange("p a b -> p (a b)"), traces)):
                    sp.dma_start(dst, src).then_inc(text_in, 16)
                sp.wait_ge(padded, 1)
                sp.wait_ge(tok_in, 16 * B)
                sp.dma_start(tok2[0:SEQ - 2], tok[2:SEQ]).then_inc(tok2_in, 16)

            @block.gpsimd
            def _(pool):
                nc.gpsimd.memset(zeros[:], 0.0).then_inc(basics, 1)
                pool.wait_ge(basics, 1)
                nc.gpsimd.memset(ones[:], 1.0).then_inc(basics, 1)
                pool.wait_ge(basics, 2)
                nc.gpsimd.memset(eps5[:], 1e-5).then_inc(basics, 1)
                pool.wait_ge(basics, 3)
                nc.gpsimd.memset(eps6[:], 1e-6).then_inc(basics, 1)
                pool.wait_ge(basics, 4)
                nc.gpsimd.affine_select(out=ident[:], in_=zeros[:, 0:P], compare_op=ALU.not_equal, fill=1.0, base=0,
                                        pattern=[[-1, P]], channel_multiplier=1).then_inc(basics, 1)
                pool.wait_ge(basics, 5)
                nc.gpsimd.memset(tok2[96:P], 0.0).then_inc(padded, 1)
                pool.wait_ge(ids_in, 16)
                for b in range(B):
                    pool.indirect_dma_start(out=tok[:, b], out_offset=None, in_=wte,
                                            in_offset=bass.IndirectOffsetOnAxis(ap=ids_s[:, b:b + 1], axis=0)).then_inc(tok_in, 16)

            @block.scalar
            def _(act):

                def square(t, u):
                    act.wait_ge(win_in[u], (t // 2) * 16 + 16 if isinstance(t, int) else t * 8 + 16 - 8 * u)
                    nc.scalar.activation(sqb[:, u], winb[:, u], ACT.Square).then_inc(squared, 1)
                pairwise(act, PAIRS, square)
                act.wait_ge(var_ready, 1)
                nc.scalar.activation(st[:, :, 2:3], st[:, :, 2:3], ACT.Sqrt, bias=eps5[:]).then_inc(std_ready, 1)
                act.wait_ge(tok_mv_ready, 1)
                nc.scalar.activation(tok_rstd[:], tok_mv[:, :, 1], ACT.Sqrt, bias=eps5[:])

            @block.vector
            def _(dve):
                dve.wait_ge(w_in, 48)
                dve.wait_ge(consts_in, 16)
                for s in range(SHIFTS):
                    for c in range(WIN_CHUNKS):
                        g = gb5s[:, 0, s, c:c + 1]
                        if s == 0:
                            last = nc.vector.tensor_scalar(wc[:, c, 0:DM], w5s[:, s, c], g, None, MUL)
                        else:
                            last = nc.vector.scalar_tensor_tensor(wc[:, c, 0:DM], w5s[:, s, c], g, wc[:, c, 0:DM], MUL, ADD)
                    dve.drain()
                nc.vector.tensor_copy(wc[:, :, DM:DM + 1].rearrange("p c a -> p (c a)"), count).then_inc(products, 1)
                dve.wait_ge(colsum_ps, 1)
                nc.vector.tensor_scalar(colsum[:], psb[0:WIN_ROWS, 0:DM], -1.0, None, MUL).then_inc(colsum_used, 1)
                dve.drain()
                for c in range(WIN_CHUNKS):
                    last = nc.vector.scalar_tensor_tensor(wc[:, c, 0:DM], colsum[:], count[:, c:c + 1], wc[:, c, 0:DM], MUL, ADD)
                last.then_inc(wc_ready, 1)
                dve.wait_ge(beta_ps, 1)
                nc.vector.tensor_copy(brow1[:], psb[0:1, 512:512 + DM]).then_inc(brow_copied, 1)
                dve.wait_ge(brow_ps, 1)
                nc.vector.tensor_tensor(brow[:], psb[:, 1024:1024 + DM], tokb[:], ADD)
                dve.wait_ge(misc_in, 32)
                nc.vector.tensor_copy(idn[:], idn_s[:])
                nc.vector.tensor_copy(linkf[:], link_s[:])
                dve.drain()
                nc.vector.tensor_scalar(mask[:], idn[:], linkf[:, 0:1], None, ALU.is_equal)
                for l in range(1, 8):
                    dve.drain()
                    nc.vector.scalar_tensor_tensor(mask[:], idn[:], linkf[:, l:l + 1], mask[:], ALU.is_equal, MAX)
                dve.drain()
                nc.vector.tensor_scalar(mask[:], mask[:], con[:, C_VALID:C_VALID + 1], None, MUL)
                dve.drain()
                nc.vector.reduce_sum(masked_rows[:], mask[:], axis=AX)
                dve.wait_ge(tok_in, 16 * B)
                for b in range(B):
                    nc.vector.bn_stats(tok_st[:, b], tok[:, b])
                dve.drain()
                for b in range(B):
                    last = nc.vector.bn_aggr(tok_mv[:, b], tok_st[:, b])
                last.then_inc(tok_mv_ready, 1)

                def take_out(t, u):
                    bank = (6 + u) * 512
                    dve.wait_ge(patch_mm, t + 1)
                    nc.vector.tensor_copy(h[:, ds(t * 3, 1)].rearrange("p a d -> p (a d)"), psb[:, bank:bank + DM])
                    nc.vector.tensor_copy(st[:, ds(t, 1), 0:2].rearrange("p a d -> p (a d)"),
                                          psb[:, bank + DM:bank + DM + 2]).then_inc(raw_out, 1)
                pairwise(dve, PAIRS, take_out)
                dve.drain()
                nc.vector.tensor_tensor(st[:, :, 2], st[:, :, 0], st[:, :, 0], MUL)
                dve.drain()
                nc.vector.tensor_tensor(st[:, :, 2], st[:, :, 1], st[:, :, 2], SUB).then_inc(var_ready, 1)
                dve.wait_ge(std_ready, 1)
                nc.vector.reciprocal(st[:, :, 3], st[:, :, 2])
                dve.drain()
                for t in range(PAIRS):
                    nc.vector.scalar_tensor_tensor(h[:, 3 * t], h[:, 3 * t], st[:, t, 3:4], brow[:], MUL, ADD)

            @block.tensor
            def _(pe):
                pe.wait_ge(basics, 5)
                pe.wait_ge(w_in, 48)
                n = SHIFTS * WIN_CHUNKS
                for k in range(n):
                    s, c = divmod(k, WIN_CHUNKS)
                    last = nc.tensor.matmul(psb[0:1, 512:512 + DM], gb5s[:, 1, s, c:c + 1], w5s[:, s, c],
                                            start=(k == 0), stop=(k == n - 1))
                last.then_inc(beta_ps, 1)
                pe.wait_ge(products, 1)
                for c in range(WIN_CHUNKS):
                    last = nc.tensor.matmul(psb[0:WIN_ROWS, 0:DM], ones[0:WIN_ROWS, 0:WIN_ROWS], wc[:, c, 0:DM],
                                            start=(c == 0), stop=(c == WIN_CHUNKS - 1))
                last.then_inc(colsum_ps, 1)
                pe.wait_ge(brow_copied, 1)
                nc.tensor.matmul(psb[:, 1024:1024 + DM], ones[0:1, :], brow1[:], start=True, stop=True).then_inc(brow_ps, 1)
                pe.wait_ge(wc_ready, 1)

                def patches(t, u):
                    bank = (6 + u) * 512
                    pe.wait_ge(squared, t + 1)
                    if late(t, 2):
                        pe.wait_ge(raw_out, t - 1)
                    for c in range(WIN_CHUNKS):
                        nc.tensor.matmul(psb[:, bank:bank + DM + 1], winb[:, u, c], wc[:, c],
                                         start=(c == 0), stop=(c == WIN_CHUNKS - 1))
                    for c in range(WIN_CHUNKS):
                        last = nc.tensor.matmul(psb[:, bank + DM + 1:bank + DM + 2], sqb[:, u, c], count[:, c:c + 1],
                                                start=(c == 0), stop=(c == WIN_CHUNKS - 1))
                    last.then_inc(patch_mm, 1)
                pairwise(pe, PAIRS, patches)

        def text_stage(ctx):
            sb, sem = tools(ctx, "text")
            den = sb("den", [P, 3])
            xb, xm = sb("xb", [P, 2, DM + 1]), sb("xm", [P, 2, DM + 1])
            xa_hi, xa_lo = sb("xa_hi", [P, B, SEQ + 1]), sb("xa_lo", [LOA, B, SEQ + 1])
            xl_hi, xl_lo = sb("xl_hi", [P, 2, SEQ]), sb("xl_lo", [LOA, 2, SEQ])
            sq, qe = sb("sq", [P, 2, QW]), sb("qe", [P, 2, QW])
            ss, nrm, wgt = sb("ss", [P, 2, HM]), sb("nrm", [P, 2, HM]), sb("wgt", [P, 2, HM])
            gram, new = sb("gram", [P, MC, P]), sb("new", [P, MC, P])
            kept = sb("kept", [P, MC, DT])
            ca_hi, ca_lo = sb("ca_hi", [P, DM]), sb("ca_lo", [LOA, DM])
            m1_hi, m1_lo = sb("m1_hi", [P, QW]), sb("m1_lo", [LO, QW])
            wpa, rts = sb("wpa", [P, MC, 256]), sb("rts", [P, MC, 256])
            na_hi, na_lo = sb("na_hi", [P, DM]), sb("na_lo", [LOA, DM])
            started, beta_ps, wp_ready, mask_tot = sem("started"), sem("beta_ps"), sem("wp_ready"), sem("mask_tot")
            x_ready, xT_ps, xT_ready, q_ps, q_squared, ss_ready, nrm_ready, qe_ready, sums_mm = (
                sem("x_ready"), sem("xT_ps"), sem("xT_ready"), sem("q_ps"), sem("q_squared"), sem("ss_ready"), sem("nrm_ready"),
                sem("qe_ready"), sem("sums_mm"))
            sums_out, small_ps, m1_out, new_ready, wpa_out, rts_out, na_out = (
                sem("sums_out"), sem("small_ps"), sem("m1_out"), sem("new_ready"), sem("wpa_out"), sem("rts_out"), sem("na_out"))
            shift_ready, out_ps, out_done = sem("shift_ready"), sem("out_ps"), sem("out_done")
            GRAM, CROSS, XT, Q = 0, 512, 1024, 2048

            def schedule(eng, before, step):
                before()
                step(0, 0)
                step(1, 1)
                with eng.Fori(1, B // 2 - 1) as i:
                    step(i * 2, 0)
                    step(i * 2 + 1, 1)
                step(B - 2, 0)
                step(B - 1, 1)

            def more(b, k):
                return not isinstance(b, int) or b + k < B

            block = ctx.enter_context(nc.Block())

            @block.sync
            def _(sp):
                sp.dma_start(down_w[:], fw2.rearrange("p (e c d) -> p e c d", e=EXP, c=FC)).then_inc(experts_in, 16)
                for dst, src in ((wall_hi[:, 0:DM], qkvT[0:P, DM:2 * DM]), (wall_lo[0:LO, 0:DM], qkvT[P:DM, DM:2 * DM]),
                                 (wv_hi[:], qkvT[0:P, 2 * DM:3 * DM]), (wv_lo[0:LO], qkvT[P:DM, 2 * DM:3 * DM]),
                                 (wv_lo[LO:LOA], qv_bias[:, DM:2 * DM]), (wq_hi[:], qkvT[0:P, 0:DM]), (wq_lo[0:LO], qkvT[P:DM, 0:DM]),
                                 (wq_lo[LO:LOA], qv_bias[:, 0:DM]), (wk_hi[:], wk[0:P]), (wk_lo[:], wk[P:DM]),
                                 (w1_hi[:], w1s[0:P]), (w1_lo[:], w1s[P:DM]), (w1c_lo[LO:LOA], b1),
                                 (pT_hi[:], projT[0:P]), (pT_lo[0:LO], projT[P:DM]), (pT_lo[LO:LOA], proj_b),
                                 (wall_hi[:, 3 * DM:], lrT[0:P]), (wall_lo[0:LO, 3 * DM:], lrT[P:DM]), (wall_lo[LO:LOA, 3 * DM:], lr_b),
                                 (rows[:].rearrange("p a d -> p (a d)"), ttt_rows), (cols_[:].rearrange("p a d -> p (a d)"), ttt_cols)):
                    sp.dma_start(dst, src).then_inc(att_in, 16)

            @block.gpsimd
            def _(pool):
                nc.gpsimd.memset(xb[:, :, DM:DM + 1], 1.0).then_inc(started, 1)
                pool.wait_ge(started, 1)
                nc.gpsimd.memset(xa_hi[:, :, 0:1], 0.0).then_inc(started, 1)
                pool.wait_ge(started, 2)
                nc.gpsimd.memset(xa_lo[:, :, 0:1], 0.0).then_inc(started, 1)
                pool.wait_ge(started, 3)
                nc.gpsimd.memset(gram[:], 0.0).then_inc(started, 1)
                pool.wait_ge(started, 4)
                nc.gpsimd.memset(new[:], 0.0).then_inc(started, 1)

            @block.scalar
            def _(act):
                act.wait_ge(started, 5)

                def take_x(b, u):
                    xt = XT + 512 * u
                    act.wait_ge(xT_ps, b + 1)
                    nc.scalar.copy(xa_hi[:, ds(b, 1), 1:SEQ + 1].rearrange("p a s -> p (a s)"), psb[:, xt:xt + SEQ])
                    nc.scalar.copy(xa_lo[:, ds(b, 1), 1:SEQ + 1].rearrange("p a s -> p (a s)"), psb[0:LOA, xt + 256:xt + 256 + SEQ])
                    nc.scalar.copy(xl_hi[:, u], psb[:, xt:xt + SEQ])
                    nc.scalar.copy(xl_lo[:, u], psb[0:LOA, xt + 256:xt + 256 + SEQ]).then_inc(xT_ready, 1)

                def square(b, u):
                    act.wait_ge(q_ps, b + 1)
                    nc.scalar.activation(sq[:, u], psb[:, Q + 512 * u:Q + 512 * u + QW], ACT.Square).then_inc(q_squared, 1)

                def norms(b, u):
                    act.wait_ge(ss_ready, b + 1)
                    nc.scalar.activation(nrm[:, u], ss[:, u], ACT.Sqrt).then_inc(nrm_ready, 1)

                def before():
                    take_x(0, 0)

                def step(b, u):
                    square(b, u)
                    if more(b, 1):
                        take_x(b + 1, 1 - u)
                    norms(b, u)
                schedule(act, before, step)
                def pair_out(t):
                    for j in range(2):
                        act.wait_ge(out_ps, t * 2 + j + 1)
                        nc.scalar.copy(h[:, ds(t * 3 + 1 + j, 1)].rearrange("p a d -> p (a d)"),
                                       psb[:, Q + 512 * j:Q + 512 * j + DM]).then_inc(out_done, 1)
                pair_out(0)
                with act.Fori(1, PAIRS) as t:
                    pair_out(t)

            @block.vector
            def _(dve):
                dve.wait_ge(text_in, 16 * 7)
                dve.wait_ge(beta_ps, 1)
                nc.vector.tensor_copy(wpT_lo[LO:LOA], psb[LO:LOA, Q:Q + QW])
                nc.vector.tensor_scalar(wpT_hi[:], wpT_hi[:], gb[:, 0, 0:1], None, MUL)
                nc.vector.tensor_scalar(wpT_lo[0:LO], wpT_lo[0:LO], gb[0:LO, 0, 1:2], None, MUL).then_inc(wp_ready, 1)
                dve.wait_ge(mask_tot, 1)
                nc.vector.tensor_scalar(den[:, 0:1], psb[:, XT + 512:XT + 513], float(HM), 1.0, MUL, MAX)
                dve.drain()
                nc.vector.reciprocal(den[:, 1:2], den[:, 0:1])
                dve.drain()
                nc.vector.tensor_scalar(den[:, 2:3], den[:, 1:2], 0.1, None, MUL)
                nc.vector.tensor_scalar(den[:, 0:1], den[:, 1:2], -0.99, None, MUL)
                nc.vector.reciprocal(tok_rstd[:], tok_rstd[:])
                dve.drain()
                dve.wait_ge(started, 5)

                def normalise(b, u):
                    if late(b, 2):
                        dve.wait_ge(xT_ps, b - 1)
                        dve.wait_ge(sums_mm, b - 1)
                    nc.vector.tensor_scalar(xb[:, u, 0:DM], tok[:, ds(b, 1)].rearrange("p a d -> p (a d)"),
                                            tok_mv[:, ds(b, 1), 0:1].rearrange("p a d -> p (a d)"), tok_rstd[:, ds(b, 1)], SUB, MUL).then_inc(x_ready, 1)
                    dve.drain()
                    nc.vector.tensor_scalar(xm[:, u], xb[:, u], mask[:, ds(b, 1)], None, MUL)

                def query(b, u):
                    dve.wait_ge(q_squared, b + 1)
                    nc.vector.reduce_sum(ss[:, u], sq[:, u].rearrange("p (h d) -> p h d", h=HM), axis=AX).then_inc(ss_ready, 1)
                    dve.wait_ge(nrm_ready, b + 1)
                    nc.vector.tensor_scalar(nrm[:, u], nrm[:, u], 1e-8, None, MAX)
                    dve.drain()
                    nc.vector.reciprocal(wgt[:, u], nrm[:, u])
                    dve.drain()
                    nc.vector.tensor_scalar(wgt[:, u], wgt[:, u], mask[:, ds(b, 1)], None, MUL)
                    dve.drain()
                    nc.vector.tensor_tensor(qe[:, u].rearrange("p (h d) -> p h d", h=HM),
                                            psb[:, Q + 512 * u:Q + 512 * u + QW].rearrange("p (h d) -> p h d", h=HM),
                                            wgt[:, u].unsqueeze(2).to_broadcast([P, HM, DT]), MUL).then_inc(qe_ready, 1)

                def before():
                    normalise(0, 0)
                    normalise(1, 1)

                def step(b, u):
                    query(b, u)
                    if more(b, 2):
                        normalise(b + 2, u)
                schedule(dve, before, step)
                dve.wait_ge(sums_mm, B)
                for half in range(2):
                    r = slice(DT * half, DT * half + DT)
                    nc.vector.tensor_copy(gram[r, :, r], psb[r, GRAM:GRAM + 512].rearrange("p (c d) -> p c d", c=MC)[:, :, r])
                nc.vector.tensor_copy(ca_hi[:], psb[:, CROSS:CROSS + DM])
                nc.vector.tensor_copy(ca_lo[:], psb[0:LOA, CROSS + 256:CROSS + 256 + DM]).then_inc(sums_out, 1)
                dve.wait_ge(small_ps, 1)
                nc.vector.tensor_copy(wpa[:, 0:2, 0:DM + 1], psb[:, XT:XT + 512].rearrange("p (c d) -> p c d", c=2)[:, :, 0:DM + 1])
                nc.vector.tensor_copy(wpa[:, 2:4, 0:DM + 1], psb[:, XT + 512:XT + 1024].rearrange("p (c d) -> p c d", c=2)[:, :, 0:DM + 1]).then_inc(wpa_out, 1)
                dve.wait_ge(small_ps, 2)
                nc.vector.tensor_copy(m1_hi[:], psb[:, Q:Q + QW])
                nc.vector.tensor_copy(m1_lo[:], psb[0:LO, Q + 512:Q + 512 + QW]).then_inc(m1_out, 1)
                dve.wait_ge(small_ps, 3)
                nc.vector.tensor_scalar(kept[:], psb[:, CROSS:CROSS + MC * DT].rearrange("p (c d) -> p c d", c=MC), den[:, 0:1], None, MUL)
                dve.drain()
                nc.vector.scalar_tensor_tensor(kept[:], old[:], 0.99, kept[:], MUL, ADD)
                dve.drain()
                dve.wait_ge(small_ps, 4)
                for half in range(2):
                    r = slice(DT * half, DT * half + DT)
                    last = nc.vector.scalar_tensor_tensor(new[r, :, r], psb[r, GRAM:GRAM + 512].rearrange("p (c d) -> p c d", c=MC)[:, :, r],
                                                          den[r, 2:3], kept[r], MUL, ADD)
                last.then_inc(new_ready, 1)
                dve.wait_ge(small_ps, 5)
                nc.vector.tensor_copy(rts[:, 0:2, 0:DM + 1], psb[:, XT:XT + 512].rearrange("p (c d) -> p c d", c=2)[:, :, 0:DM + 1])
                nc.vector.tensor_copy(rts[:, 2:4, 0:DM + 1], psb[:, XT + 512:XT + 1024].rearrange("p (c d) -> p c d", c=2)[:, :, 0:DM + 1]).then_inc(rts_out, 1)
                dve.wait_ge(small_ps, 6)
                nc.vector.tensor_copy(na_hi[:], psb[:, CROSS:CROSS + DM])
                nc.vector.tensor_copy(na_lo[:], psb[0:LOA, CROSS + 256:CROSS + 256 + DM]).then_inc(na_out, 1)

                def shifted(b, u):
                    if late(b, 2):
                        dve.wait_ge(out_ps, b - 1)
                    nc.vector.tensor_copy(xl_hi[:, u], xa_hi[:, ds(b, 1), 0:SEQ].rearrange("p a s -> p (a s)"))
                    nc.vector.tensor_copy(xl_lo[:, u], xa_lo[:, ds(b, 1), 0:SEQ].rearrange("p a s -> p (a s)")).then_inc(shift_ready, 1)
                pairwise(dve, B, shifted)

            @block.tensor
            def _(pe):
                pe.wait_ge(text_in, 16 * 7)
                nc.tensor.matmul(psb[LO:LOA, Q:Q + QW], gb[:, 1, 0:1], wpT_hi[:], start=True, stop=False)
                nc.tensor.matmul(psb[LO:LOA, Q:Q + QW], gb[0:LO, 1, 1:2], wpT_lo[0:LO], start=False, stop=True).then_inc(beta_ps, 1)
                nc.tensor.matmul(psb[:, XT + 512:XT + 513], ones[:], masked_rows[:], start=True, stop=True).then_inc(mask_tot, 1)
                nc.tensor.matmul(psb[:, GRAM:GRAM + 512], ones[:], zeros[:], start=True, stop=True)
                nc.tensor.matmul(psb[:, CROSS:CROSS + 512], ones[:], zeros[:], start=True, stop=True)
                pe.wait_ge(tok2_in, 16)
                pe.wait_ge(wp_ready, 1)

                def project(b, u):
                    xt = XT + 512 * u
                    pe.wait_ge(x_ready, b + 1)
                    if late(b, 2):
                        pe.wait_ge(xT_ready, b - 1)
                    nc.tensor.transpose(psb[:, xt:xt + SEQ], xb[:, u, 0:P], ident[:])
                    nc.tensor.transpose(psb[0:LOA, xt + 256:xt + 256 + SEQ], xb[:, u, P:DM + 1], ident[:]).then_inc(xT_ps, 1)
                    pe.wait_ge(xT_ready, b + 1)
                    if late(b, 2):
                        pe.wait_ge(qe_ready, b - 1)
                    nc.tensor.matmul(psb[:, Q + 512 * u:Q + 512 * u + QW], xl_hi[:, u], wpT_hi[:], start=True, stop=False)
                    nc.tensor.matmul(psb[:, Q + 512 * u:Q + 512 * u + QW], xl_lo[:, u], wpT_lo[:], start=False, stop=True).then_inc(q_ps, 1)

                def sums(b, u):
                    pe.wait_ge(qe_ready, b + 1)
                    for c in range(MC):
                        r = slice(P * c, P * c + P)
                        nc.tensor.matmul(psb[:, GRAM + P * c:GRAM + P * c + P], qe[:, u, r], qe[:, u, r], start=False, stop=True,
                                         skip_group_check=True)
                    v = tok2[:, ds(b, 1)].rearrange("p a d -> p (a d)")
                    nc.tensor.matmul(psb[:, CROSS:CROSS + DM], xm[:, u, 0:P], v, start=False, stop=True, skip_group_check=True)
                    nc.tensor.matmul(psb[0:LOA, CROSS + 256:CROSS + 256 + DM], xm[:, u, P:DM + 1], v, start=False, stop=True,
                                     skip_group_check=True).then_inc(sums_mm, 1)

                def before():
                    project(0, 0)

                def step(b, u):
                    if more(b, 1):
                        project(b + 1, 1 - u)
                    sums(b, u)
                schedule(pe, before, step)
                for c in range(MC):
                    o = XT + 256 * c
                    nc.tensor.transpose(psb[:, o:o + P], wpT_hi[:, P * c:P * c + P], ident[:])
                    last = nc.tensor.transpose(psb[:, o + P:o + DM + 1], wpT_lo[:, P * c:P * c + P], ident[0:LOA, 0:LOA])
                last.then_inc(small_ps, 1)
                pe.wait_ge(sums_out, 1)
                for o, m in ((Q, slice(0, P)), (Q + 512, slice(P, DM))):
                    nc.tensor.matmul(psb[0:m.stop - m.start, o:o + QW], ca_hi[:, m], wpT_hi[:], start=True, stop=False)
                    last = nc.tensor.matmul(psb[0:m.stop - m.start, o:o + QW], ca_lo[:, m], wpT_lo[:], start=False, stop=True)
                last.then_inc(small_ps, 1)
                for c in range(MC):
                    last = nc.tensor.matmul(psb[:, CROSS + DT * c:CROSS + DT * c + DT], gram[:, c], old[:, c], start=True, stop=True)
                last.then_inc(small_ps, 1)
                pe.wait_ge(m1_out, 1)
                for c in range(MC):
                    r = slice(P * c, P * c + P)
                    nc.tensor.matmul(psb[:, GRAM + P * c:GRAM + P * c + P], m1_hi[:, r], wvT_hi[:, r], start=True, stop=False)
                    last = nc.tensor.matmul(psb[:, GRAM + P * c:GRAM + P * c + P], m1_lo[:, r], wvT_lo[:, r], start=False, stop=True)
                last.then_inc(small_ps, 1)
                pe.wait_ge(new_ready, 1)
                pe.wait_ge(wpa_out, 1)
                for c in range(MC):
                    last = nc.tensor.matmul(psb[:, XT + 256 * c:XT + 256 * c + DM + 1], new[:, c], wpa[:, c, 0:DM + 1], start=True, stop=True)
                last.then_inc(small_ps, 1)
                pe.wait_ge(rts_out, 1)
                for o, m in ((CROSS, slice(0, P)), (CROSS + 256, slice(P, DM + 1))):
                    for c in range(MC):
                        last = nc.tensor.matmul(psb[0:m.stop - m.start, o:o + DM], rts[:, c, m], woT[:, c], start=(c == 0), stop=(c == MC - 1))
                last.then_inc(small_ps, 1)
                pe.wait_ge(na_out, 1)

                def recall(b, u):
                    pe.wait_ge(shift_ready, b + 1)
                    if late(b, 2):
                        pe.wait_ge(out_done, b - 1)
                    o = Q + 512 * u
                    nc.tensor.matmul(psb[:, o:o + DM], xl_hi[:, u], na_hi[:], start=True, stop=False)
                    nc.tensor.matmul(psb[:, o:o + DM], xl_lo[:, u], na_lo[:], start=False, stop=True).then_inc(out_ps, 1)
                pairwise(pe, B, recall)

        def attention_stage(ctx):
            sb, sem = tools(ctx, "att")
            ZI, TI, KI, OI = 0, 3, 6, 9
            TR_HI, TR_LO = 12 * 256, 14 * 256
            av_hi, av_lo, av_b = sb("av_hi", [P, 1]), sb("av_lo", [LO, 1]), sb("av_b", [LOA, HA])
            gam2 = sb("gam2", [P, DM])
            st, mv, rstd, shift = sb("st", [P, TILES, 6]), sb("mv", [P, TILES, 2]), sb("rstd", [P, TILES]), sb("shift", [P, TILES])
            xn = sb("xn", [P, 2, 3, DM])
            xt_hi, xt_lo = sb("xt_hi", [P, 2, N3]), sb("xt_lo", [LOA, 2, N3])
            xq_hi, xq_lo = sb("xq_hi", [P, 2, N3]), sb("xq_lo", [LOA, 2, N3])
            rt_hi, rt_lo = sb("rt_hi", [P, 2, N3]), sb("rt_lo", [LOA, 2, N3])
            ka = sb("ka", [P, 2, 3, DM + 1])
            sqz, sqo, xz, gz, tz = (sb(n, [P, 3, DM]) for n in ("sqz", "sqo", "xz", "gz", "tz"))
            zz, zh = sb("zz", [P, 2, 3, DM]), sb("zh", [P, 2, 3, DM])
            var, std, inv, sg, sx, varo, stdo, invo = (sb(n, [P, 3 * HA]) for n in ("var", "std", "inv", "sg", "sx", "varo", "stdo", "invo"))
            ex = sb("ex", [P, 2, 3 * HA])
            w1n_hi, w1n_lo = sb("w1n_hi", [P, 2, P]), sb("w1n_lo", [LOA, 2, DM])
            bias0, w1_done, wz_ps, w_done = (sem(n) for n in ("bias0", "w1_done", "wz_ps", "w_done"))
            mv_ready, lnstd_ready, ln_ready, ones_set, std_ready, stdo_ready = (
                sem(n) for n in ("mv_ready", "lnstd_ready", "ln_ready", "ones_set", "std_ready", "stdo_ready"))
            xn_ready, xT_ps, xt_ready, xq_ps, xq_ready, wall_ps, k_ready, z_squared, e_ready, var_ready, t_read, z_ready = (
                sem(n) for n in ("xn_ready", "xT_ps", "xt_ready", "xq_ps", "xq_ready", "wall_ps", "k_ready", "z_squared", "e_ready",
                                 "var_ready", "t_read", "z_ready"))
            grad_ps, w1n_ready, o_ps, o_squared, varo_ready, zh_ready, zhT_ps, rt_ready, proj_ps, h_done = (
                sem(n) for n in ("grad_ps", "w1n_ready", "o_ps", "o_squared", "varo_ready", "zh_ready", "zhT_ps",
                                 "rt_ready", "proj_ps", "h_done"))
            grad_half = sem("grad_half")
            zcol, tcol = slice(DM, 2 * DM), slice(2 * DM, ALLC)
            block = ctx.enter_context(nc.Block())

            def schedule(eng, before, step):
                before()
                step(0, 0)
                step(1, 1)
                with eng.Fori(1, PAIRS // 2 - 1) as i:
                    step(i * 2, 0)
                    step(i * 2 + 1, 1)
                step(PAIRS - 2, 0)
                step(PAIRS - 1, 1)

            def more(t, k):
                return not isinstance(t, int) or t + k < PAIRS

            @block.sync
            def _(sp):
                sp.wait_ge(empty_set, 1)
                sp.dma_start(slots_x.rearrange("(s p) d -> p s d", p=P), empty[:].unsqueeze(1).to_broadcast([P, SLOTS, ROW])).then_inc(zeroed, 16)
                sp.dma_start(acc[B * TOKENS:B * TOKENS + P], empty[:, 0:DM]).then_inc(zeroed, 16)
                sp.wait_ge(zeroed, 32)

            @block.gpsimd
            def _(pool):
                nc.gpsimd.memset(wall_lo[LO:LOA, 0:DM], 0.0).then_inc(bias0, 1)
                pool.wait_ge(bias0, 1)
                nc.gpsimd.memset(xt_lo[LO:LOA], 1.0).then_inc(ones_set, 1)
                pool.wait_ge(ones_set, 1)
                nc.gpsimd.memset(xq_lo[LO:LOA], 1.0).then_inc(ones_set, 1)
                pool.wait_ge(ones_set, 2)
                nc.gpsimd.memset(rt_lo[LO:LOA], 1.0).then_inc(ones_set, 1)
                pool.wait_ge(ones_set, 3)
                nc.gpsimd.memset(ka[:, :, :, DM:DM + 1], 1.0).then_inc(ones_set, 1)

            @block.scalar
            def _(act):
                act.wait_ge(mv_ready, 1)
                nc.scalar.activation(rstd[:], mv[:, :, 1], ACT.Sqrt, bias=eps5[:]).then_inc(lnstd_ready, 1)
                act.wait_ge(ln_ready, 1)
                act.wait_ge(ones_set, 4)

                def normalise(t, u):
                    if late(t, 2):
                        act.wait_ge(xT_ps, t - 1)
                    for k in range(3):
                        last = nc.scalar.activation(xn[:, u, k], h[:, ds(t * 3 + k, 1)].rearrange("p a d -> p (a d)"), ACT.Identity,
                                                    bias=shift[:, ds(t * 3 + k, 1)], scale=rstd[:, ds(t * 3 + k, 1)])
                    last.then_inc(xn_ready, 1)

                def take_x(t, u):
                    act.wait_ge(xT_ps, t + 1)
                    if late(t, 2):
                        act.wait_ge(xq_ps, t - 1)
                    nc.scalar.copy(xt_hi[:, u], psb[:, TR_HI:TR_HI + N3])
                    nc.scalar.copy(xt_lo[0:LO, u], psb[0:LO, TR_LO:TR_LO + N3]).then_inc(xt_ready, 1)

                def take_q(t, u):
                    act.wait_ge(xq_ps, t + 1)
                    if late(t, 2):
                        act.wait_ge(rt_ready, t - 1)
                    nc.scalar.copy(xq_hi[:, u], psb[:, TR_HI:TR_HI + N3])
                    nc.scalar.copy(xq_lo[0:LO, u], psb[0:LO, TR_LO:TR_LO + N3]).then_inc(xq_ready, 1)

                def inner(t, u):
                    act.wait_ge(wall_ps, t + 1)
                    if late(t, 1):
                        act.wait_ge(var_ready, t)
                    nc.scalar.activation(sqz[:], ps[:, ZI:ZI + 3, 0:DM], ACT.Square).then_inc(z_squared, 1)
                    if late(t, 2):
                        act.wait_ge(grad_ps, t - 1)
                    nc.scalar.copy(ka[:, u, :, 0:DM], ps[:, KI:KI + 3, 0:DM]).then_inc(k_ready, 1)
                    if late(t, 2):
                        act.wait_ge(z_ready, t - 1)
                    nc.scalar.activation(ex[:, u].rearrange("p (k a) -> p k a", k=3), ps[:, TI:TI + 3, DM:DM + HA], ACT.Exp,
                                         scale=-1.0).then_inc(e_ready, 1)
                    act.wait_ge(var_ready, t + 1)
                    nc.scalar.activation(std[:], var[:], ACT.Sqrt, bias=eps6[:], scale=1.0 / HD).then_inc(std_ready, 1)

                def outer(t, u):
                    act.wait_ge(o_ps, t + 1)
                    if late(t, 1):
                        act.wait_ge(varo_ready, t)
                    nc.scalar.activation(sqo[:], ps[:, OI:OI + 3, 0:DM], ACT.Square).then_inc(o_squared, 1)
                    act.wait_ge(varo_ready, t + 1)
                    nc.scalar.activation(stdo[:], varo[:], ACT.Sqrt, bias=eps6[:], scale=1.0 / HD).then_inc(stdo_ready, 1)

                def before():
                    normalise(0, 0)
                    take_x(0, 0)
                    normalise(1, 1)
                    take_q(0, 0)
                    inner(0, 0)
                    take_x(1, 1)
                    inner(1, 1)

                def step(t, u):
                    if more(t, 2):
                        normalise(t + 2, u)
                    if more(t, 1):
                        take_q(t + 1, 1 - u)
                    if more(t, 2):
                        take_x(t + 2, u)
                    outer(t, u)
                    if more(t, 2):
                        inner(t + 2, u)
                schedule(act, before, step)

            @block.vector
            def _(dve):
                nc.vector.memset(empty[:], 0.0)
                dve.drain()
                nc.vector.tensor_copy(empty[:, DM:DM + 1], con[:, C_EMPTY:C_EMPTY + 1]).then_inc(empty_set, 1)
                for t in range(TILES):
                    nc.vector.bn_stats(st[:, t], h[:, t])
                dve.drain()
                for t in range(TILES):
                    last = nc.vector.bn_aggr(mv[:, t], st[:, t])
                last.then_inc(mv_ready, 1)
                dve.wait_ge(lnstd_ready, 1)
                nc.vector.reciprocal(rstd[:], rstd[:])
                dve.drain()
                nc.vector.scalar_tensor_tensor(shift[:], mv[:, :, 0], -1.0, rstd[:], MUL, MUL).then_inc(ln_ready, 1)
                dve.wait_ge(att_in, 16 * 21)
                nc.vector.reduce_sum(av_hi[:], w1_hi[:], axis=AX)
                nc.vector.reduce_sum(av_lo[:], w1_lo[:], axis=AX)
                nc.vector.reduce_sum(av_b[LO:LOA], w1c_lo[LO:LOA].rearrange("p (a d) -> p a d", a=HA), axis=AX)
                dve.drain()
                nc.vector.tensor_scalar(av_hi[:], av_hi[:], 1.0 / HD, None, MUL)
                nc.vector.tensor_scalar(av_lo[:], av_lo[:], 1.0 / HD, None, MUL)
                nc.vector.tensor_scalar(av_b[LO:LOA], av_b[LO:LOA], 1.0 / HD, None, MUL)
                dve.drain()
                nc.vector.tensor_scalar(w1_hi[:], w1_hi[:], av_hi[:], None, SUB)
                nc.vector.tensor_scalar(w1_lo[:], w1_lo[:], av_lo[:], None, SUB)
                rowb = w1c_lo[LO:LOA].rearrange("p (a d) -> p a d", a=HA)
                nc.vector.tensor_tensor(rowb, rowb, av_b[LO:LOA].unsqueeze(2).to_broadcast([1, HA, HD]), SUB)
                dve.drain()
                for w, c, blk, n in ((w1_hi, w1c_hi, blk_hi, P), (w1_lo, w1c_lo, blk_lo, LO)):
                    last = nc.vector.tensor_tensor(c[0:n].rearrange("p (a d) -> p a d", a=HA), w[0:n].unsqueeze(1).to_broadcast([n, HA, HD]),
                                                   blk[0:n].rearrange("p (a d) -> p a d", a=HA), MUL)
                last.then_inc(w1_done, 1)
                nc.vector.tensor_tensor(gam2[:], rows[:, 0], rows[:, 0], MUL)
                dve.wait_ge(bias0, 1)
                nc.vector.tensor_tensor(wv_hi[:], wv_hi[:], wall_hi[:, 0:DM], SUB)
                nc.vector.tensor_tensor(wv_lo[0:LO], wv_lo[0:LO], wall_lo[0:LO, 0:DM], SUB)
                nc.vector.tensor_tensor(wv_lo[LO:LOA], wv_lo[LO:LOA], rows[LO:LOA, 1], SUB)
                dve.drain()
                nc.vector.tensor_tensor(wall_hi[:, 2 * DM:3 * DM], wv_hi[:], rows[:, 0], MUL)
                nc.vector.tensor_tensor(wall_lo[:, 2 * DM:3 * DM], wv_lo[:], rows[0:LOA, 0], MUL)
                dve.wait_ge(wz_ps, 1)
                nc.vector.tensor_copy(wall_hi[:, zcol], ps[:, 0, 0:DM])
                nc.vector.tensor_copy(wall_lo[0:LO, zcol], ps[0:LO, 2, 0:DM])
                nc.vector.tensor_copy(wall_lo[LO:LOA, zcol], w1c_lo[LO:LOA])
                nc.vector.tensor_tensor(pT_lo[LO:LOA], pT_lo[LO:LOA], ps[LO:LOA, 4, 0:DM], ADD).then_inc(w_done, 1)

                def heads(ap):
                    return ap.rearrange("p k (a d) -> p (k a) d", a=HA)

                def per_head(ap):
                    return ap.unsqueeze(2).to_broadcast([P, 3 * HA, HD])

                def zslots(s):
                    return ps[:, s:s + 3, 0:DM].rearrange("p k (a d) -> p k a d", a=HA)

                def four(ap):
                    return ap.rearrange("p k (a d) -> p k a d", a=HA)

                def per_head4(ap):
                    return ap[:].rearrange("p (k a) -> p k a", k=3).unsqueeze(3).to_broadcast([P, 3, HA, HD])

                def squares(t):
                    dve.wait_ge(z_squared, t + 1)
                    nc.vector.reduce_sum(var[:], heads(sqz[:]), axis=AX).then_inc(var_ready, 1)

                def normalised(t):
                    dve.wait_ge(std_ready, t + 1)
                    nc.vector.reciprocal(inv[:], std[:])
                    dve.drain()
                    nc.vector.tensor_tensor(four(xz[:]), zslots(ZI), per_head4(inv), MUL)
                    dve.drain()
                    nc.vector.tensor_tensor(gz[:], xz[:], gam2[:].unsqueeze(1).to_broadcast([P, 3, DM]), MUL)
                    dve.drain()
                    dve.wait_ge(e_ready, t + 1)
                    nc.vector.tensor_tensor(gz[:], gz[:], ps[:, TI:TI + 3, 0:DM], SUB).then_inc(t_read, 1)

                def sums(t, u):
                    nc.vector.tensor_scalar(ex[:, u], ex[:, u], 1.0, None, ADD)
                    dve.drain()
                    nc.vector.tensor_tensor(tz[:], gz[:], xz[:], MUL)
                    nc.vector.reciprocal(ex[:, u], ex[:, u])
                    nc.vector.reduce_sum(sg[:], heads(gz[:]), axis=AX)
                    dve.drain()
                    nc.vector.scalar_tensor_tensor(ex[:, u], ex[:, u], 1.0 / (HD * HD * TOKENS), inv[:], MUL, MUL)

                def centred(t, u):
                    nc.vector.reduce_sum(sx[:], heads(tz[:]), axis=AX)
                    nc.vector.scalar_tensor_tensor(heads(gz[:]), heads(gz[:]), float(HD), per_head(sg[:]), MUL, SUB)
                    dve.drain()
                    nc.vector.tensor_tensor(heads(tz[:]), heads(xz[:]), per_head(sx[:]), MUL)
                    dve.drain()

                def scaled(t, u):
                    nc.vector.tensor_tensor(gz[:], gz[:], tz[:], SUB)
                    dve.drain()
                    if late(t, 2):
                        dve.wait_ge(grad_ps, t - 1)
                    nc.vector.tensor_tensor(heads(zz[:, u]), heads(gz[:]), per_head(ex[:, u]), MUL).then_inc(z_ready, 1)

                def new_weights(t, u):
                    dve.wait_ge(grad_ps, t + 1)
                    if late(t, 1):
                        dve.wait_ge(o_ps, t)
                    nc.vector.tensor_tensor(w1n_hi[:], ps[:, OI].rearrange("p (j d) -> p j d", j=2), blk_hi[:, 0:P].unsqueeze(1).to_broadcast([P, 2, P]), MUL)
                    nc.vector.tensor_tensor(w1n_lo[:], ps[0:LOA, OI + 1:OI + 3, 0:DM], blk_lo.unsqueeze(1).to_broadcast([LOA, 2, DM]), MUL)
                    dve.drain()
                    nc.vector.tensor_tensor(w1n_hi[:], w1c_hi[:, 0:P].unsqueeze(1).to_broadcast([P, 2, P]), w1n_hi[:], SUB)
                    nc.vector.tensor_tensor(w1n_lo[:], w1c_lo[:].unsqueeze(1).to_broadcast([LOA, 2, DM]), w1n_lo[:], SUB).then_inc(w1n_ready, 1)

                def outer(t, u):
                    dve.wait_ge(o_squared, t + 1)
                    nc.vector.reduce_sum(varo[:], heads(sqo[:]), axis=AX).then_inc(varo_ready, 1)
                    dve.wait_ge(stdo_ready, t + 1)
                    nc.vector.reciprocal(invo[:], stdo[:])
                    dve.drain()
                    nc.vector.tensor_tensor(four(zh[:, u]), zslots(OI), per_head4(invo), MUL).then_inc(zh_ready, 1)

                def with_queries(t, u):
                    dve.wait_ge(zhT_ps, t + 1)
                    nc.vector.scalar_tensor_tensor(rt_hi[:, u], psb[:, TR_HI:TR_HI + N3], cols_[:, 0, 0:1], xq_hi[:, u], MUL, ADD)
                    nc.vector.scalar_tensor_tensor(rt_lo[0:LO, u], psb[0:LO, TR_LO:TR_LO + N3], cols_[0:LO, 0, 1:2], xq_lo[0:LO, u],
                                                   MUL, ADD).then_inc(rt_ready, 1)

                def add(t, u):
                    dve.wait_ge(proj_ps, t + 1)
                    nc.vector.tensor_tensor(h[:, ds(t * 3, 3)], h[:, ds(t * 3, 3)], ps[:, OI:OI + 3, 0:DM], ADD).then_inc(h_done, 1)

                def before():
                    squares(0)
                    normalised(0)
                    sums(0, 0)
                    centred(0, 0)
                    scaled(0, 0)
                    squares(1)

                def step(t, u):
                    if more(t, 1):
                        normalised(t + 1)
                    new_weights(t, u)
                    if more(t, 1):
                        sums(t + 1, 1 - u)
                    outer(t, u)
                    if more(t, 1):
                        centred(t + 1, 1 - u)
                    with_queries(t, u)
                    if more(t, 1):
                        scaled(t + 1, 1 - u)
                    if more(t, 2):
                        squares(t + 2)
                    add(t, u)
                schedule(dve, before, step)

            @block.tensor
            def _(pe):
                pe.wait_ge(att_in, 16 * 21)
                pe.wait_ge(w1_done, 1)
                nc.tensor.matmul(ps[:, 0, 0:DM], wk_hi[:, 0:P], w1c_hi[:], start=True, stop=False)
                nc.tensor.matmul(ps[:, 0, 0:DM], wk_lo[:, 0:P], w1c_lo[0:LO], start=False, stop=True)
                nc.tensor.matmul(ps[0:LO, 2, 0:DM], wk_hi[:, P:DM], w1c_hi[:], start=True, stop=False)
                nc.tensor.matmul(ps[0:LO, 2, 0:DM], wk_lo[:, P:DM], w1c_lo[0:LO], start=False, stop=True)
                nc.tensor.matmul(ps[LO:LOA, 4, 0:DM], cols_[:, 1, 0:1], pT_hi[:], start=True, stop=False)
                nc.tensor.matmul(ps[LO:LOA, 4, 0:DM], cols_[0:LO, 1, 1:2], pT_lo[0:LO], start=False, stop=True).then_inc(wz_ps, 1)
                pe.wait_ge(w_done, 1)

                def tile_cols(k):
                    return slice(P * k, P * k + P)

                def transposes(t, u):
                    pe.wait_ge(xn_ready, t + 1)
                    if isinstance(t, int) and t == 1:
                        pe.wait_ge(xq_ready, 1)
                    if late(t, 2):
                        pe.wait_ge(xq_ready, t)
                    for k in range(3):
                        nc.tensor.transpose(psb[:, TR_HI + P * k:TR_HI + P * k + P], xn[:, u, k, 0:P], ident[:])
                        last = nc.tensor.transpose(psb[0:LO, TR_LO + P * k:TR_LO + P * k + P], xn[:, u, k, P:DM], ident[:])
                    last.then_inc(xT_ps, 1)

                def queries(t, u):
                    pe.wait_ge(xt_ready, t + 1)
                    if late(t, 2):
                        pe.wait_ge(rt_ready, t - 1)
                    nc.tensor.matmul(psb[:, TR_HI:TR_HI + N3], wq_hi[:, 0:P], xt_hi[:, u], start=True, stop=False)
                    nc.tensor.matmul(psb[:, TR_HI:TR_HI + N3], wq_lo[:, 0:P], xt_lo[:, u], start=False, stop=True)
                    nc.tensor.matmul(psb[0:LO, TR_LO:TR_LO + N3], wq_hi[:, P:DM], xt_hi[:, u], start=True, stop=False)
                    nc.tensor.matmul(psb[0:LO, TR_LO:TR_LO + N3], wq_lo[:, P:DM], xt_lo[:, u], start=False, stop=True).then_inc(xq_ps, 1)

                def inner(t, u):
                    pe.wait_ge(xt_ready, t + 1)
                    if late(t, 1):
                        pe.wait_ge(t_read, t)
                        pe.wait_ge(k_ready, t)
                    for k in range(3):
                        for slot, c in ((ZI + k, zcol), (TI + k, tcol), (KI + k, slice(0, DM))):
                            if k == 2 and slot == KI + k and late(t, 2):
                                pe.wait_ge(zh_ready, t - 1)
                            n = c.stop - c.start
                            nc.tensor.matmul(ps[:, slot, 0:n], xt_hi[:, u, tile_cols(k)], wall_hi[:, c], start=True, stop=False)
                            last = nc.tensor.matmul(ps[:, slot, 0:n], xt_lo[:, u, tile_cols(k)], wall_lo[:, c], start=False, stop=True)
                    last.then_inc(wall_ps, 1)

                def gradient(t, u):
                    pe.wait_ge(z_ready, t + 1)
                    pe.wait_ge(k_ready, t + 2 if more(t, 1) else t + 1)
                    if late(t, 1):
                        pe.wait_ge(h_done, t)
                    for j in range(2):
                        rows_ = slice(64 * j, 64 * j + PATCHES)
                        hi, lo = ps[:, OI, P * j:P * j + P], ps[0:LOA, OI + 1 + j, 0:DM]
                        nc.tensor.matmul(hi, ka[:, u, 1 + j, 0:P], zz[:, u, 1 + j, 0:P], start=True, stop=False)
                        nc.tensor.matmul(hi, ka[rows_, u, 0, 0:P], zz[rows_, u, 0, 0:P], start=False, stop=True)
                        nc.tensor.matmul(lo, ka[:, u, 1 + j, P:DM + 1], zz[:, u, 1 + j], start=True, stop=False)
                        last = nc.tensor.matmul(lo, ka[rows_, u, 0, P:DM + 1], zz[rows_, u, 0], start=False, stop=True)
                        last.then_inc(grad_ps if j else grad_half, 1)
                        if j == 0:
                            pe.wait_ge(grad_half, t + 1)

                def outer(t, u):
                    pe.wait_ge(w1n_ready, t + 1)
                    pe.wait_ge(xq_ready, t + 1)
                    for j in range(2):
                        c = slice(64 * j, 64 * j + 64)
                        for o, q in ((ps[c, OI], c), (ps[:, OI + 1 + j], tile_cols(1 + j))):
                            nc.tensor.matmul(o[:, 0:DM], xq_lo[:, u, q], w1n_lo[:, j], start=True, stop=True)
                            last = nc.tensor.matmul(o[:, 0:P], xq_hi[:, u, q], w1n_hi[:, j], start=False, stop=True, skip_group_check=True)
                    last.then_inc(o_ps, 1)

                def back(t, u):
                    pe.wait_ge(zh_ready, t + 1)
                    if more(t, 2):
                        pe.wait_ge(xt_ready, t + 3)
                    elif more(t, 1):
                        pe.wait_ge(xq_ready, t + 2)
                    for k in range(3):
                        nc.tensor.transpose(psb[:, TR_HI + P * k:TR_HI + P * k + P], zh[:, u, k, 0:P], ident[:])
                        last = nc.tensor.transpose(psb[0:LO, TR_LO + P * k:TR_LO + P * k + P], zh[:, u, k, P:DM], ident[:])
                    last.then_inc(zhT_ps, 1)

                def project(t, u):
                    pe.wait_ge(rt_ready, t + 1)
                    if more(t, 2):
                        pe.wait_ge(k_ready, t + 3)
                    for k in range(3):
                        nc.tensor.matmul(ps[:, OI + k, 0:DM], rt_hi[:, u, tile_cols(k)], pT_hi[:], start=True, stop=False)
                        last = nc.tensor.matmul(ps[:, OI + k, 0:DM], rt_lo[:, u, tile_cols(k)], pT_lo[:], start=False, stop=True)
                    last.then_inc(proj_ps, 1)

                def before():
                    transposes(0, 0)
                    queries(0, 0)
                    inner(0, 0)
                    transposes(1, 1)
                    inner(1, 1)

                def step(t, u):
                    if more(t, 1):
                        queries(t + 1, 1 - u)
                    gradient(t, u)
                    if more(t, 2):
                        transposes(t + 2, u)
                    outer(t, u)
                    if more(t, 2):
                        inner(t + 2, u)
                    back(t, u)
                    project(t, u)
                schedule(pe, before, step)

        def route_stage(ctx):
            sb, sem = tools(ctx, "route")
            TR_HI, TR_LO, LG = 0, 512, 1024
            PART = FF // 2
            rt_hi, rt_lo = sb("rt_hi", [P, EXP]), sb("rt_lo", [LO, EXP])
            st, mv = sb("st", [P, TILES, 6]), sb("mv", [P, TILES, 2])
            r1, shift, r2 = sb("r1", [P, TILES]), sb("shift", [P, TILES]), sb("r2", [P, TILES])
            xu = sb("xu", [P, 2, 3, DM])
            xs = sb("xs", [P, 2, 3, DM])
            xf = sb("xf", [P, TILES, ROW])
            ft_hi, ft_lo = sb("ft_hi", [P, 2, N3]), sb("ft_lo", [LO, 2, N3])
            logit, top, topf = (sb(n, [P, TILES, 8]) for n in ("logit", "top", "topf"))
            topi = sb("topi", [P, TILES, 8], u32)
            oh1, oh2, sel, pos, prod = (sb(n, [P, TILES, EXP]) for n in ("oh1", "oh2", "sel", "pos", "prod"))
            tot, cum, keep = (sb(n, [P, EXP, TILES]) for n in ("tot", "cum", "keep"))
            gap, posf = sb("gap", [P, TILES]), sb("posf", [P, 2, TILES])
            iota_e, iota_s, iota_k = sb("iota_e", [P, EXP]), sb("iota_s", [P, SLOTS]), sb("iota_k", [P, MAXT])
            put_row = [sb("put_row1", [P, TILES], i32), sb("put_row2", [P, TILES], i32)]
            over = sb("over", [P, EXP, MAXT])
            tiles_e, tiles_to = sb("tiles_e", [P, EXP]), sb("tiles_to", [P, EXP])
            past, se, base = sb("past", [P, SLOTS, EXP]), sb("se", [P, SLOTS]), sb("base", [P, EXP])
            (w_in, iotas, mv_ready, std1, v2_ready, std2, ln_ready, xu_ready, xf_ready, xT_ps, xT_ready, logit_ps, logits_out,
             gap_ready, exp_ready, sel_ready, rank_ps, index_ready, scattered, regated) = (sem(n) for n in (
                 "w_in", "iotas", "mv_ready", "std1", "v2_ready", "std2", "ln_ready", "xu_ready", "xf_ready", "xT_ps", "xT_ready",
                 "logit_ps", "logits_out", "gap_ready", "exp_ready", "sel_ready", "rank_ps", "index_ready", "scattered", "regated"))
            stage = sb("stage", [P, 2, 2, PART])
            stage_in, rounded, split, summed = [sem("stage_in0"), sem("stage_in1")], sem("rounded"), sem("split"), sem("summed")
            block = ctx.enter_context(nc.Block())

            @block.sync
            def _(sp):
                sp.dma_start(rt_hi[:], router[0:P]).then_inc(w_in, 16)
                sp.dma_start(rt_lo[:], router[P:DM]).then_inc(w_in, 16)
                sp.dma_start(fgb[:].rearrange("p a b -> p (a b)"), ffn_gb).then_inc(w_in, 16)
                for t in range(PAIRS):
                    sp.wait_ge(xf_ready, t + 1)
                    for j in range(2):
                        r = (2 * t + j) * TOKENS
                        sp.dma_start(acc[r:r + PATCHES], h[64 * j:64 * j + PATCHES, 3 * t]).then_inc(summed, 16)
                        sp.dma_start(acc[r + PATCHES:r + TOKENS], h[:, 3 * t + 1 + j]).then_inc(summed, 16)

                def load_weights(n, u):
                    if late(n, 2):
                        sp.wait_ge(split, n - 1)
                    f = ds(n * PART, PART)
                    sp.dma_start(stage[:, u, 0], fw1[0:P, f]).then_inc(stage_in[u], 16)
                    sp.dma_start(stage[0:LO, u, 1], fw1[P:DM, f]).then_inc(stage_in[u], 16)
                    sp.dma_start(stage[LO:P, u, 1], fw1[P:DM, f]).then_inc(stage_in[u], 16)
                pairwise(sp, EXP * FF // PART, load_weights)
                sp.wait_ge(summed, 16 * 4 * PAIRS)

            @block.gpsimd
            def _(pool):
                nc.gpsimd.iota(iota_e[:], [[1, EXP]], base=0, channel_multiplier=0, allow_small_or_imprecise_dtypes=True).then_inc(iotas, 1)
                pool.wait_ge(iotas, 1)
                nc.gpsimd.iota(iota_s[:], [[1, SLOTS]], base=0, channel_multiplier=0, allow_small_or_imprecise_dtypes=True).then_inc(iotas, 1)
                pool.wait_ge(iotas, 2)
                nc.gpsimd.iota(iota_k[:], [[P, MAXT]], base=0, channel_multiplier=0, allow_small_or_imprecise_dtypes=True).then_inc(iotas, 1)
                pool.wait_ge(index_ready, 1)
                for k in range(2):
                    if k:
                        pool.wait_ge(scattered, 16 * TILES)
                        nc.gpsimd.tensor_copy(xf[:, :, DM + 1], gate[:, 1]).then_inc(regated, 1)
                        pool.wait_ge(regated, 1)
                    for t in range(TILES):
                        pool.indirect_dma_start(out=slots_x, out_offset=bass.IndirectOffsetOnAxis(ap=put_row[k][:, t:t + 1], axis=0),
                                                in_=xf[:, t], in_offset=None, bounds_check=SLOTS * P - 1,
                                                oob_is_err=False).then_inc(scattered, 16)
                pool.wait_ge(scattered, 16 * 2 * TILES)

            @block.scalar
            def _(act):
                act.wait_ge(mv_ready, 1)
                nc.scalar.activation(r1[:], mv[:, :, 1], ACT.Sqrt, bias=eps5[:]).then_inc(std1, 1)
                act.wait_ge(v2_ready, 1)
                nc.scalar.activation(r2[:], r2[:], ACT.Sqrt, bias=eps5[:]).then_inc(std2, 1)
                act.wait_ge(ln_ready, 1)
                act.wait_ge(w_in, 48)

                def pair(t, u):
                    if late(t, 2):
                        act.wait_ge(xf_ready, t - 1)
                    for k in range(3):
                        last = nc.scalar.activation(xu[:, u, k], h[:, ds(t * 3 + k, 1)].rearrange("p a d -> p (a d)"), ACT.Identity,
                                                    bias=shift[:, ds(t * 3 + k, 1)], scale=r1[:, ds(t * 3 + k, 1)])
                    last.then_inc(xu_ready, 1)
                    act.wait_ge(xT_ps, t + 1)
                    if late(t, 2):
                        act.wait_ge(logit_ps, t - 1)
                    nc.scalar.activation(ft_hi[:, u], psb[:, TR_HI:TR_HI + N3], ACT.Identity, bias=fgb[:, 1, 0:1], scale=fgb[:, 0, 0:1])
                    nc.scalar.activation(ft_lo[:, u], psb[0:LO, TR_LO:TR_LO + N3], ACT.Identity, bias=fgb[0:LO, 1, 1:2],
                                         scale=fgb[0:LO, 0, 1:2]).then_inc(xT_ready, 1)
                pairwise(act, PAIRS, pair)
                act.wait_ge(gap_ready, 1)
                nc.scalar.activation(gap[:], gap[:], ACT.Exp).then_inc(exp_ready, 1)

                def round_weights(n, u):
                    c = ds(n * PART, PART)
                    act.wait_ge(stage_in[u], (n // 2) * 48 + 48 if isinstance(n, int) else n * 24 + 48 - 24 * u)
                    nc.scalar.copy(upA_hi[:, c], stage[:, u, 0])
                    nc.scalar.copy(upB_hi[:, c], stage[:, u, 1]).then_inc(rounded, 1)
                pairwise(act, EXP * FF // PART, round_weights)

            @block.vector
            def _(dve):
                for t in range(TILES):
                    nc.vector.bn_stats(st[:, t], h[:, t])
                dve.drain()
                for t in range(TILES):
                    last = nc.vector.bn_aggr(mv[:, t], st[:, t])
                last.then_inc(mv_ready, 1)
                dve.wait_ge(std1, 1)
                nc.vector.reciprocal(r1[:], r1[:])
                dve.drain()
                nc.vector.scalar_tensor_tensor(shift[:], mv[:, :, 0], -1.0, r1[:], MUL, MUL)
                nc.vector.tensor_tensor(r2[:], r1[:], r1[:], MUL)
                dve.drain()
                nc.vector.tensor_tensor(r2[:], r2[:], mv[:, :, 1], MUL).then_inc(v2_ready, 1)
                dve.wait_ge(std2, 1)
                nc.vector.reciprocal(r2[:], r2[:]).then_inc(ln_ready, 1)
                dve.drain()

                def pair(t, u):
                    dve.wait_ge(xu_ready, t + 1)
                    nc.vector.tensor_tensor(xf[:, ds(t * 3, 3), 0:DM], xu[:, u], r2[:, ds(t * 3, 3)].unsqueeze(2).to_broadcast([P, 3, DM]), MUL)
                    nc.vector.tensor_tensor(h[:, ds(t * 3, 3)], h[:, ds(t * 3, 3)], xu[:, u], ADD)
                    if late(t, 2):
                        dve.wait_ge(xT_ps, t - 1)
                    nc.vector.tensor_tensor(xs[:, u], xu[:, u], r2[:, ds(t * 3, 3)].unsqueeze(2).to_broadcast([P, 3, DM]), MUL).then_inc(xf_ready, 1)
                    dve.wait_ge(logit_ps, t + 1)
                    nc.vector.tensor_copy(logit[:, ds(t * 3, 3)], psb[:, LG + 512 * u:LG + 512 * u + 24].rearrange("p (k e) -> p k e", k=3)).then_inc(logits_out, 1)
                pairwise(dve, PAIRS, pair)
                dve.drain()
                for t in range(TILES):
                    nc.vector.max(top[:, t], logit[:, t])
                dve.drain()
                for t in range(TILES):
                    nc.vector.max_index(topi[:, t], top[:, t], logit[:, t])
                nc.vector.tensor_tensor(gap[:], top[:, :, 1], top[:, :, 0], SUB).then_inc(gap_ready, 1)
                dve.drain()
                nc.vector.tensor_copy(topf[:], topi[:])
                dve.wait_ge(iotas, 3)
                dve.drain()

                def tiles_bc(ap):
                    return ap.unsqueeze(2).to_broadcast([P, TILES, EXP])
                experts_bc = iota_e[:].unsqueeze(1).to_broadcast([P, TILES, EXP])
                valid = con[:, C_TOKV:C_TOKV + TILES]
                nc.vector.tensor_tensor(oh1[:], experts_bc, tiles_bc(topf[:, :, 0]), ALU.is_equal)
                nc.vector.tensor_tensor(oh2[:], experts_bc, tiles_bc(topf[:, :, 1]), ALU.is_equal)
                dve.drain()
                nc.vector.tensor_tensor(oh1[:], oh1[:], tiles_bc(valid), MUL)
                nc.vector.tensor_tensor(oh2[:], oh2[:], tiles_bc(valid), MUL)
                dve.drain()
                nc.vector.tensor_tensor(sel[:], oh1[:], oh2[:], ADD).then_inc(sel_ready, 1)
                dve.wait_ge(exp_ready, 1)
                nc.vector.tensor_scalar(gate[:, 0], gap[:], 1.0, None, ADD)
                nc.vector.memset(keep[:], 1.0)
                dve.drain()
                nc.vector.reciprocal(gate[:, 0], gate[:, 0])
                nc.vector.memset(keep[:, :, 0:1], 0.0)
                dve.drain()
                nc.vector.tensor_tensor(gate[:, 1], gap[:], gate[:, 0], MUL)
                nc.vector.tensor_copy(xf[:, :, DM], con[:, C_ROW:C_ROW + TILES])
                nc.vector.tensor_copy(xf[:, :, DM + 1], gate[:, 0])
                dve.wait_ge(rank_ps, 1)
                nc.vector.tensor_copy(tot[:], psb[:, 512:512 + TILES * EXP].rearrange("p (t e) -> p e t", e=EXP))
                dve.drain()
                nc.vector.tensor_tensor_scan(cum[:].rearrange("p e t -> p (e t)"), keep[:].rearrange("p e t -> p (e t)"),
                                             tot[:].rearrange("p e t -> p (e t)"), 0.0, MUL, ADD)
                dve.drain()
                nc.vector.tensor_tensor(over[:], cum[:, :, TILES - 1:TILES].to_broadcast([P, EXP, MAXT]),
                                        iota_k[:].unsqueeze(1).to_broadcast([P, EXP, MAXT]), ALU.is_gt)
                nc.vector.tensor_tensor(tot[:], cum[:], tot[:], SUB)
                dve.drain()
                nc.vector.reduce_sum(tiles_e[:], over[:], axis=AX)
                dve.drain()
                nc.vector.tensor_tensor_scan(tiles_to[:], ones[:, 0:EXP], tiles_e[:], 0.0, MUL, ADD)
                dve.drain()
                nc.vector.tensor_tensor(base[:], tiles_to[:], tiles_e[:], SUB)
                dve.drain()
                nc.vector.tensor_scalar(base[:], base[:], float(P), None, MUL)
                dve.drain()
                nc.vector.tensor_tensor(pos[:], psb[:, 0:TILES * EXP].rearrange("p (t e) -> p t e", e=EXP),
                                        base[:].unsqueeze(1).to_broadcast([P, TILES, EXP]), ADD)
                dve.drain()
                nc.vector.tensor_tensor(pos[:], pos[:], tot[:].rearrange("p e t -> p t e"), ADD)
                nc.vector.tensor_scalar(gap[:], valid, -float(SLOTS * P), float(SLOTS * P), MUL, ADD)
                dve.drain()
                for k, oh in enumerate((oh1, oh2)):
                    nc.vector.tensor_tensor(prod[:], oh[:], pos[:], MUL)
                    dve.drain()
                    nc.vector.reduce_sum(posf[:, k], prod[:], axis=AX)
                    dve.drain()
                    last = nc.vector.tensor_tensor(put_row[k][:], posf[:, k], gap[:], ADD)
                last.then_inc(index_ready, 1)
                nc.vector.tensor_tensor(past[:], iota_s[:].unsqueeze(2).to_broadcast([P, SLOTS, EXP]),
                                        tiles_to[:].unsqueeze(1).to_broadcast([P, SLOTS, EXP]), ALU.is_ge)
                dve.drain()
                nc.vector.reduce_sum(se[:], past[:], axis=AX)
                dve.drain()
                nc.vector.tensor_scalar(slot_expert[:], se[:], float(EXP - 1), None, ALU.min)

                def low_parts(n, u):
                    c = ds(n * PART, PART)
                    dve.wait_ge(rounded, n + 1)
                    nc.vector.tensor_tensor(upA_lo[:, c], stage[:, u, 0], upA_hi[:, c].bitcast(f32), SUB)
                    nc.vector.tensor_tensor(upB_lo[:, c], stage[0:LO, u, 1], upB_hi[0:LO, c].bitcast(f32), SUB).then_inc(split, 1)
                pairwise(dve, EXP * FF // PART, low_parts)

            @block.tensor
            def _(pe):
                pe.wait_ge(w_in, 48)

                def pair(t, u):
                    pe.wait_ge(xf_ready, t + 1)
                    if late(t, 1):
                        pe.wait_ge(xT_ready, t)
                    for k in range(3):
                        nc.tensor.transpose(psb[:, TR_HI + P * k:TR_HI + P * k + P], xs[:, u, k, 0:P], ident[:])
                        last = nc.tensor.transpose(psb[0:LO, TR_LO + P * k:TR_LO + P * k + P], xs[:, u, k, P:DM], ident[:])
                    last.then_inc(xT_ps, 1)
                    pe.wait_ge(xT_ready, t + 1)
                    if late(t, 2):
                        pe.wait_ge(logits_out, t - 1)
                    for k in range(3):
                        o = LG + 512 * u + EXP * k
                        nc.tensor.matmul(psb[:, o:o + EXP], ft_hi[:, u, P * k:P * k + P], rt_hi[:], start=True, stop=False)
                        last = nc.tensor.matmul(psb[:, o:o + EXP], ft_lo[:, u, P * k:P * k + P], rt_lo[:], start=False, stop=True)
                    last.then_inc(logit_ps, 1)
                pairwise(pe, PAIRS, pair)
                pe.wait_ge(sel_ready, 1)
                chosen = sel[:].rearrange("p t e -> p (t e)")
                nc.tensor.matmul(psb[:, 0:TILES * EXP], upper, chosen, start=True, stop=True)
                nc.tensor.matmul(psb[:, 512:512 + TILES * EXP], ones[:], chosen, start=True, stop=True).then_inc(rank_ps, 1)

        def expert_stage(ctx):
            sb, sem = tools(ctx, "exp")
            XC, YC, HTC = 6 * 512, 7 * 512, 4 * 512
            HALF = FF // 2
            xs = sb("xs", [P, 2, ROW])
            xg = sb("xg", [P, 2, 2, P])
            xA_hi, xA_lo, xB = (sb(n, [P, 2, P], f32r) for n in ("xA_hi", "xA_lo", "xB"))
            hs, hT, ys = sb("hs", [P, 2, FF]), sb("hT", [P, 2, FC, P]), sb("ys", [P, 2, DM])
            into, turn = sb("into", [P, 2], i32), sem("turn")
            meta, gates = sb("meta", [P, 2, 2]), sb("gates", [P, 2])
            x_in = [sem(f"x_in{i}") for i in range(2)]
            xT_ps, xg_ready, xT_ready, h_ps, h_ready, hT_ps, hT_ready, y_ps, y_ready, y_added, copied = (sem(n) for n in (
                "xT_ps", "xg_ready", "xT_ready", "h_ps", "h_ready", "hT_ps", "hT_ready", "y_ps", "y_ready", "y_added", "copied"))
            block = ctx.enter_context(nc.Block())

            def schedule(eng, before, step):
                before()
                step(0, 0)
                step(1, 1)
                with eng.Fori(1, SLOTS // 2 - 1) as i:
                    step(i * 2, 0)
                    step(i * 2 + 1, 1)
                step(SLOTS - 2, 0)
                step(SLOTS - 1, 1)

            def more(s, k):
                return not isinstance(s, int) or s + k < SLOTS

            @block.sync
            def _(sp):
                def load(s, u):
                    if late(s, 2):
                        sp.wait_ge(xT_ready, s - 1)
                    sp.dma_start(xs[:, u], slots_x[ds(s * P, P)]).then_inc(x_in[u], 16)
                pairwise(sp, SLOTS, load)
                sp.wait_ge(y_added, 16 * SLOTS)
                sp.dma_start(out.rearrange("b n d -> (b n) d"), acc[0:B * TOKENS]).then_inc(copied, 16)
                sp.wait_ge(copied, 16)

            @block.gpsimd
            def _(pool):
                def add_rows(s, u):
                    pool.wait_ge(y_ready, s + 1)
                    if late(s, 1):
                        pool.wait_ge(y_added, s * 16)
                    pool.sem_inc(turn, 1)
                    pool.indirect_dma_start(out=acc, out_offset=bass.IndirectOffsetOnAxis(ap=into[:, u:u + 1], axis=0), in_=ys[:, u],
                                            in_offset=None, compute_op=ADD).then_inc(y_added, 16)
                pairwise(pool, SLOTS, add_rows)

            @block.scalar
            def _(act):
                def take_x(s, u):
                    act.wait_ge(xT_ps, s + 1)
                    if late(s, 2):
                        act.wait_ge(xT_ready, s - 1)
                    nc.scalar.activation(xg[:, u, 0], psb[:, XC:XC + P], ACT.Identity, bias=fgb[:, 1, 0:1], scale=fgb[:, 0, 0:1])
                    nc.scalar.activation(xg[0:LO, u, 1], psb[0:LO, XC + P:XC + 2 * P], ACT.Identity, bias=fgb[0:LO, 1, 1:2],
                                         scale=fgb[0:LO, 0, 1:2]).then_inc(xg_ready, 1)

                def hidden(s, u):
                    act.wait_ge(h_ps, s + 1)
                    if late(s, 2):
                        act.wait_ge(hT_ps, s - 1)
                    nc.scalar.activation(hs[:, u].rearrange("p (b f) -> p b f", b=2),
                                         psb[:, 1024 * u:1024 * u + 1024].rearrange("p (b f) -> p b f", b=2)[:, :, 0:HALF],
                                         ACT.Silu).then_inc(h_ready, 1)

                def before():
                    take_x(0, 0)
                    hidden(0, 0)
                    take_x(1, 1)

                def step(s, u):
                    if more(s, 1):
                        hidden(s + 1, 1 - u)
                    if more(s, 2):
                        take_x(s + 2, u)
                schedule(act, before, step)

            @block.vector
            def _(dve):
                def split_x(s, u):
                    dve.wait_ge(xg_ready, s + 1)
                    if late(s, 2):
                        dve.wait_ge(h_ps, s - 1)
                    nc.vector.tensor_copy(meta[:, u], xs[:, u, DM:ROW])
                    nc.vector.tensor_copy(xA_hi[:, u], xg[:, u, 0])
                    nc.vector.tensor_copy(xB[0:LO, u], xg[0:LO, u, 1])
                    dve.drain()
                    nc.vector.tensor_tensor(xA_lo[:, u], xg[:, u, 0], xA_hi[:, u].bitcast(f32), SUB)
                    nc.vector.tensor_tensor(xB[LO:P, u], xg[0:LO, u, 1], xB[0:LO, u].bitcast(f32), SUB).then_inc(xT_ready, 1)

                def take_hT(s, u):
                    dve.wait_ge(hT_ps, s + 1)
                    if late(s, 2):
                        dve.wait_ge(y_ps, s - 1)
                    nc.vector.tensor_copy(hT[:, u].rearrange("p (b c) n -> p b (c n)", b=2),
                                          psb[:, HTC:HTC + 1024].rearrange("p (b f) -> p b f", b=2)[:, :, 0:HALF]).then_inc(hT_ready, 1)

                def result_meta(s, u):
                    if late(s, 2):
                        dve.wait_ge(y_added, (s - 1) * 16)
                    nc.vector.tensor_copy(into[:, u:u + 1], meta[:, u, 0:1])
                    nc.vector.tensor_copy(gates[:, u:u + 1], meta[:, u, 1:2])

                def result(s, u):
                    dve.wait_ge(y_ps, s + 1)
                    nc.vector.tensor_scalar(ys[:, u], psb[:, YC:YC + DM], gates[:, u:u + 1], None, MUL).then_inc(y_ready, 1)

                def before():
                    split_x(0, 0)
                    split_x(1, 1)

                def step(s, u):
                    take_hT(s, u)
                    result_meta(s, u)
                    dve.drain()
                    if more(s, 2):
                        split_x(s + 2, u)
                    result(s, u)
                schedule(dve, before, step)

            @block.tensor
            def _(pe):
                pe.wait_ge(experts_in, 16)

                def of_slot(s):
                    return pe.value_load(slot_expert[0:1, ds(s, 1)], min_val=0, max_val=EXP - 1)

                def turn_x(s, u):
                    pe.wait_ge(x_in[u], (s // 2) * 16 + 16 if isinstance(s, int) else s * 8 + 16 - 8 * u)
                    if late(s, 1):
                        pe.wait_ge(xg_ready, s)
                    nc.tensor.transpose(psb[:, XC:XC + P], xs[:, u, 0:P], ident[:])
                    nc.tensor.transpose(psb[0:LO, XC + P:XC + 2 * P], xs[:, u, P:DM], ident[:]).then_inc(xT_ps, 1)

                def up(s, u):
                    e = of_slot(s)
                    pe.wait_ge(xT_ready, s + 1)
                    if late(s, 2):
                        pe.wait_ge(h_ready, s - 1)
                    for b in range(2):
                        o = 1024 * u + 512 * b
                        parts = ((xA_hi[:, u], upA_hi), (xA_hi[:, u], upA_lo), (xA_lo[:, u], upA_hi),
                                 (xB[:, u], upB_hi), (xB[0:LO, u], upB_lo))
                        for n, (x, w) in enumerate(parts):
                            last = nc.tensor.matmul(psb[:, o:o + HALF], x, w[:, ds(e * FF + HALF * b, HALF)],
                                                    start=(n == 0), stop=(n == len(parts) - 1))
                    last.then_inc(h_ps, 1)

                def turn_h(s, u):
                    pe.wait_ge(h_ready, s + 1)
                    if late(s, 1):
                        pe.wait_ge(hT_ready, s)
                    for c in range(FC):
                        o = HTC + 512 * (c // 3) + P * (c % 3)
                        last = nc.tensor.transpose(psb[:, o:o + P], hs[:, u, P * c:P * c + P], ident[:])
                    last.then_inc(hT_ps, 1)

                def down(s, u):
                    e = of_slot(s)
                    pe.wait_ge(hT_ready, s + 1)
                    if late(s, 1):
                        pe.wait_ge(y_ready, s)
                    for c in range(FC):
                        last = nc.tensor.matmul(psb[:, YC:YC + DM], hT[:, u, c], down_w[:, ds(e, 1), c].rearrange("p a d -> p (a d)"),
                                                start=(c == 0), stop=(c == FC - 1))
                    last.then_inc(y_ps, 1)

                def before():
                    turn_x(0, 0)
                    up(0, 0)
                    turn_x(1, 1)

                def step(s, u):
                    turn_h(s, u)
                    if more(s, 1):
                        up(s + 1, 1 - u)
                    if more(s, 2):
                        turn_x(s + 2, u)
                    down(s, u)
                schedule(pe, before, step)

        down_w = sb("down_w", [P, EXP, FC, DM])
        slot_expert = sb("slot_expert", [P, SLOTS], i32)
        slots_x = nc.dram_tensor("slots_x", (SLOTS * P, ROW), f32).ap()
        acc = nc.dram_tensor("sums", (B * TOKENS + P, DM), f32).ap()
        experts_in = sem("experts_in")
        with ExitStack() as attention:
            sb, sem = tools(attention, "att")
            ALLC = 3 * DM + HA
            wall_hi, wall_lo = sb("wall_hi", [P, ALLC]), sb("wall_lo", [LOA, ALLC])
            wv_hi, wv_lo = sb("wv_hi", [P, DM]), sb("wv_lo", [LOA, DM])
            wq_hi, wq_lo = sb("wq_hi", [P, DM]), sb("wq_lo", [LOA, DM])
            wk_hi, wk_lo = sb("wk_hi", [P, DM]), sb("wk_lo", [LO, DM])
            w1_hi, w1_lo = sb("w1_hi", [P, HD]), sb("w1_lo", [LO, HD])
            w1c_hi, w1c_lo = sb("w1c_hi", [P, DM]), sb("w1c_lo", [LOA, DM])
            pT_hi, pT_lo = sb("pT_hi", [P, DM]), sb("pT_lo", [LOA, DM])
            rows, cols_ = sb("rows", [P, 2, DM]), sb("cols", [P, 2, 2])
            att_in = sem("att_in")
            with ExitStack() as early:
                sb, sem = tools(early, "early")
                zeros = sb("zeros", [P, 512])
                ids_s, idn_s, link_s = sb("ids_s", [P, B], i32), sb("idn_s", [P, B], i32), sb("link_s", [P, 8], i32)
                idn, linkf, mask, masked_rows = sb("idn", [P, B]), sb("linkf", [P, 8]), sb("mask", [P, B]), sb("masked_rows", [P, 1])
                gb = sb("gb", [P, 2, 2])
                tok, tok2 = sb("tok", [P, B, DM]), sb("tok2", [P, B, DM])
                tok_st, tok_mv, tok_rstd = sb("tok_st", [P, B, 6]), sb("tok_mv", [P, B, 2]), sb("tok_rstd", [P, B])
                wpT_hi, wpT_lo = sb("wpT_hi", [P, QW]), sb("wpT_lo", [LOA, QW])
                wvT_hi, wvT_lo = sb("wvT_hi", [P, QW]), sb("wvT_lo", [LO, QW])
                woT, old = sb("woT", [P, MC, DM]), sb("old", [P, MC, DT])
                ids_in, misc_in, text_in, tok_in, tok2_in, padded = (
                    sem(n) for n in ("ids_in", "misc_in", "text_in", "tok_in", "tok2_in", "padded"))
                with ExitStack() as ctx:
                    image_stage(ctx)
                with ExitStack() as ctx:
                    text_stage(ctx)
            with ExitStack() as ctx:
                empty, zeroed, empty_set = tools(ctx, "all")[0]("empty", [P, ROW]), tools(ctx, "all")[1]("zeroed"), tools(ctx, "all")[1]("empty_set")
                attention_stage(ctx)
        sb, sem = tools(whole, "moe")
        fgb = sb("fgb", [P, 2, 2])
        upA_hi, upA_lo, upB_hi, upB_lo = (sb("upA_hi", [P, EXP * FF], f32r), sb("upA_lo", [P, EXP * FF], f32r),
                                          sb("upB_hi", [P, EXP * FF], f32r), sb("upB_lo", [LO, EXP * FF], f32r))
        with ExitStack() as ctx:
            gate = tools(ctx, "all")[0]("gate", [P, 2, TILES])
            route_stage(ctx)
        with ExitStack() as ctx:
            expert_stage(ctx)


def _shape_constants(np):
    pixels = [(y, x) for y in range(16) for x in range(16)]
    pixels += [(-1, x) for x in range(16)] + [(16, x) for x in range(16)]
    pixels += [(y, -1) for y in range(16)] + [(y, 16) for y in range(16)]
    moves = [(0, 0), (0, 1), (0, -1), (1, 0), (-1, 0)]
    source = np.array([[(y + dy) * 16 + x + dx if 0 <= y + dy < 16 and 0 <= x + dx < 16 else -1
                        for y, x in pixels] for dy, dx in moves])
    c = np.zeros((P, CONSTS), np.float32)
    often = np.tile((source >= 0).sum(0), 3) / 3840.0
    c[0:WIN_ROWS, C_COUNT:C_COUNT + WIN_CHUNKS] = often.reshape(WIN_CHUNKS, WIN_ROWS).T
    c[0:SEQ - 2, C_VALID] = 1.0
    c[:, C_TOKV:C_TOKV + TILES] = 1.0
    c[PATCHES:64, C_TOKV:C_TOKV + TILES:3] = 0.0
    c[64 + PATCHES:, C_TOKV:C_TOKV + TILES:3] = 0.0
    own = (np.arange(DM)[:, None] // HD == np.arange(DM)[None, :] // HD).astype(np.float32)
    c[:, C_BLKHI:C_BLKHI + DM] = own[0:P]
    c[0:LO, C_BLKLO:C_BLKLO + DM] = own[P:DM]
    c[LO, C_BLKLO:C_BLKLO + DM] = 1.0
    c[:, C_UT:C_UT + P] = (np.arange(P)[:, None] < np.arange(P)[None, :])
    row = np.arange(P)
    for t in range(PAIRS):
        c[:, C_ROW + 3 * t] = (2 * t + row // 64) * TOKENS + row % 64
        for j in range(2):
            c[:, C_ROW + 3 * t + 1 + j] = (2 * t + j) * TOKENS + PATCHES + row
    c[:, C_EMPTY] = B * TOKENS + row
    return pixels, source, c


def kernel(**inputs):
    import numpy as np
    import concourse.bacc as bacc
    from concourse.bass_utils import run_bass_kernel_spmd as run

    x = {k.replace("L0_", ""): np.asarray(v) for k, v in inputs.items()}
    pixels, source, consts = _shape_constants(np)
    ys, xs = (np.array(v) for v in zip(*pixels))

    def window_rows(w):
        w = w.reshape(256, SHIFTS, 3, -1)
        o = np.zeros((SHIFTS, 3, len(pixels), w.shape[-1]), w.dtype)
        for s in range(SHIFTS):
            k = source[s] >= 0
            o[s][:, k] = w[source[s][k], s].transpose(1, 0, 2)
        return o.reshape(SHIFTS, WIN_CHUNKS, WIN_ROWS, -1).transpose(2, 0, 1, 3)

    image = np.pad(x["x"], ((0, 0), (0, 0), (1, 1), (1, 1)))
    at = np.arange(7) * 16 + 1
    w = image[:, :, (at[:, None] + ys[None])[:, None, :], (at[:, None] + xs[None])[None, :, :]]
    w = w.transpose(0, 2, 3, 1, 4).reshape(B, PATCHES, 3 * len(pixels))
    win = np.zeros((B, 64, 3 * len(pixels)), w.dtype)
    win[:, :PATCHES] = w
    win = win.reshape(PAIRS, P, WIN_CHUNKS, WIN_ROWS).transpose(0, 3, 2, 1)

    def cols(*vectors):
        o = np.zeros((P, len(vectors), 2), vectors[0].dtype)
        for n, v in enumerate(vectors):
            o[:, n, 0], o[0:LO, n, 1] = v[:P], v[P:]
        return o

    def spread(*rows):
        return np.broadcast_to(np.stack(rows)[None], (P, len(rows), rows[0].shape[-1]))

    ids = x["x_txt"].T
    nxt = np.zeros_like(ids)
    nxt[:-1] = ids[1:]
    qkv = x["attn_qkv_weight"]
    data = dict(
        win=win, w5=window_rows(x["tok_W"]),
        gb5=np.stack([window_rows(x["tok_ln_gamma"][:, None]), window_rows(x["tok_ln_beta"][:, None])], 1),
        tok_b=spread(x["tok_b"]), ids=ids, ids_next=nxt,
        link=np.broadcast_to(x["txt_link_ids"].astype(np.int32)[None], (P, 8)), wte=x["txt_wte"],
        txt_gb=cols(x["txt_gamma"], x["txt_beta"]), wprojT=x["txt_W_proj"].T, wvalT=x["txt_W_val"].T,
        woutT=x["txt_W_out"].T.reshape(MC, P, DM).transpose(1, 0, 2),
        traces=x["txt_value_traces"].reshape(MC, P, DT).transpose(1, 0, 2),
        qkvT=qkv.T, wk=qkv[DM:2 * DM], qv_bias=np.stack([x["attn_q_bias"], x["attn_v_bias"]])[None],
        projT=x["attn_proj_weight"].T, proj_b=x["attn_proj_bias"][None], lrT=x["attn_ttt_lr_weight"][:, 0].T,
        lr_b=x["attn_ttt_lr_bias"].T, ttt_rows=spread(x["attn_ttt_norm_weight"].reshape(-1), x["attn_ttt_norm_bias"].reshape(-1)),
        ttt_cols=cols(x["attn_ttt_norm_weight"].reshape(-1), x["attn_ttt_norm_bias"].reshape(-1)),
        w1s=x["attn_W1"].reshape(DM, HD), b1=x["attn_b1"].reshape(1, DM), ffn_gb=cols(x["ffn_ln_gamma"], x["ffn_ln_beta"]),
        router=x["ffn_router_w"], fw1=x["ffn_w1"].transpose(1, 0, 2),
        fw2=x["ffn_w2"].reshape(EXP, FC, P, DM).transpose(2, 0, 1, 3), consts=consts)
    flat = {"win": (PAIRS, WIN_ROWS, WIN_CHUNKS * P)}
    nc = bacc.Bacc("TRN2", target_bir_lowering=False, num_devices=1)
    arrays, args = {}, []
    for name, a in data.items():
        a = np.ascontiguousarray(a)
        a = a.reshape(flat[name] if name in flat else (a.shape[0], -1))
        arrays["in_" + name] = a
        args.append(nc.dram_tensor("in_" + name, a.shape, mybir.dt.from_np(a.dtype), kind="ExternalInput").ap())
    res = nc.dram_tensor("out_h", (B, TOKENS, DM), mybir.dt.float32, kind="ExternalOutput").ap()
    early_fusion(nc, *args, res)
    return run(nc, [arrays], core_ids=[0]).results[0]["out_h"]
```

```python
import concourse.bass as bass
from concourse import mybir
from contextlib import ExitStack

B, SEQ, DM, PATCHES = 16, 128, 192, 49
P = 128
PAIRS = B // 2
TILES = 3 * PAIRS
LO = DM - P
LOA = LO + 1
WIN_ROWS, WIN_CHUNKS = 120, 8
SHIFTS = 5
HM, DT = 8, 64
QW = HM * DT
MC = QW // P
HA, HD = 12, 16
TOKENS = PATCHES + SEQ
EXP, FF = 8, 768
FC = FF // P
SLOTS = (2 * B * TOKENS + EXP * (P - 1)) // P
MAXT = (B * TOKENS + P - 1) // P
N3 = 3 * P
C_COUNT, C_VALID, C_TOKV = 0, 8, 9
C_BLKHI, C_BLKLO, C_UT = 33, 225, 417
C_ROW, C_EMPTY = C_UT + P, C_UT + P + TILES
CONSTS = C_EMPTY + 1
ROW = DM + 1


def early_fusion(nc: bass.Bass, win, w5, gb5, tok_b, ids, ids_next, link, wte, txt_gb, wprojT, wvalT, woutT,
                 traces, qkvT, wk, qv_bias, projT, proj_b, lrT, lr_b, ttt_rows, ttt_cols,
                 w1s, b1, ffn_gb, router, fw1, fw2, consts, out):
    f32, f32r, i32, u32 = mybir.dt.float32, mybir.dt.float32r, mybir.dt.int32, mybir.dt.uint32
    ALU, ACT, AX = mybir.AluOpType, mybir.ActivationFunctionType, mybir.AxisListType.X
    ADD, SUB, MUL, MAX = ALU.add, ALU.subtract, ALU.mult, ALU.max
    ds = bass.ds

    def tools(ctx, stage):
        def sb(name, shape, dt=f32):
            return ctx.enter_context(nc.sbuf_tensor(f"{stage}_{name}", shape, dt))

        def sem(name):
            return ctx.enter_context(nc.semaphore(f"{stage}_{name}"))
        return sb, sem

    def pairwise(eng, n, body):
        body(0, 0)
        body(1, 1)
        with eng.Fori(1, n // 2) as i:
            body(i * 2, 0)
            body(i * 2 + 1, 1)

    def late(t, k):
        return not isinstance(t, int) or t >= k

    whole = ExitStack()
    with whole:
        sb, sem = tools(whole, "all")
        h = sb("h", [P, TILES, DM])
        con = sb("con", [P, CONSTS])
        ident = sb("ident", [P, P])
        ones = sb("ones", [P, P])
        eps5, eps6 = sb("eps5", [P, 1]), sb("eps6", [P, 1])
        ps = whole.enter_context(nc.psum_tensor("ps", [P, 16, 256], f32))
        psb = ps[:].rearrange("p s c -> p (s c)")
        count = con[0:WIN_ROWS, C_COUNT:C_COUNT + WIN_CHUNKS]
        blk_hi, blk_lo = con[:, C_BLKHI:C_BLKHI + DM], con[0:LOA, C_BLKLO:C_BLKLO + DM]
        upper = con[:, C_UT:C_UT + P]

        def image_stage(ctx):
            sb, sem = tools(ctx, "image")
            w5s = sb("w5s", [WIN_ROWS, SHIFTS, WIN_CHUNKS, DM])
            gb5s = sb("gb5s", [WIN_ROWS, 2, SHIFTS, WIN_CHUNKS])
            wc = sb("wc", [WIN_ROWS, WIN_CHUNKS, DM + 1])
            colsum = sb("colsum", [WIN_ROWS, DM])
            brow1 = colsum[0:1]
            winb = sb("winb", [WIN_ROWS, 2, WIN_CHUNKS, P])
            sqb = sb("sqb", [WIN_ROWS, 2, WIN_CHUNKS, P])
            sqsum = sb("sqsum", [WIN_ROWS, 2, P])
            consts_in, w_in, gb_in = sem("consts_in"), sem("w_in"), sem("gb_in")
            win_in = [sem("win_in0"), sem("win_in1")]
            basics, products, colsum_ps, colsum_used, wc_ready = (
                sem("basics"), sem("products"), sem("colsum_ps"), sem("colsum_used"), sem("wc_ready"))
            beta_ps, brow_copied, brow_ps = sem("beta_ps"), sem("brow_copied"), sem("brow_ps")
            tok_mv_ready, window_mm, weighed = sem("tok_mv_ready"), sem("window_mm"), sem("weighed")
            shift_in = [sem(f"shift_in{s}") for s in range(SHIFTS)]
            squared, patch_mm, raw_out, var_ready, std_ready = (
                sem("squared"), sem("patch_mm"), sem("raw_out"), sem("var_ready"), sem("std_ready"))
            block = ctx.enter_context(nc.Block())

            @block.sync
            def _(sp):
                sp.dma_start(gb5s[:], gb5.rearrange("p (a s c) -> p a s c", a=2, s=SHIFTS)).then_inc(gb_in, 16)
                sp.dma_start(ids_s[:], ids).then_inc(ids_in, 16)
                for s in range(SHIFTS):
                    sp.dma_start(w5s[:, s], w5.rearrange("p (s c d) -> p s c d", s=SHIFTS, c=WIN_CHUNKS)[:, s]).then_inc(shift_in[s], 16)
                sp.dma_start(tokb[:], tok_b).then_inc(w_in, 16)
                sp.dma_start(con[:], consts).then_inc(consts_in, 16)

                def load(t, u):
                    if late(t, 2):
                        sp.wait_ge(window_mm, t - 1)
                        sp.wait_ge(squared, t - 1)
                    sp.dma_start(winb[:, u].rearrange("p c n -> p (c n)"),
                                 win[ds(t, 1)].rearrange("a p n -> (a p) n")).then_inc(win_in[u], 16)
                sp.dma_start(idn_s[:], ids_next).then_inc(misc_in, 16)
                sp.dma_start(link_s[:], link).then_inc(misc_in, 16)
                pairwise(sp, PAIRS, load)
                for dst, src in ((gb[:].rearrange("p a b -> p (a b)"), txt_gb), (wpT_hi[:], wprojT[0:P]), (wpT_lo[0:LO], wprojT[P:DM])):
                    sp.dma_start(dst, src).then_inc(text_in, 16)

            @block.gpsimd
            def _(pool):
                nc.gpsimd.memset(zeros[:], 0.0).then_inc(basics, 1)
                pool.wait_ge(basics, 1)
                nc.gpsimd.memset(ones[:], 1.0).then_inc(basics, 1)
                pool.wait_ge(basics, 2)
                nc.gpsimd.memset(eps5[:], 1e-5).then_inc(basics, 1)
                pool.wait_ge(basics, 3)
                nc.gpsimd.memset(eps6[:], 1e-6).then_inc(basics, 1)
                pool.wait_ge(basics, 4)
                nc.gpsimd.affine_select(out=ident[:], in_=zeros[:, 0:P], compare_op=ALU.not_equal, fill=1.0, base=0,
                                        pattern=[[-1, P]], channel_multiplier=1).then_inc(basics, 1)
                pool.wait_ge(ids_in, 16)
                for b in range(B):
                    pool.indirect_dma_start(out=tok[:, b], out_offset=None, in_=wte,
                                            in_offset=bass.IndirectOffsetOnAxis(ap=ids_s[:, b:b + 1], axis=0)).then_inc(tok_in, 16)

            @block.scalar
            def _(act):

                def square(t, u):
                    if late(t, 2):
                        act.wait_ge(weighed, t - 1)
                    act.wait_ge(win_in[u], (t // 2) * 16 + 16 if isinstance(t, int) else t * 8 + 16 - 8 * u)
                    nc.scalar.activation(sqb[:, u], winb[:, u], ACT.Square).then_inc(squared, 1)
                pairwise(act, PAIRS, square)
                act.wait_ge(var_ready, 1)
                nc.scalar.activation(st[:, :, 2:3], st[:, :, 2:3], ACT.Sqrt, bias=eps5[:]).then_inc(std_ready, 1)
                act.wait_ge(tok_mv_ready, 1)
                nc.scalar.activation(tok_rstd[:], tok_mv[:, :, 1], ACT.Sqrt, bias=eps5[:])

            @block.vector
            def _(dve):
                dve.wait_ge(gb_in, 16)
                for s in range(SHIFTS):
                    dve.wait_ge(shift_in[s], 16)
                    for c in range(WIN_CHUNKS):
                        g = gb5s[:, 0, s, c:c + 1]
                        if s == 0:
                            last = nc.vector.tensor_scalar(wc[:, c, 0:DM], w5s[:, s, c], g, None, MUL)
                        else:
                            last = nc.vector.scalar_tensor_tensor(wc[:, c, 0:DM], w5s[:, s, c], g, wc[:, c, 0:DM], MUL, ADD)
                    dve.drain()
                dve.wait_ge(consts_in, 16)
                nc.vector.tensor_copy(wc[:, :, DM:DM + 1].rearrange("p c a -> p (c a)"), count).then_inc(products, 1)
                dve.wait_ge(misc_in, 32)
                nc.vector.tensor_copy(idn[:], idn_s[:])
                nc.vector.tensor_copy(linkf[:], link_s[:])
                dve.drain()
                nc.vector.tensor_scalar(mask[:], idn[:], linkf[:, 0:1], None, ALU.is_equal)
                for l in range(1, 8):
                    dve.drain()
                    nc.vector.scalar_tensor_tensor(mask[:], idn[:], linkf[:, l:l + 1], mask[:], ALU.is_equal, MAX)
                dve.drain()
                nc.vector.tensor_scalar(mask[:], mask[:], con[:, C_VALID:C_VALID + 1], None, MUL)
                dve.drain()
                nc.vector.reduce_sum(masked_rows[:], mask[:], axis=AX)
                dve.wait_ge(colsum_ps, 1)
                nc.vector.tensor_scalar(colsum[:], psb[0:WIN_ROWS, 0:DM], -1.0, None, MUL).then_inc(colsum_used, 1)
                dve.drain()
                for c in range(WIN_CHUNKS):
                    last = nc.vector.scalar_tensor_tensor(wc[:, c, 0:DM], colsum[:], count[:, c:c + 1], wc[:, c, 0:DM], MUL, ADD)
                last.then_inc(wc_ready, 1)
                dve.wait_ge(tok_in, 16 * B)

                def weigh(t, u):
                    dve.wait_ge(squared, t + 1)
                    nc.vector.tensor_tensor(sqb[:, u], sqb[:, u], count.unsqueeze(2).to_broadcast([WIN_ROWS, WIN_CHUNKS, P]), MUL)
                    dve.drain()
                    if late(t, 2):
                        dve.wait_ge(patch_mm, t - 1)
                    nc.vector.reduce_sum(sqsum[:, u], sqb[:, u].rearrange("p c n -> p n c"), axis=AX).then_inc(weighed, 1)
                    for j in range(2):
                        nc.vector.bn_stats(tok_st[:, ds(t * 2 + j, 1)].rearrange("p a d -> p (a d)"),
                                           tok[:, ds(t * 2 + j, 1)].rearrange("p a d -> p (a d)"))

                def take_out(t, u):
                    bank = (6 + u) * 512
                    dve.wait_ge(patch_mm, t + 1)
                    nc.vector.tensor_copy(h[:, ds(t * 3, 1)].rearrange("p a d -> p (a d)"), psb[:, bank:bank + DM])
                    nc.vector.tensor_copy(st[:, ds(t, 1), 0:2].rearrange("p a d -> p (a d)"),
                                          psb[:, bank + DM:bank + DM + 2]).then_inc(raw_out, 1)

                weigh(0, 0)
                for t in range(2):
                    weigh(t + 1, 1 - t)
                    take_out(t, t)
                with dve.Fori(1, PAIRS // 2 - 1) as i:
                    for u in range(2):
                        weigh(i * 2 + u + 1, 1 - u)
                        take_out(i * 2 + u, u)
                weigh(PAIRS - 1, 1)
                take_out(PAIRS - 2, 0)
                take_out(PAIRS - 1, 1)
                dve.drain()
                for b in range(B):
                    last = nc.vector.bn_aggr(tok_mv[:, b], tok_st[:, b])
                last.then_inc(tok_mv_ready, 1)
                nc.vector.tensor_tensor(st[:, :, 2], st[:, :, 0], st[:, :, 0], MUL)
                dve.drain()
                nc.vector.tensor_tensor(st[:, :, 2], st[:, :, 1], st[:, :, 2], SUB).then_inc(var_ready, 1)
                dve.wait_ge(std_ready, 1)
                nc.vector.reciprocal(st[:, :, 3], st[:, :, 2])
                dve.wait_ge(beta_ps, 1)
                nc.vector.tensor_copy(brow1, psb[0:1, 512:512 + DM]).then_inc(brow_copied, 1)
                dve.wait_ge(brow_ps, 1)
                dve.wait_ge(w_in, 16)
                nc.vector.tensor_tensor(tokb[:], psb[:, 1024:1024 + DM], tokb[:], ADD)

            @block.tensor
            def _(pe):
                pe.wait_ge(basics, 5)
                pe.wait_ge(gb_in, 16)

                def beta(shifts):
                    for s in shifts:
                        pe.wait_ge(shift_in[s], 16)
                        for c in range(WIN_CHUNKS):
                            last = nc.tensor.matmul(psb[0:1, 512:512 + DM], gb5s[:, 1, s, c:c + 1], w5s[:, s, c],
                                                    start=(s + c == 0), stop=(s == SHIFTS - 1 and c == WIN_CHUNKS - 1))
                    return last
                beta(range(3))
                pe.wait_ge(products, 1)
                for c in range(WIN_CHUNKS):
                    last = nc.tensor.matmul(psb[0:WIN_ROWS, 0:DM], ones[0:WIN_ROWS, 0:WIN_ROWS], wc[:, c, 0:DM],
                                            start=(c == 0), stop=(c == WIN_CHUNKS - 1))
                last.then_inc(colsum_ps, 1)
                beta(range(3, SHIFTS - 1))
                pe.wait_ge(wc_ready, 1)

                def patches(t, u):
                    bank = (6 + u) * 512
                    pe.wait_ge(win_in[u], (t // 2) * 16 + 16 if isinstance(t, int) else t * 8 + 16 - 8 * u)
                    if late(t, 2):
                        pe.wait_ge(raw_out, t - 1)
                    for c in range(WIN_CHUNKS):
                        last = nc.tensor.matmul(psb[:, bank:bank + DM + 1], winb[:, u, c], wc[:, c],
                                                start=(c == 0), stop=(c == WIN_CHUNKS - 1))
                    last.then_inc(window_mm, 1)
                    pe.wait_ge(weighed, t + 1)
                    last = nc.tensor.matmul(psb[:, bank + DM + 1:bank + DM + 2], sqsum[:, u], ones[0:WIN_ROWS, 0:1], start=True, stop=True)
                    last.then_inc(patch_mm, 1)
                pairwise(pe, PAIRS, patches)
                beta([SHIFTS - 1]).then_inc(beta_ps, 1)
                pe.wait_ge(brow_copied, 1)
                nc.tensor.matmul(psb[:, 1024:1024 + DM], ones[0:1, :], brow1, start=True, stop=True).then_inc(brow_ps, 1)

        def text_stage(ctx):
            sb, sem = tools(ctx, "text")
            den = sb("den", [P, 3])
            later = sb("later", [P, B * DM])
            tok2 = later[:].rearrange("p (b d) -> p b d", b=B)
            wvT_hi, wvT_lo = sb("wvT_hi", [P, QW]), sb("wvT_lo", [LO, QW])
            woT, old = sb("woT", [P, MC, DM]), sb("old", [P, MC, DT])
            tok2_in, memory_in = [sem("tok2_in0"), sem("tok2_in1")], sem("memory_in")
            xb, xm = sb("xb", [P, 2, DM + 1]), sb("xm", [P, 2, DM + 1])
            xa_hi, xa_lo = sb("xa_hi", [P, B, SEQ + 1]), sb("xa_lo", [LOA, B, SEQ + 1])
            xl_hi, xl_lo = sb("xl_hi", [P, 2, SEQ]), sb("xl_lo", [LOA, 2, SEQ])
            sq, qe = sb("sq", [P, 2, QW]), sb("qe", [P, 2, QW])
            ss, nrm, wgt = sb("ss", [P, 2, HM]), sb("nrm", [P, 2, HM]), sb("wgt", [P, 2, HM])
            gram, new = sb("gram", [P, MC, P]), sb("new", [P, MC, P])
            kept = sb("kept", [P, MC, DT])
            ca_hi, ca_lo = xm[:, 0, 0:DM], xm[0:LOA, 1, 0:DM]
            m1_hi, m1_lo = sq[:, 0], sq[0:LO, 1]
            wpa = qe[:].rearrange("p a (b c) -> p (a b) c", b=2)
            rts = later[:, 0:MC * 256].rearrange("p (a b) -> p a b", a=MC)
            na_hi, na_lo = xb[:, 0, 0:DM], xb[0:LOA, 1, 0:DM]
            started, beta_ps, wp_ready, mask_tot = sem("started"), sem("beta_ps"), sem("wp_ready"), sem("mask_tot")
            x_ready, xT_ps, xT_ready, q_ps, q_squared, ss_ready, nrm_ready, qe_ready, sums_mm = (
                sem("x_ready"), sem("xT_ps"), sem("xT_ready"), sem("q_ps"), sem("q_squared"), sem("ss_ready"), sem("nrm_ready"),
                sem("qe_ready"), sem("sums_mm"))
            sums_out, small_ps, m1_out, new_ready, wpa_out, rts_out, na_out = (
                sem("sums_out"), sem("small_ps"), sem("m1_out"), sem("new_ready"), sem("wpa_out"), sem("rts_out"), sem("na_out"))
            shift_ready, out_ps, out_done = sem("shift_ready"), sem("out_ps"), sem("out_done")
            GRAM, CROSS, XT, Q = 0, 512, 1024, 2048

            def schedule(eng, before, step):
                before()
                step(0, 0)
                step(1, 1)
                with eng.Fori(1, B // 2 - 1) as i:
                    step(i * 2, 0)
                    step(i * 2 + 1, 1)
                step(B - 2, 0)
                step(B - 1, 1)

            def more(b, k):
                return not isinstance(b, int) or b + k < B

            block = ctx.enter_context(nc.Block())

            @block.sync
            def _(sp):
                for part, b in enumerate((slice(0, 2), slice(2, B))):
                    sp.dma_start(tok2[0:SEQ - 2, b], tok[2:SEQ, b]).then_inc(tok2_in[part], 16)
                    sp.dma_start(tok2[SEQ - 2:SEQ, b], zeros[0:2, 0:DM].unsqueeze(1).to_broadcast([2, b.stop - b.start, DM])).then_inc(tok2_in[part], 16)
                for dst, src in ((wvT_hi[:], wvalT[0:P]), (wvT_lo[:], wvalT[P:DM]),
                                 (woT[:].rearrange("p a b -> p (a b)"), woutT), (old[:].rearrange("p a b -> p (a b)"), traces)):
                    sp.dma_start(dst, src).then_inc(memory_in, 16)
                for dst, src in ((wall_hi[:, 0:DM], qkvT[0:P, DM:2 * DM]), (wall_lo[0:LO, 0:DM], qkvT[P:DM, DM:2 * DM]),
                                 (wv_hi[:], qkvT[0:P, 2 * DM:3 * DM]), (wv_lo[0:LO], qkvT[P:DM, 2 * DM:3 * DM]),
                                 (wv_lo[LO:LOA], qv_bias[:, DM:2 * DM]), (wq_hi[:], qkvT[0:P, 0:DM]), (wq_lo[0:LO], qkvT[P:DM, 0:DM]),
                                 (wq_lo[LO:LOA], qv_bias[:, 0:DM]), (wk_hi[:], wk[0:P]), (wk_lo[:], wk[P:DM]),
                                 (w1_hi[:], w1s[0:P]), (w1_lo[:], w1s[P:DM]), (w1c_lo[LO:LOA], b1),
                                 (pT_hi[:], projT[0:P]), (pT_lo[0:LO], projT[P:DM]), (pT_lo[LO:LOA], proj_b),
                                 (wall_hi[:, 3 * DM:], lrT[0:P]), (wall_lo[0:LO, 3 * DM:], lrT[P:DM]), (wall_lo[LO:LOA, 3 * DM:], lr_b),
                                 (rows[:].rearrange("p a d -> p (a d)"), ttt_rows), (cols_[:].rearrange("p a d -> p (a d)"), ttt_cols)):
                    sp.dma_start(dst, src).then_inc(att_in, 16)

            @block.gpsimd
            def _(pool):
                nc.gpsimd.memset(xb[:, :, DM:DM + 1], 1.0).then_inc(started, 1)
                pool.wait_ge(started, 1)
                nc.gpsimd.memset(xa_hi[:, :, 0:1], 0.0).then_inc(started, 1)
                pool.wait_ge(started, 2)
                nc.gpsimd.memset(xa_lo[:, :, 0:1], 0.0).then_inc(started, 1)
                pool.wait_ge(started, 3)
                nc.gpsimd.memset(gram[:], 0.0).then_inc(started, 1)
                pool.wait_ge(started, 4)
                nc.gpsimd.memset(new[:], 0.0).then_inc(started, 1)
                pool.wait_ge(started, 5)
                nc.gpsimd.memset(wall_lo[LO:LOA, 0:DM], 0.0).then_inc(started, 1)

            @block.scalar
            def _(act):
                act.wait_ge(started, 5)

                def take_x(b, u):
                    xt = XT + 512 * u
                    act.wait_ge(xT_ps, b + 1)
                    nc.scalar.copy(xa_hi[:, ds(b, 1), 1:SEQ + 1].rearrange("p a s -> p (a s)"), psb[:, xt:xt + SEQ])
                    nc.scalar.copy(xa_lo[:, ds(b, 1), 1:SEQ + 1].rearrange("p a s -> p (a s)"), psb[0:LOA, xt + 256:xt + 256 + SEQ])
                    nc.scalar.copy(xl_hi[:, u], psb[:, xt:xt + SEQ])
                    nc.scalar.copy(xl_lo[:, u], psb[0:LOA, xt + 256:xt + 256 + SEQ]).then_inc(xT_ready, 1)

                def square(b, u):
                    act.wait_ge(q_ps, b + 1)
                    nc.scalar.activation(sq[:, u], psb[:, Q + 512 * u:Q + 512 * u + QW], ACT.Square).then_inc(q_squared, 1)

                def norms(b, u):
                    act.wait_ge(ss_ready, b + 1)
                    nc.scalar.activation(nrm[:, u], ss[:, u], ACT.Sqrt).then_inc(nrm_ready, 1)

                def before():
                    take_x(0, 0)
                    take_x(1, 1)

                def step(b, u):
                    square(b, u)
                    norms(b, u)
                    if more(b, 2):
                        take_x(b + 2, u)
                schedule(act, before, step)
                act.drain()

                def shifted(b, u):
                    if late(b, 2):
                        act.wait_ge(out_ps, b - 1)
                    nc.scalar.copy(xl_hi[:, u], xa_hi[:, ds(b, 1), 0:SEQ].rearrange("p a s -> p (a s)"))
                    nc.scalar.copy(xl_lo[:, u], xa_lo[:, ds(b, 1), 0:SEQ].rearrange("p a s -> p (a s)")).then_inc(shift_ready, 1)

                def pair_out(t, more_pairs=True):
                    for j in range(2):
                        act.wait_ge(out_ps, t * 2 + j + 1)
                        nc.scalar.copy(h[:, ds(t * 3 + 1 + j, 1)].rearrange("p a d -> p (a d)"),
                                       psb[:, Q + 512 * j:Q + 512 * j + DM]).then_inc(out_done, 1)
                        if more_pairs:
                            shifted(t * 2 + j + 2, j)
                shifted(0, 0)
                shifted(1, 1)
                pair_out(0)
                with act.Fori(1, PAIRS - 1) as t:
                    pair_out(t)
                pair_out(PAIRS - 1, more_pairs=False)

            @block.vector
            def _(dve):
                dve.wait_ge(text_in, 16 * 3)
                dve.wait_ge(beta_ps, 1)
                nc.vector.tensor_copy(wpT_lo[LO:LOA], psb[LO:LOA, Q:Q + QW])
                nc.vector.tensor_scalar(wpT_hi[:], wpT_hi[:], gb[:, 0, 0:1], None, MUL)
                nc.vector.tensor_scalar(wpT_lo[0:LO], wpT_lo[0:LO], gb[0:LO, 0, 1:2], None, MUL).then_inc(wp_ready, 1)
                dve.wait_ge(mask_tot, 1)
                nc.vector.tensor_scalar(den[:, 0:1], psb[:, XT + 512:XT + 513], float(HM), 1.0, MUL, MAX)
                dve.drain()
                nc.vector.reciprocal(den[:, 1:2], den[:, 0:1])
                dve.drain()
                nc.vector.tensor_scalar(den[:, 2:3], den[:, 1:2], 0.1, None, MUL)
                nc.vector.tensor_scalar(den[:, 0:1], den[:, 1:2], -0.99, None, MUL)
                nc.vector.reciprocal(tok_rstd[:], tok_rstd[:])
                dve.drain()
                dve.wait_ge(started, 5)

                def normalise(b, u):
                    if late(b, 2):
                        dve.drain()
                        dve.wait_ge(xT_ps, b - 1)
                    nc.vector.tensor_scalar(xb[:, u, 0:DM], tok[:, ds(b, 1)].rearrange("p a d -> p (a d)"),
                                            tok_mv[:, ds(b, 1), 0:1].rearrange("p a d -> p (a d)"), tok_rstd[:, ds(b, 1)], SUB, MUL).then_inc(x_ready, 1)

                def masked(b, u):
                    if late(b, 2):
                        dve.wait_ge(sums_mm, b - 1)
                    nc.vector.tensor_scalar(xm[:, u], xb[:, u], mask[:, ds(b, 1)], None, MUL)

                def query(b, u):
                    dve.wait_ge(q_squared, b + 1)
                    nc.vector.reduce_sum(ss[:, u], sq[:, u].rearrange("p (h d) -> p h d", h=HM), axis=AX).then_inc(ss_ready, 1)
                    dve.wait_ge(nrm_ready, b + 1)
                    nc.vector.tensor_scalar(nrm[:, u], nrm[:, u], 1e-8, None, MAX)
                    dve.drain()
                    nc.vector.reciprocal(wgt[:, u], nrm[:, u])
                    dve.drain()
                    nc.vector.tensor_scalar(wgt[:, u], wgt[:, u], mask[:, ds(b, 1)], None, MUL)
                    dve.drain()
                    nc.vector.tensor_tensor(qe[:, u].rearrange("p (h d) -> p h d", h=HM),
                                            psb[:, Q + 512 * u:Q + 512 * u + QW].rearrange("p (h d) -> p h d", h=HM),
                                            wgt[:, u].unsqueeze(2).to_broadcast([P, HM, DT]), MUL).then_inc(qe_ready, 1)

                def before():
                    normalise(0, 0)
                    normalise(1, 1)
                    dve.drain()
                    masked(0, 0)

                def step(b, u):
                    if more(b, 2):
                        normalise(b + 2, u)
                    query(b, u)
                    if more(b, 1):
                        masked(b + 1, 1 - u)
                schedule(dve, before, step)
                dve.wait_ge(sums_mm, B)
                for half in range(2):
                    r = slice(DT * half, DT * half + DT)
                    nc.vector.tensor_copy(gram[r, :, r], psb[r, GRAM:GRAM + 512].rearrange("p (c d) -> p c d", c=MC)[:, :, r])
                nc.vector.tensor_copy(ca_hi, psb[:, CROSS:CROSS + DM])
                nc.vector.tensor_copy(ca_lo, psb[0:LOA, CROSS + 256:CROSS + 256 + DM]).then_inc(sums_out, 1)
                dve.wait_ge(small_ps, 1)
                nc.vector.tensor_copy(wpa[:, 0:2, 0:DM + 1], psb[:, XT:XT + 512].rearrange("p (c d) -> p c d", c=2)[:, :, 0:DM + 1])
                nc.vector.tensor_copy(wpa[:, 2:4, 0:DM + 1], psb[:, XT + 512:XT + 1024].rearrange("p (c d) -> p c d", c=2)[:, :, 0:DM + 1]).then_inc(wpa_out, 1)
                dve.wait_ge(small_ps, 2)
                nc.vector.tensor_copy(m1_hi, psb[:, Q:Q + QW])
                nc.vector.tensor_copy(m1_lo, psb[0:LO, Q + 512:Q + 512 + QW]).then_inc(m1_out, 1)
                dve.wait_ge(small_ps, 3)
                nc.vector.tensor_scalar(kept[:], psb[:, CROSS:CROSS + MC * DT].rearrange("p (c d) -> p c d", c=MC), den[:, 0:1], None, MUL)
                dve.drain()
                dve.wait_ge(memory_in, 64)
                nc.vector.scalar_tensor_tensor(kept[:], old[:], 0.99, kept[:], MUL, ADD)
                dve.drain()
                dve.wait_ge(small_ps, 4)
                for half in range(2):
                    r = slice(DT * half, DT * half + DT)
                    last = nc.vector.scalar_tensor_tensor(new[r, :, r], psb[r, GRAM:GRAM + 512].rearrange("p (c d) -> p c d", c=MC)[:, :, r],
                                                          den[r, 2:3], kept[r], MUL, ADD)
                last.then_inc(new_ready, 1)
                dve.wait_ge(att_in, 16 * 21)
                nc.vector.reduce_sum(av_hi[:], w1_hi[:], axis=AX)
                nc.vector.reduce_sum(av_lo[:], w1_lo[:], axis=AX)
                nc.vector.reduce_sum(av_b[LO:LOA], w1c_lo[LO:LOA].rearrange("p (a d) -> p a d", a=HA), axis=AX)
                dve.drain()
                nc.vector.tensor_scalar(av_hi[:], av_hi[:], 1.0 / HD, None, MUL)
                nc.vector.tensor_scalar(av_lo[:], av_lo[:], 1.0 / HD, None, MUL)
                nc.vector.tensor_scalar(av_b[LO:LOA], av_b[LO:LOA], 1.0 / HD, None, MUL)
                dve.drain()
                nc.vector.tensor_scalar(w1_hi[:], w1_hi[:], av_hi[:], None, SUB)
                nc.vector.tensor_scalar(w1_lo[:], w1_lo[:], av_lo[:], None, SUB)
                rowb = w1c_lo[LO:LOA].rearrange("p (a d) -> p a d", a=HA)
                nc.vector.tensor_tensor(rowb, rowb, av_b[LO:LOA].unsqueeze(2).to_broadcast([1, HA, HD]), SUB)
                dve.drain()
                for w, c, blk, n in ((w1_hi, w1c_hi, blk_hi, P), (w1_lo, w1c_lo, blk_lo, LO)):
                    nc.vector.tensor_tensor(c[0:n].rearrange("p (a d) -> p a d", a=HA), w[0:n].unsqueeze(1).to_broadcast([n, HA, HD]),
                                                   blk[0:n].rearrange("p (a d) -> p a d", a=HA), MUL)
                dve.wait_ge(small_ps, 5)
                nc.vector.tensor_copy(rts[:, 0:2, 0:DM + 1], psb[:, XT:XT + 512].rearrange("p (c d) -> p c d", c=2)[:, :, 0:DM + 1])
                nc.vector.tensor_copy(rts[:, 2:4, 0:DM + 1], psb[:, XT + 512:XT + 1024].rearrange("p (c d) -> p c d", c=2)[:, :, 0:DM + 1]).then_inc(rts_out, 1)
                dve.wait_ge(started, 6)
                nc.vector.tensor_tensor(gam2[:], rows[:, 0], rows[:, 0], MUL)
                nc.vector.tensor_tensor(wv_hi[:], wv_hi[:], wall_hi[:, 0:DM], SUB)
                nc.vector.tensor_tensor(wv_lo[0:LO], wv_lo[0:LO], wall_lo[0:LO, 0:DM], SUB)
                nc.vector.tensor_tensor(wv_lo[LO:LOA], wv_lo[LO:LOA], rows[LO:LOA, 1], SUB)
                dve.drain()
                nc.vector.tensor_tensor(wall_hi[:, 2 * DM:3 * DM], wv_hi[:], rows[:, 0], MUL)
                nc.vector.tensor_tensor(wall_lo[:, 2 * DM:3 * DM], wv_lo[:], rows[0:LOA, 0], MUL)
                dve.wait_ge(small_ps, 6)
                nc.vector.tensor_copy(na_hi, psb[:, CROSS:CROSS + DM])
                nc.vector.tensor_copy(na_lo, psb[0:LOA, CROSS + 256:CROSS + 256 + DM]).then_inc(na_out, 1)

                def statistics(t):
                    patch = h[:, ds(t * 3, 1)].rearrange("p a d -> p (a d)")
                    nc.vector.scalar_tensor_tensor(patch, patch, st[:, ds(t, 1), 3:4].rearrange("p a d -> p (a d)"), tokb[:], MUL, ADD)
                    for j in range(2):
                        dve.wait_ge(out_done, t * 2 + j + 1)
                        tile = ds(t * 3 + 1 + j, 1)
                        nc.vector.bn_stats(h_st[:, tile].rearrange("p a d -> p (a d)"), h[:, tile].rearrange("p a d -> p (a d)"))
                    dve.drain()
                    nc.vector.bn_stats(h_st[:, ds(t * 3, 1)].rearrange("p a d -> p (a d)"), patch)
                with dve.Fori(0, PAIRS) as t:
                    statistics(t)

            @block.tensor
            def _(pe):
                pe.wait_ge(text_in, 16 * 3)
                nc.tensor.matmul(psb[LO:LOA, Q:Q + QW], gb[:, 1, 0:1], wpT_hi[:], start=True, stop=False)
                nc.tensor.matmul(psb[LO:LOA, Q:Q + QW], gb[0:LO, 1, 1:2], wpT_lo[0:LO], start=False, stop=True).then_inc(beta_ps, 1)
                nc.tensor.matmul(psb[:, XT + 512:XT + 513], ones[:], masked_rows[:], start=True, stop=True).then_inc(mask_tot, 1)
                nc.tensor.matmul(psb[:, GRAM:GRAM + 512], ones[:], zeros[:], start=True, stop=True)
                nc.tensor.matmul(psb[:, CROSS:CROSS + 512], ones[:], zeros[:], start=True, stop=True)
                pe.wait_ge(wp_ready, 1)

                def transposes(b, u):
                    xt = XT + 512 * u
                    pe.wait_ge(x_ready, b + 1)
                    if late(b, 2):
                        pe.wait_ge(xT_ready, b - 1)
                    nc.tensor.transpose(psb[:, xt:xt + SEQ], xb[:, u, 0:P], ident[:])
                    nc.tensor.transpose(psb[0:LOA, xt + 256:xt + 256 + SEQ], xb[:, u, P:DM + 1], ident[:]).then_inc(xT_ps, 1)

                def project(b, u):
                    pe.wait_ge(xT_ready, b + 1)
                    if late(b, 2):
                        pe.wait_ge(qe_ready, b - 1)
                    nc.tensor.matmul(psb[:, Q + 512 * u:Q + 512 * u + QW], xl_hi[:, u], wpT_hi[:], start=True, stop=False)
                    nc.tensor.matmul(psb[:, Q + 512 * u:Q + 512 * u + QW], xl_lo[:, u], wpT_lo[:], start=False, stop=True).then_inc(q_ps, 1)

                def sums(b, u):
                    pe.wait_ge(qe_ready, b + 1)
                    for c in range(MC):
                        r = slice(P * c, P * c + P)
                        nc.tensor.matmul(psb[:, GRAM + P * c:GRAM + P * c + P], qe[:, u, r], qe[:, u, r], start=False, stop=True,
                                         skip_group_check=True)
                    if isinstance(b, int) and b == 0:
                        pe.wait_ge(tok2_in[0], 32)
                    v = tok2[:, ds(b, 1)].rearrange("p a d -> p (a d)")
                    nc.tensor.matmul(psb[:, CROSS:CROSS + DM], xm[:, u, 0:P], v, start=False, stop=True, skip_group_check=True)
                    nc.tensor.matmul(psb[0:LOA, CROSS + 256:CROSS + 256 + DM], xm[:, u, P:DM + 1], v, start=False, stop=True,
                                     skip_group_check=True).then_inc(sums_mm, 1)

                def before():
                    transposes(0, 0)
                    project(0, 0)
                    transposes(1, 1)

                def step(b, u):
                    if more(b, 1):
                        project(b + 1, 1 - u)
                    if more(b, 2):
                        transposes(b + 2, u)
                    sums(b, u)
                    if isinstance(b, int) and b == 1:
                        pe.wait_ge(tok2_in[1], 32)
                schedule(pe, before, step)
                for c in range(MC):
                    o = XT + 256 * c
                    nc.tensor.transpose(psb[:, o:o + P], wpT_hi[:, P * c:P * c + P], ident[:])
                    last = nc.tensor.transpose(psb[:, o + P:o + DM + 1], wpT_lo[:, P * c:P * c + P], ident[0:LOA, 0:LOA])
                last.then_inc(small_ps, 1)
                pe.wait_ge(sums_out, 1)
                pe.wait_ge(memory_in, 64)
                for o, m in ((Q, slice(0, P)), (Q + 512, slice(P, DM))):
                    nc.tensor.matmul(psb[0:m.stop - m.start, o:o + QW], ca_hi[:, m], wpT_hi[:], start=True, stop=False)
                    last = nc.tensor.matmul(psb[0:m.stop - m.start, o:o + QW], ca_lo[:, m], wpT_lo[:], start=False, stop=True)
                last.then_inc(small_ps, 1)
                for c in range(MC):
                    last = nc.tensor.matmul(psb[:, CROSS + DT * c:CROSS + DT * c + DT], gram[:, c], old[:, c], start=True, stop=True)
                last.then_inc(small_ps, 1)
                pe.wait_ge(m1_out, 1)
                for c in range(MC):
                    r = slice(P * c, P * c + P)
                    nc.tensor.matmul(psb[:, GRAM + P * c:GRAM + P * c + P], m1_hi[:, r], wvT_hi[:, r], start=True, stop=False)
                    last = nc.tensor.matmul(psb[:, GRAM + P * c:GRAM + P * c + P], m1_lo[:, r], wvT_lo[:, r], start=False, stop=True)
                last.then_inc(small_ps, 1)
                pe.wait_ge(new_ready, 1)
                pe.wait_ge(wpa_out, 1)
                for c in range(MC):
                    last = nc.tensor.matmul(psb[:, XT + 256 * c:XT + 256 * c + DM + 1], new[:, c], wpa[:, c, 0:DM + 1], start=True, stop=True)
                last.then_inc(small_ps, 1)
                pe.wait_ge(rts_out, 1)
                for o, m in ((CROSS, slice(0, P)), (CROSS + 256, slice(P, DM + 1))):
                    for c in range(MC):
                        last = nc.tensor.matmul(psb[0:m.stop - m.start, o:o + DM], rts[:, c, m], woT[:, c], start=(c == 0), stop=(c == MC - 1))
                last.then_inc(small_ps, 1)
                pe.wait_ge(na_out, 1)

                def recall(b, u):
                    pe.wait_ge(shift_ready, b + 1)
                    if late(b, 2):
                        pe.wait_ge(out_done, b - 1)
                    o = Q + 512 * u
                    nc.tensor.matmul(psb[:, o:o + DM], xl_hi[:, u], na_hi, start=True, stop=False)
                    nc.tensor.matmul(psb[:, o:o + DM], xl_lo[:, u], na_lo, start=False, stop=True).then_inc(out_ps, 1)
                pairwise(pe, B, recall)

        def attention_stage(ctx):
            sb, sem = tools(ctx, "ttt")
            empty, empty_set, zeroed = sb("empty", [P, ROW]), sem("empty_set"), sem("zeroed")
            ZI, TI, KI, OI = 0, 3, 6, 9
            TR_HI, TR_LO = 12 * 256, 14 * 256
            mv, rstd, shift = sb("mv", [P, TILES, 2]), sb("rstd", [P, TILES]), sb("shift", [P, TILES])
            xn = sb("xn", [P, 2, 3, DM])
            xt_hi, xt_lo = sb("xt_hi", [P, 2, N3]), sb("xt_lo", [LOA, 2, N3])
            xq_hi, xq_lo = sb("xq_hi", [P, 2, N3]), sb("xq_lo", [LOA, 2, N3])
            rt_hi, rt_lo = sb("rt_hi", [P, 2, N3]), sb("rt_lo", [LOA, 2, N3])
            ka = sb("ka", [P, 2, 3, DM + 1])
            sqz, sqo, xz, gz, tz = (sb(n, [P, 3, DM]) for n in ("sqz", "sqo", "xz", "gz", "tz"))
            zz, zh = sb("zz", [P, 2, 3, DM]), sb("zh", [P, 2, 3, DM])
            var, std, inv, sg, sx, varo, stdo, invo = (sb(n, [P, 3 * HA]) for n in ("var", "std", "inv", "sg", "sx", "varo", "stdo", "invo"))
            ex = sb("ex", [P, 2, 3 * HA])
            w1n_hi, w1n_lo = sb("w1n_hi", [P, 2, P]), sb("w1n_lo", [LOA, 2, DM])
            wz_ps, w_done = sem("wz_ps"), sem("w_done")
            mv_ready, lnstd_ready, ln_ready, ones_set, std_ready, stdo_ready = (
                sem(n) for n in ("mv_ready", "lnstd_ready", "ln_ready", "ones_set", "std_ready", "stdo_ready"))
            xn_ready, xT_ps, xt_ready, xq_ps, xq_ready, wall_ps, k_ready, z_squared, e_ready, var_ready, t_read, z_ready = (
                sem(n) for n in ("xn_ready", "xT_ps", "xt_ready", "xq_ps", "xq_ready", "wall_ps", "k_ready", "z_squared", "e_ready",
                                 "var_ready", "t_read", "z_ready"))
            grad_ps, w1n_ready, o_ps, o_squared, varo_ready, zh_ready, zhT_ps, rt_ready, proj_ps, h_done = (
                sem(n) for n in ("grad_ps", "w1n_ready", "o_ps", "o_squared", "varo_ready", "zh_ready", "zhT_ps",
                                 "rt_ready", "proj_ps", "h_done"))
            grad_half, keys_ps = sem("grad_half"), sem("keys_ps")
            PART = FF // 2
            up, up_in, split, turn = sb("up", [P, 2, 2, PART]), [sem("up_in0"), sem("up_in1")], sem("split"), sem("turn")
            zcol, tcol = slice(DM, 2 * DM), slice(2 * DM, ALLC)
            block = ctx.enter_context(nc.Block())

            def schedule(eng, before, step):
                before()
                step(0, 0)
                step(1, 1)
                with eng.Fori(1, PAIRS // 2 - 1) as i:
                    step(i * 2, 0)
                    step(i * 2 + 1, 1)
                step(PAIRS - 2, 0)
                step(PAIRS - 1, 1)

            def more(t, k):
                return not isinstance(t, int) or t + k < PAIRS

            @block.sync
            def _(sp):
                sp.wait_ge(empty_set, 1)
                sp.dma_start(table[TILES * P:TILES * P + P], empty[:]).then_inc(zeroed, 16)

                def load_up(n, u):
                    if late(n, 2):
                        sp.wait_ge(split, n * 4 - 4)
                    f = ds(n * PART, PART)
                    sp.dma_start(up[:, u, 0], fw1[0:P, f]).then_inc(up_in[u], 16)
                    sp.dma_start(up[0:LO, u, 1], fw1[P:DM, f]).then_inc(up_in[u], 16)
                    sp.dma_start(up[LO:P, u, 1], fw1[P:DM, f]).then_inc(up_in[u], 16)
                pairwise(sp, EXP * FF // PART, load_up)
                sp.wait_ge(zeroed, 16)

            @block.gpsimd
            def _(pool):
                nc.gpsimd.memset(xt_lo[LO:LOA], 1.0).then_inc(ones_set, 1)
                pool.wait_ge(ones_set, 1)
                nc.gpsimd.memset(xq_lo[LO:LOA], 1.0).then_inc(ones_set, 1)
                pool.wait_ge(ones_set, 2)
                nc.gpsimd.memset(rt_lo[LO:LOA], 1.0).then_inc(ones_set, 1)
                pool.wait_ge(ones_set, 3)
                nc.gpsimd.memset(ka[:, :, :, DM:DM + 1], 1.0).then_inc(ones_set, 1)
                pool.wait_ge(ones_set, 4)

                def split_up(n, u):
                    c = ds(n * PART, PART)
                    pool.wait_ge(up_in[u], (n // 2) * 48 + 48 if isinstance(n, int) else n * 24 + 48 - 24 * u)
                    pool.sem_inc(turn, 1)
                    nc.gpsimd.tensor_copy(upA_hi[:, c], up[:, u, 0]).then_inc(split, 1)
                    pool.wait_ge(split, n * 4 + 1)
                    pool.sem_inc(turn, 1)
                    nc.gpsimd.tensor_copy(upB_hi[:, c], up[:, u, 1]).then_inc(split, 1)
                    pool.wait_ge(split, n * 4 + 2)
                    pool.sem_inc(turn, 1)
                    nc.gpsimd.tensor_tensor(upA_lo[:, c], up[:, u, 0], upA_hi[:, c].bitcast(f32), SUB).then_inc(split, 1)
                    pool.wait_ge(split, n * 4 + 3)
                    pool.sem_inc(turn, 1)
                    nc.gpsimd.tensor_tensor(upB_lo[:, c], up[0:LO, u, 1], upB_hi[0:LO, c].bitcast(f32), SUB).then_inc(split, 1)
                    pool.wait_ge(split, n * 4 + 4)
                    pool.sem_inc(turn, 1)
                pairwise(pool, EXP * FF // PART, split_up)

            @block.scalar
            def _(act):
                act.wait_ge(mv_ready, 1)
                nc.scalar.activation(rstd[:], mv[:, :, 1], ACT.Sqrt, bias=eps5[:]).then_inc(lnstd_ready, 1)
                act.wait_ge(ln_ready, 1)
                act.wait_ge(ones_set, 4)

                def normalise(t, u):
                    if late(t, 2):
                        act.wait_ge(xT_ps, t - 1)
                    for k in range(3):
                        last = nc.scalar.activation(xn[:, u, k], h[:, ds(t * 3 + k, 1)].rearrange("p a d -> p (a d)"), ACT.Identity,
                                                    bias=shift[:, ds(t * 3 + k, 1)], scale=rstd[:, ds(t * 3 + k, 1)])
                    last.then_inc(xn_ready, 1)

                def take_x(t, u):
                    act.wait_ge(xT_ps, t + 1)
                    if late(t, 2):
                        act.wait_ge(xq_ps, t - 1)
                    nc.scalar.copy(xt_hi[:, u], psb[:, TR_HI:TR_HI + N3])
                    nc.scalar.copy(xt_lo[0:LO, u], psb[0:LO, TR_LO:TR_LO + N3]).then_inc(xt_ready, 1)

                def take_q(t, u):
                    act.wait_ge(xq_ps, t + 1)
                    if late(t, 2):
                        act.wait_ge(rt_ready, t - 1)
                    nc.scalar.copy(xq_hi[:, u], psb[:, TR_HI:TR_HI + N3])
                    nc.scalar.copy(xq_lo[0:LO, u], psb[0:LO, TR_LO:TR_LO + N3]).then_inc(xq_ready, 1)

                def inner(t, u):
                    act.wait_ge(keys_ps, t + 1)
                    if late(t, 2):
                        act.wait_ge(grad_ps, t - 1)
                    nc.scalar.copy(ka[:, u, :, 0:DM], ps[:, KI:KI + 3, 0:DM]).then_inc(k_ready, 1)
                    act.wait_ge(wall_ps, t + 1)
                    if late(t, 1):
                        act.wait_ge(var_ready, t)
                    nc.scalar.activation(sqz[:], ps[:, ZI:ZI + 3, 0:DM], ACT.Square).then_inc(z_squared, 1)

                def rate_and_deviation(t, u):
                    if late(t, 2):
                        act.wait_ge(z_ready, t - 1)
                    nc.scalar.activation(ex[:, u].rearrange("p (k a) -> p k a", k=3), ps[:, TI:TI + 3, DM:DM + HA], ACT.Exp,
                                         scale=-1.0).then_inc(e_ready, 1)
                    act.wait_ge(var_ready, t + 1)
                    nc.scalar.activation(std[:], var[:], ACT.Sqrt, bias=eps6[:], scale=1.0 / HD).then_inc(std_ready, 1)

                def outer(t, u):
                    act.wait_ge(o_ps, t + 1)
                    if late(t, 1):
                        act.wait_ge(varo_ready, t)
                    nc.scalar.activation(sqo[:], ps[:, OI:OI + 3, 0:DM], ACT.Square).then_inc(o_squared, 1)
                    act.wait_ge(varo_ready, t + 1)
                    nc.scalar.activation(stdo[:], varo[:], ACT.Sqrt, bias=eps6[:], scale=1.0 / HD).then_inc(stdo_ready, 1)

                def before():
                    normalise(0, 0)
                    take_x(0, 0)
                    normalise(1, 1)
                    take_q(0, 0)
                    inner(0, 0)
                    rate_and_deviation(0, 0)
                    take_x(1, 1)
                    inner(1, 1)

                def step(t, u):
                    if more(t, 2):
                        normalise(t + 2, u)
                    if more(t, 1):
                        rate_and_deviation(t + 1, 1 - u)
                    if more(t, 2):
                        take_x(t + 2, u)
                    if more(t, 1):
                        take_q(t + 1, 1 - u)
                    outer(t, u)
                    if more(t, 2):
                        inner(t + 2, u)
                schedule(act, before, step)

            @block.vector
            def _(dve):
                nc.vector.memset(empty[:], 0.0)
                dve.drain()
                nc.vector.tensor_copy(empty[:, DM:DM + 1], con[:, C_EMPTY:C_EMPTY + 1]).then_inc(empty_set, 1)
                for t in range(TILES):
                    last = nc.vector.bn_aggr(mv[:, t], h_st[:, t])
                last.then_inc(mv_ready, 1)
                dve.wait_ge(lnstd_ready, 1)
                nc.vector.reciprocal(rstd[:], rstd[:])
                dve.drain()
                nc.vector.scalar_tensor_tensor(shift[:], mv[:, :, 0], -1.0, rstd[:], MUL, MUL).then_inc(ln_ready, 1)
                dve.wait_ge(wz_ps, 1)
                nc.vector.tensor_copy(wall_hi[:, zcol], ps[:, 0, 0:DM])
                nc.vector.tensor_copy(wall_lo[0:LO, zcol], ps[0:LO, 2, 0:DM])
                nc.vector.tensor_copy(wall_lo[LO:LOA, zcol], w1c_lo[LO:LOA])
                nc.vector.tensor_tensor(pT_lo[LO:LOA], pT_lo[LO:LOA], ps[LO:LOA, 4, 0:DM], ADD).then_inc(w_done, 1)

                def heads(ap):
                    return ap.rearrange("p k (a d) -> p (k a) d", a=HA)

                def per_head(ap):
                    return ap.unsqueeze(2).to_broadcast([P, 3 * HA, HD])

                def zslots(s):
                    return ps[:, s:s + 3, 0:DM].rearrange("p k (a d) -> p k a d", a=HA)

                def four(ap):
                    return ap.rearrange("p k (a d) -> p k a d", a=HA)

                def per_head4(ap):
                    return ap[:].rearrange("p (k a) -> p k a", k=3).unsqueeze(3).to_broadcast([P, 3, HA, HD])

                def squares(t):
                    dve.wait_ge(z_squared, t + 1)
                    nc.vector.reduce_sum(var[:], heads(sqz[:]), axis=AX).then_inc(var_ready, 1)

                def normalised(t):
                    dve.wait_ge(std_ready, t + 1)
                    nc.vector.reciprocal(inv[:], std[:])
                    dve.drain()
                    nc.vector.tensor_tensor(four(xz[:]), zslots(ZI), per_head4(inv), MUL)
                    dve.drain()
                    nc.vector.tensor_tensor(gz[:], xz[:], gam2[:].unsqueeze(1).to_broadcast([P, 3, DM]), MUL)

                def less_targets(t):
                    dve.drain()
                    dve.wait_ge(e_ready, t + 1)
                    nc.vector.tensor_tensor(gz[:], gz[:], ps[:, TI:TI + 3, 0:DM], SUB).then_inc(t_read, 1)

                def sums(t, u):
                    nc.vector.tensor_scalar(ex[:, u], ex[:, u], 1.0, None, ADD)
                    dve.drain()
                    nc.vector.tensor_tensor(tz[:], gz[:], xz[:], MUL)
                    nc.vector.reciprocal(ex[:, u], ex[:, u])
                    nc.vector.reduce_sum(sg[:], heads(gz[:]), axis=AX)
                    dve.drain()
                    nc.vector.scalar_tensor_tensor(ex[:, u], ex[:, u], 1.0 / (HD * HD * TOKENS), inv[:], MUL, MUL)

                def centred(t, u):
                    nc.vector.reduce_sum(sx[:], heads(tz[:]), axis=AX)
                    nc.vector.scalar_tensor_tensor(heads(gz[:]), heads(gz[:]), float(HD), per_head(sg[:]), MUL, SUB)
                    dve.drain()
                    nc.vector.tensor_tensor(heads(tz[:]), heads(xz[:]), per_head(sx[:]), MUL)
                    dve.drain()

                def scaled(t, u):
                    nc.vector.tensor_tensor(gz[:], gz[:], tz[:], SUB)
                    dve.drain()
                    if late(t, 2):
                        dve.wait_ge(grad_ps, t - 1)
                    nc.vector.tensor_tensor(heads(zz[:, u]), heads(gz[:]), per_head(ex[:, u]), MUL).then_inc(z_ready, 1)

                def new_weights(t, u):
                    dve.wait_ge(grad_ps, t + 1)
                    if late(t, 1):
                        dve.wait_ge(o_ps, t)
                    nc.vector.tensor_tensor(w1n_hi[:], ps[:, OI].rearrange("p (j d) -> p j d", j=2), blk_hi[:, 0:P].unsqueeze(1).to_broadcast([P, 2, P]), MUL)
                    nc.vector.tensor_tensor(w1n_lo[:], ps[0:LOA, OI + 1:OI + 3, 0:DM], blk_lo.unsqueeze(1).to_broadcast([LOA, 2, DM]), MUL)
                    dve.drain()
                    nc.vector.tensor_tensor(w1n_hi[:], w1c_hi[:, 0:P].unsqueeze(1).to_broadcast([P, 2, P]), w1n_hi[:], SUB)
                    nc.vector.tensor_tensor(w1n_lo[:], w1c_lo[:].unsqueeze(1).to_broadcast([LOA, 2, DM]), w1n_lo[:], SUB).then_inc(w1n_ready, 1)

                def outer(t, u):
                    dve.wait_ge(o_squared, t + 1)
                    nc.vector.reduce_sum(varo[:], heads(sqo[:]), axis=AX).then_inc(varo_ready, 1)
                    dve.wait_ge(stdo_ready, t + 1)
                    nc.vector.reciprocal(invo[:], stdo[:])
                    dve.drain()
                    nc.vector.tensor_tensor(four(zh[:, u]), zslots(OI), per_head4(invo), MUL).then_inc(zh_ready, 1)

                def with_queries(t, u):
                    dve.wait_ge(zhT_ps, t + 1)
                    nc.vector.scalar_tensor_tensor(rt_hi[:, u], psb[:, TR_HI:TR_HI + N3], cols_[:, 0, 0:1], xq_hi[:, u], MUL, ADD)
                    nc.vector.scalar_tensor_tensor(rt_lo[0:LO, u], psb[0:LO, TR_LO:TR_LO + N3], cols_[0:LO, 0, 1:2], xq_lo[0:LO, u],
                                                   MUL, ADD).then_inc(rt_ready, 1)

                def add(t, u):
                    dve.wait_ge(proj_ps, t + 1)
                    nc.vector.tensor_tensor(h[:, ds(t * 3, 3)], h[:, ds(t * 3, 3)], ps[:, OI:OI + 3, 0:DM], ADD).then_inc(h_done, 1)

                def statistics(t):
                    for k in range(3):
                        nc.vector.bn_stats(h_st[:, ds(t * 3 + k, 1)].rearrange("p a d -> p (a d)"),
                                           h[:, ds(t * 3 + k, 1)].rearrange("p a d -> p (a d)"))

                def before():
                    squares(0)
                    normalised(0)
                    less_targets(0)
                    sums(0, 0)
                    centred(0, 0)
                    scaled(0, 0)
                    squares(1)

                def step(t, u):
                    if more(t, 1):
                        normalised(t + 1)
                    new_weights(t, u)
                    if more(t, 1):
                        less_targets(t + 1)
                    if late(t, 1):
                        statistics(t - 1)
                    if more(t, 1):
                        sums(t + 1, 1 - u)
                    outer(t, u)
                    if more(t, 1):
                        centred(t + 1, 1 - u)
                    with_queries(t, u)
                    if more(t, 1):
                        scaled(t + 1, 1 - u)
                    if more(t, 2):
                        squares(t + 2)
                    if isinstance(t, int) and t == PAIRS - 1:
                        for tile in range(3 * t):
                            nc.vector.bn_aggr(h_mv[:, tile], h_st[:, tile])
                    add(t, u)
                schedule(dve, before, step)
                dve.drain()
                statistics(PAIRS - 1)
                dve.drain()
                for tile in range(TILES - 3, TILES):
                    nc.vector.bn_aggr(h_mv[:, tile], h_st[:, tile])

            @block.tensor
            def _(pe):
                nc.tensor.matmul(ps[:, 0, 0:DM], wk_hi[:, 0:P], w1c_hi[:], start=True, stop=False)
                nc.tensor.matmul(ps[:, 0, 0:DM], wk_lo[:, 0:P], w1c_lo[0:LO], start=False, stop=True)
                nc.tensor.matmul(ps[0:LO, 2, 0:DM], wk_hi[:, P:DM], w1c_hi[:], start=True, stop=False)
                nc.tensor.matmul(ps[0:LO, 2, 0:DM], wk_lo[:, P:DM], w1c_lo[0:LO], start=False, stop=True)
                nc.tensor.matmul(ps[LO:LOA, 4, 0:DM], cols_[:, 1, 0:1], pT_hi[:], start=True, stop=False)
                nc.tensor.matmul(ps[LO:LOA, 4, 0:DM], cols_[0:LO, 1, 1:2], pT_lo[0:LO], start=False, stop=True).then_inc(wz_ps, 1)
                pe.wait_ge(w_done, 1)

                def tile_cols(k):
                    return slice(P * k, P * k + P)

                def transposes(t, u):
                    pe.wait_ge(xn_ready, t + 1)
                    if isinstance(t, int) and t == 1:
                        pe.wait_ge(xq_ready, 1)
                    if isinstance(t, int) and t == 2:
                        pe.wait_ge(xt_ready, 2)
                    if late(t, 3):
                        pe.wait_ge(rt_ready, t - 2)
                    for k in range(3):
                        nc.tensor.transpose(psb[:, TR_HI + P * k:TR_HI + P * k + P], xn[:, u, k, 0:P], ident[:])
                        last = nc.tensor.transpose(psb[0:LO, TR_LO + P * k:TR_LO + P * k + P], xn[:, u, k, P:DM], ident[:])
                    last.then_inc(xT_ps, 1)

                def queries(t, u, x_after=True):
                    pe.wait_ge(xt_ready, t + 2 if x_after else t + 1)
                    if late(t, 2):
                        pe.wait_ge(rt_ready, t - 1)
                    nc.tensor.matmul(psb[:, TR_HI:TR_HI + N3], wq_hi[:, 0:P], xt_hi[:, u], start=True, stop=False)
                    nc.tensor.matmul(psb[:, TR_HI:TR_HI + N3], wq_lo[:, 0:P], xt_lo[:, u], start=False, stop=True)
                    nc.tensor.matmul(psb[0:LO, TR_LO:TR_LO + N3], wq_hi[:, P:DM], xt_hi[:, u], start=True, stop=False)
                    nc.tensor.matmul(psb[0:LO, TR_LO:TR_LO + N3], wq_lo[:, P:DM], xt_lo[:, u], start=False, stop=True).then_inc(xq_ps, 1)

                def product(u, slot, k, c):
                    n = c.stop - c.start
                    nc.tensor.matmul(ps[:, slot, 0:n], xt_hi[:, u, tile_cols(k)], wall_hi[:, c], start=True, stop=False)
                    return nc.tensor.matmul(ps[:, slot, 0:n], xt_lo[:, u, tile_cols(k)], wall_lo[:, c], start=False, stop=True)

                def inner(t, u):
                    pe.wait_ge(xt_ready, t + 1)
                    if late(t, 1):
                        pe.wait_ge(t_read, t)
                        pe.wait_ge(k_ready, t)
                    for k in range(2):
                        product(u, ZI + k, k, zcol)
                        product(u, TI + k, k, tcol)
                    for k in range(3):
                        if k == 2 and late(t, 2):
                            pe.wait_ge(zh_ready, t - 1)
                        last = product(u, KI + k, k, slice(0, DM))
                    last.then_inc(keys_ps, 1)

                def inner_rest(t, u):
                    product(u, ZI + 2, 2, zcol)
                    product(u, TI + 2, 2, tcol).then_inc(wall_ps, 1)

                def gradient(t, u):
                    pe.wait_ge(z_ready, t + 1)
                    pe.wait_ge(k_ready, t + 2 if more(t, 1) else t + 1)
                    if late(t, 1):
                        pe.wait_ge(h_done, t)
                    for j in range(2):
                        rows_ = slice(64 * j, 64 * j + PATCHES)
                        hi, lo = ps[:, OI, P * j:P * j + P], ps[0:LOA, OI + 1 + j, 0:DM]
                        nc.tensor.matmul(hi, ka[:, u, 1 + j, 0:P], zz[:, u, 1 + j, 0:P], start=True, stop=False)
                        nc.tensor.matmul(hi, ka[rows_, u, 0, 0:P], zz[rows_, u, 0, 0:P], start=False, stop=True)
                        nc.tensor.matmul(lo, ka[:, u, 1 + j, P:DM + 1], zz[:, u, 1 + j], start=True, stop=False)
                        last = nc.tensor.matmul(lo, ka[rows_, u, 0, P:DM + 1], zz[rows_, u, 0], start=False, stop=True)
                        last.then_inc(grad_ps if j else grad_half, 1)
                        if j == 0:
                            pe.wait_ge(grad_half, t + 1)

                def outer(t, u):
                    pe.wait_ge(w1n_ready, t + 1)
                    pe.wait_ge(xq_ready, t + 1)
                    for j in range(2):
                        c = slice(64 * j, 64 * j + 64)
                        for o, q in ((ps[c, OI], c), (ps[:, OI + 1 + j], tile_cols(1 + j))):
                            nc.tensor.matmul(o[:, 0:DM], xq_lo[:, u, q], w1n_lo[:, j], start=True, stop=True)
                            last = nc.tensor.matmul(o[:, 0:P], xq_hi[:, u, q], w1n_hi[:, j], start=False, stop=True, skip_group_check=True)
                    last.then_inc(o_ps, 1)

                def back(t, u):
                    pe.wait_ge(zh_ready, t + 1)
                    if more(t, 1):
                        pe.wait_ge(xq_ready, t + 2)
                    for k in range(3):
                        nc.tensor.transpose(psb[:, TR_HI + P * k:TR_HI + P * k + P], zh[:, u, k, 0:P], ident[:])
                        last = nc.tensor.transpose(psb[0:LO, TR_LO + P * k:TR_LO + P * k + P], zh[:, u, k, P:DM], ident[:])
                    last.then_inc(zhT_ps, 1)

                def project(t, u):
                    pe.wait_ge(rt_ready, t + 1)
                    if more(t, 2):
                        pe.wait_ge(k_ready, t + 3)
                    for k in range(3):
                        nc.tensor.matmul(ps[:, OI + k, 0:DM], rt_hi[:, u, tile_cols(k)], pT_hi[:], start=True, stop=False)
                        last = nc.tensor.matmul(ps[:, OI + k, 0:DM], rt_lo[:, u, tile_cols(k)], pT_lo[:], start=False, stop=True)
                    last.then_inc(proj_ps, 1)

                def before():
                    transposes(0, 0)
                    queries(0, 0, x_after=False)
                    inner(0, 0)
                    inner_rest(0, 0)
                    transposes(1, 1)
                    inner(1, 1)
                    inner_rest(1, 1)

                def step(t, u):
                    if more(t, 2):
                        transposes(t + 2, u)
                    gradient(t, u)
                    if more(t, 1):
                        queries(t + 1, 1 - u, x_after=more(t, 2))
                    outer(t, u)
                    if more(t, 2):
                        inner(t + 2, u)
                    back(t, u)
                    if more(t, 2):
                        inner_rest(t + 2, u)
                    project(t, u)
                schedule(pe, before, step)

        def route_stage(ctx):
            sb, sem = tools(ctx, "route")
            LG = 2048
            rt_hi, rt_lo = sb("rt_hi", [P, EXP]), sb("rt_lo", [LO, EXP])
            r1, shift, r2 = sb("r1", [P, TILES]), sb("shift", [P, TILES]), sb("r2", [P, TILES])
            xu, xs = sb("xu", [P, 2, 3, DM]), sb("xs", [P, 2, 3, ROW])
            ft_hi, ft_lo = sb("ft_hi", [P, 2, N3]), sb("ft_lo", [LO, 2, N3])
            top, topf = sb("top", [P, TILES, 8]), sb("topf", [P, TILES, 8])
            logit, best, besti = sb("logit", [P, 3, EXP]), sb("best", [P, 3, 8]), sb("besti", [P, 3, 8], u32)
            oh1, oh2, sel, pos, prod = (sb(n, [P, TILES, EXP]) for n in ("oh1", "oh2", "sel", "pos", "prod"))
            tot, cum, keep = (sb(n, [P, EXP, TILES]) for n in ("tot", "cum", "keep"))
            gate, gap, posf = sb("gate", [P, 2, TILES]), sb("gap", [P, TILES]), sb("posf", [P, 2, TILES])
            iota_e, iota_s, iota_k = sb("iota_e", [P, EXP]), sb("iota_s", [P, SLOTS]), sb("iota_k", [P, MAXT])
            iota_r, number, first = sb("iota_r", [P, P]), sb("number", [P, TILES]), sb("first", [P, 1])
            put, part = sb("put", [P, 2, TILES], i32), sb("part", [P, 2, 2, TILES], i32)
            place, taken = sb("place", [P, 2, 2, TILES]), sb("taken", [P, 2, TILES])
            over = sb("over", [P, EXP, MAXT])
            tiles_e, tiles_to = sb("tiles_e", [P, EXP]), sb("tiles_to", [P, EXP])
            past, se, base = sb("past", [P, SLOTS, EXP]), sb("se", [P, SLOTS]), sb("base", [P, EXP])
            BUF = 3
            of_row, of_slot = sb("of_row", [P, BUF, 2, 3, P]), sb("of_slot", [P, BUF, 2, 3, 2, SLOTS])
            in_slot = sb("in_slot", [P, BUF, 2, 3, SLOTS])
            (w_in, iotas, std1, v2_ready, std2, ln_ready, xu_ready, xs_ready, res_ready, xT_ps, xT_ready, logit_ps,
             logits_out, gap_ready, exp_ready, sel_ready, rank_ps, summed, one_hot, slot_ready, placed) = (sem(n) for n in (
                 "w_in", "iotas", "std1", "v2_ready", "std2", "ln_ready", "xu_ready", "xs_ready", "res_ready", "xT_ps",
                 "xT_ready", "logit_ps", "logits_out", "gap_ready", "exp_ready", "sel_ready", "rank_ps", "summed", "one_hot",
                 "slot_ready", "placed"))
            pool_step, turn, number_ready = sem("pool_step"), sem("turn"), sem("number_ready")
            zeros = sb("zeros", [P, 1])
            tabled = [sem("tabled0"), sem("tabled1")]
            block = ctx.enter_context(nc.Block())

            def schedule(eng, before, step):
                before()
                step(0, 0)
                step(1, 1)
                with eng.Fori(1, PAIRS // 2 - 1) as i:
                    step(i * 2, 0)
                    step(i * 2 + 1, 1)
                step(PAIRS - 2, 0)
                step(PAIRS - 1, 1)

            def more(t, k):
                return not isinstance(t, int) or t + k < PAIRS

            @block.sync
            def _(sp):
                sp.dma_start(rt_hi[:], router[0:P]).then_inc(w_in, 16)
                sp.dma_start(rt_lo[:], router[P:DM]).then_inc(w_in, 16)
                sp.dma_start(fgb[:].rearrange("p a b -> p (a b)"), ffn_gb).then_inc(w_in, 16)
                for t in range(PAIRS):
                    sp.wait_ge(xs_ready, t + 1)
                    sp.dma_start(table[3 * t * P:3 * t * P + N3].rearrange("(k p) d -> p k d", p=P), xs[:, t % 2]).then_inc(tabled[t % 2], 16)
                    sp.wait_ge(res_ready, t + 1)
                    for j in range(2):
                        r = (2 * t + j) * TOKENS
                        sp.dma_start(acc[r:r + PATCHES], h[64 * j:64 * j + PATCHES, 3 * t]).then_inc(summed, 16)
                        sp.dma_start(acc[r + PATCHES:r + TOKENS], h[:, 3 * t + 1 + j]).then_inc(summed, 16)
                sp.dma_start(down_w[:], fw2.rearrange("p (e c d) -> p e c d", e=EXP, c=FC)).then_inc(experts_in, 16)
                sp.wait_ge(tabled[0], 8 * PAIRS)
                sp.wait_ge(tabled[1], 8 * PAIRS)
                sp.wait_ge(summed, 16 * 4 * PAIRS)

            @block.gpsimd
            def _(pool):
                for n, (dst, pattern, start, down) in enumerate((
                        (iota_e, [[1, EXP]], 0, 0), (iota_s, [[1, SLOTS]], 0, 0), (iota_k, [[P, MAXT]], 0, 0),
                        (iota_r, [[1, P]], 0, 0), (number, [[P, TILES]], -TILES * P, 1), (first, [[1, 1]], TILES * P, 1))):
                    if n:
                        pool.wait_ge(iotas, n)
                    nc.gpsimd.iota(dst[:], pattern, base=start, channel_multiplier=down,
                                   allow_small_or_imprecise_dtypes=True).then_inc(iotas, 1)
                pool.wait_ge(iotas, 6)
                nc.gpsimd.memset(slot_row[:], 0).then_inc(iotas, 1)
                pool.wait_ge(iotas, 7)
                nc.gpsimd.memset(zeros[:], 0.0).then_inc(iotas, 1)
                pool.wait_ge(iotas, 8)

                def slots_of(t, u):
                    pool.wait_ge(one_hot, t + 1)
                    if late(t, BUF):
                        pool.wait_ge(placed, t + 1 - BUF)
                    pool.sem_inc(turn, 1)
                    for n, (k, m, factor) in enumerate(((0, 1, gate), (1, 0, taken), (1, 1, gate))):
                        nc.gpsimd.tensor_tensor(of_slot[:, u, k, :, m], in_slot[:, u, k],
                                                factor[:, k, ds(t * 3, 3)].unsqueeze(2).to_broadcast([P, 3, SLOTS]), MUL).then_inc(pool_step, 1)
                        pool.wait_ge(pool_step, t * 3 + n + 1)
                        pool.sem_inc(turn, 1)
                    pool.sem_inc(slot_ready, 1)
                for t in range(PAIRS):
                    slots_of(t, t % BUF)

            @block.scalar
            def _(act):
                nc.scalar.activation(r1[:], h_mv[:, :, 1], ACT.Sqrt, bias=eps5[:]).then_inc(std1, 1)
                act.wait_ge(v2_ready, 1)
                nc.scalar.activation(r2[:], r2[:], ACT.Sqrt, bias=eps5[:]).then_inc(std2, 1)
                act.wait_ge(ln_ready, 1)
                act.wait_ge(w_in, 48)

                def normalise(t, u):
                    if late(t, 2):
                        act.wait_ge(res_ready, t - 1)
                    for k in range(3):
                        last = nc.scalar.activation(xu[:, u, k], h[:, ds(t * 3 + k, 1)].rearrange("p a d -> p (a d)"), ACT.Identity,
                                                    bias=shift[:, ds(t * 3 + k, 1)], scale=r1[:, ds(t * 3 + k, 1)])
                    last.then_inc(xu_ready, 1)

                def take_x(t, u):
                    act.wait_ge(xT_ps, t + 1)
                    if late(t, 2):
                        act.wait_ge(logit_ps, t - 1)
                    c = 1024 * u
                    nc.scalar.activation(ft_hi[:, u], psb[:, c:c + N3], ACT.Identity, bias=fgb[:, 1, 0:1], scale=fgb[:, 0, 0:1])
                    nc.scalar.activation(ft_lo[:, u], psb[0:LO, c + 512:c + 512 + N3], ACT.Identity, bias=fgb[0:LO, 1, 1:2],
                                         scale=fgb[0:LO, 0, 1:2]).then_inc(xT_ready, 1)

                def before():
                    normalise(0, 0)
                    normalise(1, 1)

                def step(t, u):
                    take_x(t, u)
                    if more(t, 2):
                        normalise(t + 2, u)
                schedule(act, before, step)
                act.wait_ge(gap_ready, 1)
                nc.scalar.activation(gap[:], gap[:], ACT.Exp).then_inc(exp_ready, 1)

                def numbers_of(t, u):
                    act.wait_ge(one_hot, t + 1)
                    if late(t, BUF):
                        act.wait_ge(placed, t + 1 - BUF)
                    for n in range(3):
                        last = nc.scalar.activation(of_slot[:, u, 0, n, 0], in_slot[:, u, 0, n], ACT.Identity, bias=zeros[:, 0:1],
                                                    scale=taken[:, 0, ds(t * 3 + n, 1)])
                    last.then_inc(number_ready, 1)
                for t in range(PAIRS):
                    numbers_of(t, t % BUF)

            @block.vector
            def _(dve):
                dve.wait_ge(std1, 1)
                nc.vector.reciprocal(r1[:], r1[:])
                dve.drain()
                nc.vector.scalar_tensor_tensor(shift[:], h_mv[:, :, 0], -1.0, r1[:], MUL, MUL)
                nc.vector.tensor_tensor(r2[:], r1[:], r1[:], MUL)
                dve.drain()
                nc.vector.tensor_tensor(r2[:], r2[:], h_mv[:, :, 1], MUL).then_inc(v2_ready, 1)
                dve.wait_ge(std2, 1)
                nc.vector.reciprocal(r2[:], r2[:]).then_inc(ln_ready, 1)
                dve.drain()


                def second_norm(t, u):
                    dve.wait_ge(xu_ready, t + 1)
                    if late(t, 2):
                        dve.wait_ge(xT_ps, t - 1)
                        dve.wait_ge(tabled[u], (t // 2) * 16 if isinstance(t, int) else t * 8 - 8 * u)
                    scale = r2[:, ds(t * 3, 3)].unsqueeze(2).to_broadcast([P, 3, DM])
                    nc.vector.tensor_copy(xs[:, u, :, DM], con[:, ds(t * 3 + C_ROW, 3)])
                    nc.vector.tensor_tensor(xs[:, u, :, 0:DM], xu[:, u], scale, MUL).then_inc(xs_ready, 1)
                    nc.vector.tensor_tensor(h[:, ds(t * 3, 3)], h[:, ds(t * 3, 3)], xu[:, u], ADD).then_inc(res_ready, 1)

                def take_logits(t, u):
                    dve.wait_ge(logit_ps, t + 1)
                    nc.vector.tensor_copy(logit[:], psb[:, LG + 512 * u:LG + 512 * u + 24].rearrange("p (k e) -> p k e", k=3)).then_inc(logits_out, 1)
                    dve.drain()
                    for k in range(3):
                        nc.vector.max(best[:, k], logit[:, k])
                    dve.drain()
                    for k in range(3):
                        nc.vector.max_index(besti[:, k], best[:, k], logit[:, k])
                    nc.vector.tensor_copy(top[:, ds(t * 3, 3)], best[:])
                    dve.drain()
                    nc.vector.tensor_copy(topf[:, ds(t * 3, 3)], besti[:])

                def before():
                    second_norm(0, 0)
                    second_norm(1, 1)

                def step(t, u):
                    if more(t, 2):
                        second_norm(t + 2, u)
                    take_logits(t, u)
                schedule(dve, before, step)
                dve.drain()
                nc.vector.tensor_tensor(gap[:], top[:, :, 1], top[:, :, 0], SUB).then_inc(gap_ready, 1)
                dve.drain()
                dve.wait_ge(iotas, 3)
                dve.drain()

                def tiles_bc(ap):
                    return ap.unsqueeze(2).to_broadcast([P, TILES, EXP])
                experts_bc = iota_e[:].unsqueeze(1).to_broadcast([P, TILES, EXP])
                valid = con[:, C_TOKV:C_TOKV + TILES]
                nc.vector.tensor_tensor(oh1[:], experts_bc, tiles_bc(topf[:, :, 0]), ALU.is_equal)
                nc.vector.tensor_tensor(oh2[:], experts_bc, tiles_bc(topf[:, :, 1]), ALU.is_equal)
                dve.drain()
                nc.vector.tensor_tensor(oh1[:], oh1[:], tiles_bc(valid), MUL)
                nc.vector.tensor_tensor(oh2[:], oh2[:], tiles_bc(valid), MUL)
                dve.drain()
                nc.vector.tensor_tensor(sel[:], oh1[:], oh2[:], ADD).then_inc(sel_ready, 1)
                dve.wait_ge(exp_ready, 1)
                nc.vector.tensor_scalar(gate[:, 0], gap[:], 1.0, None, ADD)
                nc.vector.memset(keep[:], 1.0)
                dve.drain()
                nc.vector.reciprocal(gate[:, 0], gate[:, 0])
                nc.vector.memset(keep[:, :, 0:1], 0.0)
                dve.drain()
                nc.vector.tensor_tensor(gate[:, 1], gap[:], gate[:, 0], MUL)
                dve.wait_ge(rank_ps, 1)
                nc.vector.tensor_copy(tot[:], psb[:, 512:512 + TILES * EXP].rearrange("p (t e) -> p e t", e=EXP))
                dve.drain()
                nc.vector.tensor_tensor_scan(cum[:].rearrange("p e t -> p (e t)"), keep[:].rearrange("p e t -> p (e t)"),
                                             tot[:].rearrange("p e t -> p (e t)"), 0.0, MUL, ADD)
                dve.drain()
                nc.vector.tensor_tensor(over[:], cum[:, :, TILES - 1:TILES].to_broadcast([P, EXP, MAXT]),
                                        iota_k[:].unsqueeze(1).to_broadcast([P, EXP, MAXT]), ALU.is_gt)
                nc.vector.tensor_tensor(tot[:], cum[:], tot[:], SUB)
                dve.drain()
                nc.vector.reduce_sum(tiles_e[:], over[:], axis=AX)
                dve.drain()
                nc.vector.tensor_tensor_scan(tiles_to[:], ones[:, 0:EXP], tiles_e[:], 0.0, MUL, ADD)
                dve.drain()
                nc.vector.tensor_tensor(base[:], tiles_to[:], tiles_e[:], SUB)
                dve.drain()
                nc.vector.tensor_scalar(base[:], base[:], float(P), None, MUL)
                dve.drain()
                nc.vector.tensor_tensor(pos[:], psb[:, 0:TILES * EXP].rearrange("p (t e) -> p t e", e=EXP),
                                        base[:].unsqueeze(1).to_broadcast([P, TILES, EXP]), ADD)
                dve.drain()
                nc.vector.tensor_tensor(pos[:], pos[:], tot[:].rearrange("p e t -> p t e"), ADD)
                nc.vector.tensor_scalar(gap[:], valid, -float(SLOTS * P), float(SLOTS * P), MUL, ADD)
                dve.drain()
                for k, oh in enumerate((oh1, oh2)):
                    nc.vector.tensor_tensor(prod[:], oh[:], pos[:], MUL)
                    dve.drain()
                    nc.vector.reduce_sum(posf[:, k], prod[:], axis=AX)
                    dve.drain()
                nc.vector.tensor_tensor(put[:], posf[:], gap[:].unsqueeze(1).to_broadcast([P, 2, TILES]), ADD)
                dve.wait_ge(iotas, 8)
                dve.drain()
                nc.vector.tensor_scalar(part[:, 0], put[:], P - 1, None, ALU.bitwise_and)
                nc.vector.tensor_scalar(part[:, 1], put[:], P.bit_length() - 1, None, ALU.logical_shift_right)
                dve.drain()
                nc.vector.tensor_copy(place[:], part[:])
                dve.drain()
                nc.vector.tensor_tensor(taken[:], number[:].unsqueeze(1).to_broadcast([P, 2, TILES]), place[:, 0], SUB)
                dve.drain()

                def rows_of(t, u):
                    if late(t, BUF):
                        dve.wait_ge(placed, t + 1 - BUF)
                    for k in range(2):
                        nc.vector.tensor_tensor(in_slot[:, u, k], iota_s[:].unsqueeze(1).to_broadcast([P, 3, SLOTS]),
                                                place[:, 1, k, ds(t * 3, 3)].unsqueeze(2).to_broadcast([P, 3, SLOTS]), ALU.is_equal)
                        last = nc.vector.tensor_tensor(of_row[:, u, k], iota_r[:].unsqueeze(1).to_broadcast([P, 3, P]),
                                                       place[:, 0, k, ds(t * 3, 3)].unsqueeze(2).to_broadcast([P, 3, P]), ALU.is_equal)
                    last.then_inc(one_hot, 1)
                for t in range(PAIRS):
                    rows_of(t, t % BUF)
                nc.vector.tensor_tensor(past[:], iota_s[:].unsqueeze(2).to_broadcast([P, SLOTS, EXP]),
                                        tiles_to[:].unsqueeze(1).to_broadcast([P, SLOTS, EXP]), ALU.is_ge)
                dve.drain()
                nc.vector.reduce_sum(se[:], past[:], axis=AX)
                dve.drain()
                nc.vector.tensor_scalar(slot_expert[:], se[:], float(EXP - 1), None, ALU.min)

                dve.wait_ge(placed, PAIRS)
                nc.vector.tensor_scalar(slot_row[:, 0:SLOTS], psb[:, 1024:1024 + SLOTS], first[:], None, ADD)
                nc.vector.tensor_copy(slot_gate[:], psb[:, 1024 + SLOTS:1024 + 2 * SLOTS])

            @block.tensor
            def _(pe):
                pe.wait_ge(w_in, 48)

                def transposes(t, u):
                    pe.wait_ge(xs_ready, t + 1)
                    if late(t, 2):
                        pe.wait_ge(xT_ready, t - 1)
                    c = 1024 * u
                    for k in range(3):
                        nc.tensor.transpose(psb[:, c + P * k:c + P * k + P], xs[:, u, k, 0:P], ident[:])
                        last = nc.tensor.transpose(psb[0:LO, c + 512 + P * k:c + 512 + P * k + P], xs[:, u, k, P:DM], ident[:])
                    last.then_inc(xT_ps, 1)

                def logits(t, u):
                    pe.wait_ge(xT_ready, t + 1)
                    if late(t, 2):
                        pe.wait_ge(logits_out, t - 1)
                    for k in range(3):
                        o = LG + 512 * u + EXP * k
                        nc.tensor.matmul(psb[:, o:o + EXP], ft_hi[:, u, P * k:P * k + P], rt_hi[:], start=True, stop=False)
                        last = nc.tensor.matmul(psb[:, o:o + EXP], ft_lo[:, u, P * k:P * k + P], rt_lo[:], start=False, stop=True)
                    last.then_inc(logit_ps, 1)

                def before():
                    transposes(0, 0)

                def step(t, u):
                    if more(t, 1):
                        transposes(t + 1, 1 - u)
                    logits(t, u)
                schedule(pe, before, step)
                pe.wait_ge(sel_ready, 1)
                chosen = sel[:].rearrange("p t e -> p (t e)")
                nc.tensor.matmul(psb[:, 0:TILES * EXP], upper, chosen, start=True, stop=True)
                nc.tensor.matmul(psb[:, 512:512 + TILES * EXP], ones[:], chosen, start=True, stop=True).then_inc(rank_ps, 1)

                def fill(t, u):
                    pe.wait_ge(one_hot, t + 1)
                    pe.wait_ge(slot_ready, t + 1)
                    pe.wait_ge(number_ready, t + 1)
                    for k in range(2):
                        for n in range(3):
                            first_one = isinstance(t, int) and t + k + n == 0
                            last = nc.tensor.matmul(psb[:, 1024:1024 + 2 * SLOTS], of_row[:, u, k, n],
                                                    of_slot[:, u, k, n].rearrange("p a s -> p (a s)"), start=first_one, stop=True,
                                                    skip_group_check=True)
                    last.then_inc(placed, 1)
                for t in range(PAIRS):
                    fill(t, t % BUF)

        def expert_stage(ctx):
            sb, sem = tools(ctx, "exp")
            XC, YC, HTC = 6 * 512, 7 * 512, 4 * 512
            HALF = FF // 2
            xs = sb("xs", [P, 2, ROW])
            xg = sb("xg", [P, 2, 2, P])
            xA_hi, xA_lo, xB = (sb(n, [P, 2, P], f32r) for n in ("xA_hi", "xA_lo", "xB"))
            hs, hT, ys = sb("hs", [P, 2, FF]), sb("hT", [P, 2, FC, P]), sb("ys", [P, 2, DM])
            into, turn = sb("into", [P, 2], i32), sem("turn")
            meta, row, first_rows = sb("meta", [P, 2]), sb("row", [P, 2], i32), sem("first_rows")
            x_in = [sem(f"x_in{i}") for i in range(2)]
            xT_ps, xg_ready, xT_ready, h_ps, h_ready, hT_ps, hT_ready, y_ps, y_ready, y_added = (sem(n) for n in (
                "xT_ps", "xg_ready", "xT_ready", "h_ps", "h_ready", "hT_ps", "hT_ready", "y_ps", "y_ready", "y_added"))
            block = ctx.enter_context(nc.Block())

            def schedule(eng, before, step):
                before()
                step(0, 0)
                step(1, 1)
                with eng.Fori(1, SLOTS // 2 - 1) as i:
                    step(i * 2, 0)
                    step(i * 2 + 1, 1)
                step(SLOTS - 2, 0)
                step(SLOTS - 1, 1)

            def more(s, k):
                return not isinstance(s, int) or s + k < SLOTS

            @block.gpsimd
            def _(pool):
                def gather(s, u):
                    pool.wait_ge(xT_ready, s - 1) if late(s, 2) else pool.wait_ge(first_rows, 1)
                    pool.sem_inc(turn, 1)
                    pool.indirect_dma_start(out=xs[:, u], out_offset=None, in_=table,
                                            in_offset=bass.IndirectOffsetOnAxis(ap=row[:, u:u + 1], axis=0)).then_inc(x_in[u], 16)

                def add_rows(s, u):
                    pool.wait_ge(y_ready, s + 1)
                    if late(s, 1):
                        pool.wait_ge(y_added, s * 16)
                    pool.sem_inc(turn, 1)
                    pool.indirect_dma_start(out=acc, out_offset=bass.IndirectOffsetOnAxis(ap=into[:, u:u + 1], axis=0), in_=ys[:, u],
                                            in_offset=None, compute_op=ADD, bounds_check=B * TOKENS - 1,
                                            oob_is_err=False).then_inc(y_added, 16)
                gather(0, 0)
                gather(1, 1)
                gather(2, 0)

                def step(s, u):
                    if not isinstance(s, int) or s + 3 < SLOTS:
                        gather(s + 3, 1 - u)
                    add_rows(s, u)
                step(0, 0)
                step(1, 1)
                with pool.Fori(1, SLOTS // 2 - 2) as i:
                    step(i * 2, 0)
                    step(i * 2 + 1, 1)
                for s in range(SLOTS - 4, SLOTS):
                    step(s, s % 2)
                pool.wait_ge(y_added, 16 * SLOTS)

            @block.scalar
            def _(act):
                def take_x(s, u):
                    act.wait_ge(xT_ps, s + 1)
                    if late(s, 2):
                        act.wait_ge(xT_ready, s - 1)
                    nc.scalar.activation(xg[:, u, 0], psb[:, XC:XC + P], ACT.Identity, bias=fgb[:, 1, 0:1], scale=fgb[:, 0, 0:1])
                    nc.scalar.activation(xg[0:LO, u, 1], psb[0:LO, XC + P:XC + 2 * P], ACT.Identity, bias=fgb[0:LO, 1, 1:2],
                                         scale=fgb[0:LO, 0, 1:2]).then_inc(xg_ready, 1)

                def hidden(s, u):
                    act.wait_ge(h_ps, s + 1)
                    if late(s, 2):
                        act.wait_ge(hT_ps, s - 1)
                    nc.scalar.activation(hs[:, u].rearrange("p (b f) -> p b f", b=2),
                                         psb[:, 1024 * u:1024 * u + 1024].rearrange("p (b f) -> p b f", b=2)[:, :, 0:HALF],
                                         ACT.Silu).then_inc(h_ready, 1)

                def before():
                    take_x(0, 0)
                    hidden(0, 0)
                    take_x(1, 1)

                def step(s, u):
                    if more(s, 1):
                        hidden(s + 1, 1 - u)
                    if more(s, 2):
                        take_x(s + 2, u)
                schedule(act, before, step)

            @block.vector
            def _(dve):
                def split_x(s, u):
                    dve.wait_ge(xg_ready, s + 1)
                    if late(s, 2):
                        dve.wait_ge(h_ps, s - 1)
                    nc.vector.tensor_copy(meta[:, u:u + 1], xs[:, u, DM:ROW])
                    nc.vector.tensor_copy(row[:, u:u + 1], slot_row[:, ds(s + 2, 1)])
                    nc.vector.tensor_copy(xA_hi[:, u], xg[:, u, 0])
                    nc.vector.tensor_copy(xB[0:LO, u], xg[0:LO, u, 1])
                    dve.drain()
                    nc.vector.tensor_tensor(xA_lo[:, u], xg[:, u, 0], xA_hi[:, u].bitcast(f32), SUB)
                    nc.vector.tensor_tensor(xB[LO:P, u], xg[0:LO, u, 1], xB[0:LO, u].bitcast(f32), SUB).then_inc(xT_ready, 1)

                def take_hT(s, u):
                    dve.wait_ge(hT_ps, s + 1)
                    if late(s, 2):
                        dve.wait_ge(y_ps, s - 1)
                    nc.vector.tensor_copy(hT[:, u].rearrange("p (b c) n -> p b (c n)", b=2),
                                          psb[:, HTC:HTC + 1024].rearrange("p (b f) -> p b f", b=2)[:, :, 0:HALF]).then_inc(hT_ready, 1)

                def result_meta(s, u):
                    if late(s, 2):
                        dve.wait_ge(y_added, (s - 1) * 16)
                    nc.vector.tensor_copy(into[:, u:u + 1], meta[:, u:u + 1])

                def result(s, u):
                    dve.wait_ge(y_ps, s + 1)
                    nc.vector.tensor_scalar(ys[:, u], psb[:, YC:YC + DM], slot_gate[:, ds(s, 1)], None, MUL).then_inc(y_ready, 1)

                nc.vector.tensor_copy(row[:], slot_row[:, 0:2]).then_inc(first_rows, 1)

                def before():
                    split_x(0, 0)
                    split_x(1, 1)

                def step(s, u):
                    take_hT(s, u)
                    result_meta(s, u)
                    dve.drain()
                    if more(s, 2):
                        split_x(s + 2, u)
                    result(s, u)
                schedule(dve, before, step)

            @block.tensor
            def _(pe):
                pe.wait_ge(experts_in, 16)

                def of_slot(s):
                    return pe.value_load(slot_expert[0:1, ds(s, 1)], min_val=0, max_val=EXP - 1)

                def turn_x(s, u):
                    pe.wait_ge(x_in[u], (s // 2) * 16 + 16 if isinstance(s, int) else s * 8 + 16 - 8 * u)
                    if late(s, 1):
                        pe.wait_ge(xg_ready, s)
                    nc.tensor.transpose(psb[:, XC:XC + P], xs[:, u, 0:P], ident[:])
                    nc.tensor.transpose(psb[0:LO, XC + P:XC + 2 * P], xs[:, u, P:DM], ident[:]).then_inc(xT_ps, 1)

                def up(s, u):
                    e = of_slot(s)
                    pe.wait_ge(xT_ready, s + 1)
                    if late(s, 2):
                        pe.wait_ge(h_ready, s - 1)
                    for b in range(2):
                        o = 1024 * u + 512 * b
                        parts = ((xA_hi[:, u], upA_hi), (xA_hi[:, u], upA_lo), (xA_lo[:, u], upA_hi),
                                 (xB[:, u], upB_hi), (xB[0:LO, u], upB_lo))
                        for n, (x, w) in enumerate(parts):
                            last = nc.tensor.matmul(psb[:, o:o + HALF], x, w[:, ds(e * FF + HALF * b, HALF)],
                                                    start=(n == 0), stop=(n == len(parts) - 1))
                    last.then_inc(h_ps, 1)

                def turn_h(s, u):
                    pe.wait_ge(h_ready, s + 1)
                    if late(s, 1):
                        pe.wait_ge(hT_ready, s)
                    for c in range(FC):
                        o = HTC + 512 * (c // 3) + P * (c % 3)
                        last = nc.tensor.transpose(psb[:, o:o + P], hs[:, u, P * c:P * c + P], ident[:])
                    last.then_inc(hT_ps, 1)

                def down(s, u):
                    e = of_slot(s)
                    pe.wait_ge(hT_ready, s + 1)
                    if late(s, 1):
                        pe.wait_ge(y_ready, s)
                    for c in range(FC):
                        last = nc.tensor.matmul(psb[:, YC:YC + DM], hT[:, u, c], down_w[:, ds(e, 1), c].rearrange("p a d -> p (a d)"),
                                                start=(c == 0), stop=(c == FC - 1))
                    last.then_inc(y_ps, 1)

                def before():
                    turn_x(0, 0)
                    up(0, 0)
                    turn_x(1, 1)

                def step(s, u):
                    turn_h(s, u)
                    if more(s, 1):
                        up(s + 1, 1 - u)
                    if more(s, 2):
                        turn_x(s + 2, u)
                    down(s, u)
                schedule(pe, before, step)

        slot_expert = sb("slot_expert", [P, SLOTS], i32)
        slot_row, slot_gate = sb("slot_row", [P, SLOTS + 2], i32), sb("slot_gate", [P, SLOTS])
        fgb = sb("fgb", [P, 2, 2])
        h_st, h_mv = sb("h_st", [P, TILES, 6]), sb("h_mv", [P, TILES, 2])
        upA_hi, upA_lo, upB_hi, upB_lo = (sb(name, [p, EXP * FF], f32r) for name, p in (
            ("upA_hi", P), ("upA_lo", P), ("upB_hi", P), ("upB_lo", LO)))
        table = nc.dram_tensor("table", (TILES * P + P, ROW), f32).ap()
        acc = out.rearrange("b n d -> (b n) d")
        experts_in = sem("experts_in")
        with ExitStack() as attention:
            sb, sem = tools(attention, "att")
            ALLC = 3 * DM + HA
            wall_hi, wall_lo = sb("wall_hi", [P, ALLC]), sb("wall_lo", [LOA, ALLC])
            wv_hi, wv_lo = sb("wv_hi", [P, DM]), sb("wv_lo", [LOA, DM])
            wq_hi, wq_lo = sb("wq_hi", [P, DM]), sb("wq_lo", [LOA, DM])
            wk_hi, wk_lo = sb("wk_hi", [P, DM]), sb("wk_lo", [LO, DM])
            w1_hi, w1_lo = sb("w1_hi", [P, HD]), sb("w1_lo", [LO, HD])
            w1c_hi, w1c_lo = sb("w1c_hi", [P, DM]), sb("w1c_lo", [LOA, DM])
            pT_hi, pT_lo = sb("pT_hi", [P, DM]), sb("pT_lo", [LOA, DM])
            rows, cols_, gam2 = sb("rows", [P, 2, DM]), sb("cols", [P, 2, 2]), sb("gam2", [P, DM])
            av_hi, av_lo, av_b = sb("av_hi", [P, 1]), sb("av_lo", [LO, 1]), sb("av_b", [LOA, HA])
            att_in = sem("att_in")
            with ExitStack() as early:
                sb, sem = tools(early, "early")
                zeros = sb("zeros", [P, 512])
                ids_s, idn_s, link_s = sb("ids_s", [P, B], i32), sb("idn_s", [P, B], i32), sb("link_s", [P, 8], i32)
                idn, linkf, mask, masked_rows = sb("idn", [P, B]), sb("linkf", [P, 8]), sb("mask", [P, B]), sb("masked_rows", [P, 1])
                gb = sb("gb", [P, 2, 2])
                tokb, st = sb("tokb", [P, DM]), sb("st", [P, PAIRS, 4])
                tok = sb("tok", [P, B, DM])
                tok_st, tok_mv, tok_rstd = sb("tok_st", [P, B, 6]), sb("tok_mv", [P, B, 2]), sb("tok_rstd", [P, B])
                wpT_hi, wpT_lo = sb("wpT_hi", [P, QW]), sb("wpT_lo", [LOA, QW])
                ids_in, misc_in, text_in, tok_in = (sem(n) for n in ("ids_in", "misc_in", "text_in", "tok_in"))
                with ExitStack() as ctx:
                    image_stage(ctx)
                with ExitStack() as ctx:
                    text_stage(ctx)
            with ExitStack() as ctx:
                attention_stage(ctx)
        down_w = whole.enter_context(nc.sbuf_tensor("down_w", [P, EXP, FC, DM], f32))
        with ExitStack() as ctx:
            route_stage(ctx)
        with ExitStack() as ctx:
            expert_stage(ctx)


def _shape_constants(np):
    pixels = [(y, x) for y in range(16) for x in range(16)]
    pixels += [(-1, x) for x in range(16)] + [(16, x) for x in range(16)]
    pixels += [(y, -1) for y in range(16)] + [(y, 16) for y in range(16)]
    moves = [(0, 0), (0, 1), (0, -1), (1, 0), (-1, 0)]
    source = np.array([[(y + dy) * 16 + x + dx if 0 <= y + dy < 16 and 0 <= x + dx < 16 else -1
                        for y, x in pixels] for dy, dx in moves])
    c = np.zeros((P, CONSTS), np.float32)
    often = np.tile((source >= 0).sum(0), 3) / 3840.0
    c[0:WIN_ROWS, C_COUNT:C_COUNT + WIN_CHUNKS] = often.reshape(WIN_CHUNKS, WIN_ROWS).T
    c[0:SEQ - 2, C_VALID] = 1.0
    c[:, C_TOKV:C_TOKV + TILES] = 1.0
    c[PATCHES:64, C_TOKV:C_TOKV + TILES:3] = 0.0
    c[64 + PATCHES:, C_TOKV:C_TOKV + TILES:3] = 0.0
    own = (np.arange(DM)[:, None] // HD == np.arange(DM)[None, :] // HD).astype(np.float32)
    c[:, C_BLKHI:C_BLKHI + DM] = own[0:P]
    c[0:LO, C_BLKLO:C_BLKLO + DM] = own[P:DM]
    c[LO, C_BLKLO:C_BLKLO + DM] = 1.0
    c[:, C_UT:C_UT + P] = (np.arange(P)[:, None] < np.arange(P)[None, :])
    row = np.arange(P)
    for t in range(PAIRS):
        c[:, C_ROW + 3 * t] = (2 * t + row // 64) * TOKENS + row % 64
        for j in range(2):
            c[:, C_ROW + 3 * t + 1 + j] = (2 * t + j) * TOKENS + PATCHES + row
    c[:, C_EMPTY] = B * TOKENS + row
    return pixels, source, c


def kernel(**inputs):
    import numpy as np
    import concourse.bacc as bacc
    from concourse.bass_utils import run_bass_kernel_spmd as run

    x = {k.replace("L0_", ""): np.asarray(v) for k, v in inputs.items()}
    pixels, source, consts = _shape_constants(np)
    ys, xs = (np.array(v) for v in zip(*pixels))

    def window_rows(w):
        w = w.reshape(256, SHIFTS, 3, -1)
        o = np.zeros((SHIFTS, 3, len(pixels), w.shape[-1]), w.dtype)
        for s in range(SHIFTS):
            k = source[s] >= 0
            o[s][:, k] = w[source[s][k], s].transpose(1, 0, 2)
        return o.reshape(SHIFTS, WIN_CHUNKS, WIN_ROWS, -1).transpose(2, 0, 1, 3)

    image = np.pad(x["x"], ((0, 0), (0, 0), (1, 1), (1, 1)))
    at = np.arange(7) * 16 + 1
    w = image[:, :, (at[:, None] + ys[None])[:, None, :], (at[:, None] + xs[None])[None, :, :]]
    w = w.transpose(0, 2, 3, 1, 4).reshape(B, PATCHES, 3 * len(pixels))
    win = np.zeros((B, 64, 3 * len(pixels)), w.dtype)
    win[:, :PATCHES] = w
    win = win.reshape(PAIRS, P, WIN_CHUNKS, WIN_ROWS).transpose(0, 3, 2, 1)

    def cols(*vectors):
        o = np.zeros((P, len(vectors), 2), vectors[0].dtype)
        for n, v in enumerate(vectors):
            o[:, n, 0], o[0:LO, n, 1] = v[:P], v[P:]
        return o

    def spread(*rows):
        return np.broadcast_to(np.stack(rows)[None], (P, len(rows), rows[0].shape[-1]))

    ids = x["x_txt"].T
    nxt = np.zeros_like(ids)
    nxt[:-1] = ids[1:]
    qkv = x["attn_qkv_weight"]
    data = dict(
        win=win, w5=window_rows(x["tok_W"]),
        gb5=np.stack([window_rows(x["tok_ln_gamma"][:, None]), window_rows(x["tok_ln_beta"][:, None])], 1),
        tok_b=spread(x["tok_b"]), ids=ids, ids_next=nxt,
        link=np.broadcast_to(x["txt_link_ids"].astype(np.int32)[None], (P, 8)), wte=x["txt_wte"],
        txt_gb=cols(x["txt_gamma"], x["txt_beta"]), wprojT=x["txt_W_proj"].T, wvalT=x["txt_W_val"].T,
        woutT=x["txt_W_out"].T.reshape(MC, P, DM).transpose(1, 0, 2),
        traces=x["txt_value_traces"].reshape(MC, P, DT).transpose(1, 0, 2),
        qkvT=qkv.T, wk=qkv[DM:2 * DM], qv_bias=np.stack([x["attn_q_bias"], x["attn_v_bias"]])[None],
        projT=x["attn_proj_weight"].T, proj_b=x["attn_proj_bias"][None], lrT=x["attn_ttt_lr_weight"][:, 0].T,
        lr_b=x["attn_ttt_lr_bias"].T, ttt_rows=spread(x["attn_ttt_norm_weight"].reshape(-1), x["attn_ttt_norm_bias"].reshape(-1)),
        ttt_cols=cols(x["attn_ttt_norm_weight"].reshape(-1), x["attn_ttt_norm_bias"].reshape(-1)),
        w1s=x["attn_W1"].reshape(DM, HD), b1=x["attn_b1"].reshape(1, DM), ffn_gb=cols(x["ffn_ln_gamma"], x["ffn_ln_beta"]),
        router=x["ffn_router_w"], fw1=x["ffn_w1"].transpose(1, 0, 2),
        fw2=x["ffn_w2"].reshape(EXP, FC, P, DM).transpose(2, 0, 1, 3), consts=consts)
    flat = {"win": (PAIRS, WIN_ROWS, WIN_CHUNKS * P)}
    nc = bacc.Bacc("TRN2", target_bir_lowering=False, num_devices=1)
    arrays, args = {}, []
    for name, a in data.items():
        a = np.ascontiguousarray(a)
        a = a.reshape(flat[name] if name in flat else (a.shape[0], -1))
        arrays["in_" + name] = a
        args.append(nc.dram_tensor("in_" + name, a.shape, mybir.dt.from_np(a.dtype), kind="ExternalInput").ap())
    res = nc.dram_tensor("out_h", (B, TOKENS, DM), mybir.dt.float32, kind="ExternalOutput").ap()
    early_fusion(nc, *args, res)
    return run(nc, [arrays], core_ids=[0]).results[0]["out_h"]
```
